# Optimizing a Trainium2 kernel written in Bass

```python
import numpy as np
import jax
import jax.numpy as jnp

def _softmax(x, axis=-1):
    return jax.nn.softmax(x, axis=axis)

def _gelu(x):
    return jax.nn.gelu(x, approximate=True)

def _silu(x):
    return jax.nn.silu(x)

def _sigmoid(x):
    return jax.nn.sigmoid(x)

def _layernorm(x, axis=-1, eps=1e-05):
    m = jnp.mean(x, axis=axis, keepdims=True)
    v = jnp.var(x, axis=axis, keepdims=True)
    return (x - m) / jnp.sqrt(v + eps)

def _scatter_add(tgt, idx, src, axis=0):
    return tgt.at[idx].add(src)

def _segment_sum(src, seg, n):
    return jax.ops.segment_sum(src, seg, n)
kernel_name = 'mk_gnn_resnorm_d4_gnn_r64_6207bd'

def setup_inputs(seed: int=0):
    np.random.seed(seed)
    _w = jnp.asarray

    def _rec_inputs():
        import jax
        import jax.numpy as jnp
        _gk = jax.random.key(seed)
        x = -0.0003713 + 1 * jax.random.normal(jax.random.fold_in(_gk, 1), (100000, 128), jnp.float32)
        src = jax.random.randint(jax.random.fold_in(_gk, 2), (50000,), 0, 100000, jnp.int32)
        dst = jnp.minimum((100000 * jax.random.uniform(jax.random.fold_in(_gk, 3), (50000,)) ** 2.0).astype(jnp.int32), 99999)
        _o = jnp.argsort(dst, stable=True)
        src = src[_o]
        dst = dst[_o]
        edge_attr_16 = 0.000254156 + 0.999948 * jax.random.normal(jax.random.fold_in(_gk, 12), (50000, 16), jnp.float32)
        edge_weight = jax.random.uniform(jax.random.fold_in(_gk, 14), (50000,), jnp.float32, 0.0, 0.999999)
        return (x, src, dst, edge_attr_16, edge_weight)
    x, src, dst, edge_attr_16, edge_weight = _rec_inputs()

    def _L0_gnn_setup():
        import jax, jax.numpy as jnp
        import numpy as np
        N = 100000
        E = 25000
        D = 128
        L = 3
        BN_EPS = 1e-05

        def _gcn_conv(x, src, dst, ew, W, b):
            loop = jnp.arange(N, dtype=src.dtype)
            src2 = jnp.concatenate([src, loop])
            dst2 = jnp.concatenate([dst, loop])
            ew2 = jnp.concatenate([ew, jnp.ones((N,), dtype=ew.dtype)])
            deg = jax.ops.segment_sum(ew2, dst2, num_segments=N)
            dinv = jnp.where(deg > 0, jax.lax.rsqrt(jnp.maximum(deg, 1e-12)), 0.0)
            norm = dinv[src2] * ew2 * dinv[dst2]
            h = x @ W
            msg = norm[:, None] * h[src2]
            out = jax.ops.segment_sum(msg, dst2, num_segments=N)
            return out + b

        def _batchnorm(x, gamma, beta):
            mean = jnp.mean(x, axis=0)
            var = jnp.mean(jnp.square(x - mean), axis=0)
            return (x - mean) * jax.lax.rsqrt(var + BN_EPS) * gamma + beta
        key = jax.random.key(seed)
        ks = jax.random.split(key, 5)
        x = jax.random.normal(ks[0], (N, D), dtype=jnp.float32)
        edge_index = jax.random.randint(ks[1], (2, E), 0, N, dtype=jnp.int32)
        edge_weight = jax.random.uniform(ks[2], (E,), dtype=jnp.float32)
        Ws = jax.random.normal(ks[3], (L, D, D), dtype=jnp.float32) / np.sqrt(D)
        bs = jnp.zeros((L, D), dtype=jnp.float32)
        gammas = jnp.ones((L, D), dtype=jnp.float32)
        betas = jnp.zeros((L, D), dtype=jnp.float32)
        return {'x': x, 'edge_index': edge_index, 'edge_weight': edge_weight, 'Ws': Ws, 'bs': bs, 'gammas': gammas, 'betas': betas}
    _L0_gnn_all = _L0_gnn_setup()
    _L0_gnn_in = {k: v for k, v in _L0_gnn_all.items() if k in ('Ws', 'bs', 'gammas', 'betas')}
    del _L0_gnn_all

    def _L1_gnn_setup():
        import jax, jax.numpy as jnp
        import numpy as np
        N_NODES = 50000
        N_EDGES = 12500
        IN_FEATS = 128
        H_FEATS = 128

        def eve_conv(x, src, dst, wpool, bpool, wself, weve, wconv, bconv, bias):
            n = x.shape[0]
            p = jax.nn.relu(x @ wpool.T + bpool)
            m = p[src]
            xmax = jax.ops.segment_max(m, dst, num_segments=n)
            xmin = jax.ops.segment_min(m, dst, num_segments=n)
            deg = jax.ops.segment_sum(jnp.ones_like(dst, jnp.float32), dst, num_segments=n)
            has = (deg > 0)[:, None]
            xmax = jnp.where(has, xmax, 0.0)
            xmin = jnp.where(has, xmin, 0.0)
            eve = jax.nn.relu(wconv[0] * xmax + wconv[1] * xmin + bconv[0])
            return x @ wself.T + eve @ weve.T + bias
        key = jax.random.key(seed)
        ks = jax.random.split(key, 16)
        s = 0.05
        d = {'feat': jax.random.normal(ks[0], (N_NODES, IN_FEATS), jnp.float32), 'src': jax.random.randint(ks[1], (N_EDGES,), 0, N_NODES, jnp.int32), 'dst': jax.random.randint(ks[2], (N_EDGES,), 0, N_NODES, jnp.int32), 'wpool1': jax.random.normal(ks[3], (IN_FEATS, IN_FEATS), jnp.float32) * s, 'bpool1': jnp.zeros((IN_FEATS,), jnp.float32), 'wself1': jax.random.normal(ks[4], (H_FEATS, IN_FEATS), jnp.float32) * s, 'weve1': jax.random.normal(ks[5], (H_FEATS, IN_FEATS), jnp.float32) * s, 'wconv1': jax.random.normal(ks[6], (2,), jnp.float32), 'bconv1': jnp.zeros((1,), jnp.float32), 'bias1': jnp.zeros((H_FEATS,), jnp.float32), 'wpool2': jax.random.normal(ks[7], (H_FEATS, H_FEATS), jnp.float32) * s, 'bpool2': jnp.zeros((H_FEATS,), jnp.float32), 'wself2': jax.random.normal(ks[8], (H_FEATS, H_FEATS), jnp.float32) * s, 'weve2': jax.random.normal(ks[9], (H_FEATS, H_FEATS), jnp.float32) * s, 'wconv2': jax.random.normal(ks[10], (2,), jnp.float32), 'bconv2': jnp.zeros((1,), jnp.float32), 'bias2': jnp.zeros((H_FEATS,), jnp.float32)}
        return d
    _L1_gnn_all = _L1_gnn_setup()
    _L1_gnn_in = {k: v for k, v in _L1_gnn_all.items() if k in ('wpool1', 'bpool1', 'wself1', 'weve1', 'wconv1', 'bconv1', 'bias1', 'wpool2', 'bpool2', 'wself2', 'weve2', 'wconv2', 'bconv2', 'bias2')}
    del _L1_gnn_all

    def _L2_gnn_setup():
        import jax, jax.numpy as jnp
        import numpy as np
        N_NODES = 100000
        N_EDGES = 12500
        D = 128

        def segment_mean(vals, seg_ids, num_segments):
            summed = jax.ops.segment_sum(vals, seg_ids, num_segments=num_segments)
            deg = jax.ops.segment_sum(jnp.ones((vals.shape[0],), vals.dtype), seg_ids, num_segments=num_segments)
            return summed / jnp.maximum(deg, 1.0)[:, None]

        def sage_conv(x, src, dst, W_l, W_r, b, num_nodes):
            agg = segment_mean(x[src], dst, num_nodes)
            return agg @ W_l.T + b + x @ W_r.T

        def swish(h):
            return h * jax.nn.sigmoid(h)
        key = jax.random.key(seed)
        ks = jax.random.split(key, 8)
        s = 1.0 / np.sqrt(D)
        return {'x': jax.random.normal(ks[0], (N_NODES, D), jnp.float32), 'edge_index': jax.random.randint(ks[1], (2, N_EDGES), 0, N_NODES, jnp.int64), 'W1_l': jax.random.uniform(ks[2], (D, D), jnp.float32, -s, s), 'W1_r': jax.random.uniform(ks[3], (D, D), jnp.float32, -s, s), 'b1': jnp.zeros((D,), jnp.float32), 'W2_l': jax.random.uniform(ks[4], (D, D), jnp.float32, -s, s), 'W2_r': jax.random.uniform(ks[5], (D, D), jnp.float32, -s, s), 'b2': jnp.zeros((D,), jnp.float32)}
    _L2_gnn_all = _L2_gnn_setup()
    _L2_gnn_in = {k: v for k, v in _L2_gnn_all.items() if k in ('W1_l', 'W1_r', 'b1', 'W2_l', 'W2_r', 'b2')}
    del _L2_gnn_all

    def _L3_gnn_setup():
        import jax, jax.numpy as jnp
        import numpy as np
        N, E, D_IN, D_OUT, H, EDGE_DIM = (50000, 12500, 128, 128, 4, 16)
        C = D_OUT // H
        NEG_SLOPE = 0.2
        LN_EPS = 1e-05
        key = jax.random.key(seed)
        ks = jax.random.split(key, 12)
        g_in = 1.0 / np.sqrt(D_IN)
        g_e = 1.0 / np.sqrt(EDGE_DIM)
        return {'x': jax.random.normal(ks[0], (N, D_IN), jnp.float32), 'edge_index': jax.random.randint(ks[1], (2, E), 0, N, jnp.int64), 'edge_attr': jax.random.normal(ks[2], (E, EDGE_DIM), jnp.float32), 'Wl': jax.random.normal(ks[3], (D_IN, H * C), jnp.float32) * g_in, 'bl': jnp.zeros((H * C,), jnp.float32), 'Wr': jax.random.normal(ks[4], (D_IN, H * C), jnp.float32) * g_in, 'br': jnp.zeros((H * C,), jnp.float32), 'We': jax.random.normal(ks[5], (EDGE_DIM, H * C), jnp.float32) * g_e, 'att': jax.random.normal(ks[6], (H, C), jnp.float32) * (1.0 / np.sqrt(C)), 'bias': jnp.zeros((H * C,), jnp.float32), 'gamma': jnp.ones((D_OUT,), jnp.float32), 'beta': jnp.zeros((D_OUT,), jnp.float32)}
    _L3_gnn_all = _L3_gnn_setup()
    _L3_gnn_in = {k: v for k, v in _L3_gnn_all.items() if k in ('Wl', 'bl', 'Wr', 'br', 'We', 'att', 'bias', 'gamma', 'beta')}
    del _L3_gnn_all
    return {'x': x, 'src': src, 'dst': dst, 'edge_attr_16': edge_attr_16, 'edge_weight': edge_weight, 'L0_gnn_Ws': _L0_gnn_in['Ws'], 'L0_gnn_bs': _L0_gnn_in['bs'], 'L0_gnn_gammas': _L0_gnn_in['gammas'], 'L0_gnn_betas': _L0_gnn_in['betas'], 'L1_gnn_wpool1': _L1_gnn_in['wpool1'], 'L1_gnn_bpool1': _L1_gnn_in['bpool1'], 'L1_gnn_wself1': _L1_gnn_in['wself1'], 'L1_gnn_weve1': _L1_gnn_in['weve1'], 'L1_gnn_wconv1': _L1_gnn_in['wconv1'], 'L1_gnn_bconv1': _L1_gnn_in['bconv1'], 'L1_gnn_bias1': _L1_gnn_in['bias1'], 'L1_gnn_wpool2': _L1_gnn_in['wpool2'], 'L1_gnn_bpool2': _L1_gnn_in['bpool2'], 'L1_gnn_wself2': _L1_gnn_in['wself2'], 'L1_gnn_weve2': _L1_gnn_in['weve2'], 'L1_gnn_wconv2': _L1_gnn_in['wconv2'], 'L1_gnn_bconv2': _L1_gnn_in['bconv2'], 'L1_gnn_bias2': _L1_gnn_in['bias2'], 'L2_gnn_W1_l': _L2_gnn_in['W1_l'], 'L2_gnn_W1_r': _L2_gnn_in['W1_r'], 'L2_gnn_b1': _L2_gnn_in['b1'], 'L2_gnn_W2_l': _L2_gnn_in['W2_l'], 'L2_gnn_W2_r': _L2_gnn_in['W2_r'], 'L2_gnn_b2': _L2_gnn_in['b2'], 'L3_gnn_Wl': _L3_gnn_in['Wl'], 'L3_gnn_bl': _L3_gnn_in['bl'], 'L3_gnn_Wr': _L3_gnn_in['Wr'], 'L3_gnn_br': _L3_gnn_in['br'], 'L3_gnn_We': _L3_gnn_in['We'], 'L3_gnn_att': _L3_gnn_in['att'], 'L3_gnn_bias': _L3_gnn_in['bias'], 'L3_gnn_gamma': _L3_gnn_in['gamma'], 'L3_gnn_beta': _L3_gnn_in['beta']}

def reference(x, src, dst, edge_attr_16, edge_weight, L0_gnn_Ws, L0_gnn_bs, L0_gnn_gammas, L0_gnn_betas, L1_gnn_wpool1, L1_gnn_bpool1, L1_gnn_wself1, L1_gnn_weve1, L1_gnn_wconv1, L1_gnn_bconv1, L1_gnn_bias1, L1_gnn_wpool2, L1_gnn_bpool2, L1_gnn_wself2, L1_gnn_weve2, L1_gnn_wconv2, L1_gnn_bconv2, L1_gnn_bias2, L2_gnn_W1_l, L2_gnn_W1_r, L2_gnn_b1, L2_gnn_W2_l, L2_gnn_W2_r, L2_gnn_b2, L3_gnn_Wl, L3_gnn_bl, L3_gnn_Wr, L3_gnn_br, L3_gnn_We, L3_gnn_att, L3_gnn_bias, L3_gnn_gamma, L3_gnn_beta):
    import jax
    import jax.numpy as jnp

    def _L0_gnn_ref(x, edge_index, edge_weight, Ws, bs, gammas, betas):
        import jax, jax.numpy as jnp
        import numpy as np
        N = 100000
        E = 25000
        D = 128
        L = 3
        BN_EPS = 1e-05

        def _gcn_conv(x, src, dst, ew, W, b):
            loop = jnp.arange(N, dtype=src.dtype)
            src2 = jnp.concatenate([src, loop])
            dst2 = jnp.concatenate([dst, loop])
            ew2 = jnp.concatenate([ew, jnp.ones((N,), dtype=ew.dtype)])
            deg = jax.ops.segment_sum(ew2, dst2, num_segments=N)
            dinv = jnp.where(deg > 0, jax.lax.rsqrt(jnp.maximum(deg, 1e-12)), 0.0)
            norm = dinv[src2] * ew2 * dinv[dst2]
            h = x @ W
            msg = norm[:, None] * h[src2]
            out = jax.ops.segment_sum(msg, dst2, num_segments=N)
            return out + b

        def _batchnorm(x, gamma, beta):
            mean = jnp.mean(x, axis=0)
            var = jnp.mean(jnp.square(x - mean), axis=0)
            return (x - mean) * jax.lax.rsqrt(var + BN_EPS) * gamma + beta
        x0 = x
        src, dst = (edge_index[0], edge_index[1])
        h = x
        for i in range(L):
            h = _gcn_conv(h, src, dst, edge_weight, Ws[i], bs[i])
            h = h + x0
            if i < L - 1:
                h = jax.nn.relu(h)
            h = _batchnorm(h, gammas[i], betas[i])
        return h

    def _L1_gnn_ref(feat, src, dst, wpool1, bpool1, wself1, weve1, wconv1, bconv1, bias1, wpool2, bpool2, wself2, weve2, wconv2, bconv2, bias2):
        import jax, jax.numpy as jnp
        import numpy as np
        N_NODES = 50000
        N_EDGES = 12500
        IN_FEATS = 128
        H_FEATS = 128

        def eve_conv(x, src, dst, wpool, bpool, wself, weve, wconv, bconv, bias):
            n = x.shape[0]
            p = jax.nn.relu(x @ wpool.T + bpool)
            m = p[src]
            xmax = jax.ops.segment_max(m, dst, num_segments=n)
            xmin = jax.ops.segment_min(m, dst, num_segments=n)
            deg = jax.ops.segment_sum(jnp.ones_like(dst, jnp.float32), dst, num_segments=n)
            has = (deg > 0)[:, None]
            xmax = jnp.where(has, xmax, 0.0)
            xmin = jnp.where(has, xmin, 0.0)
            eve = jax.nn.relu(wconv[0] * xmax + wconv[1] * xmin + bconv[0])
            return x @ wself.T + eve @ weve.T + bias
        h = eve_conv(feat, src, dst, wpool1, bpool1, wself1, weve1, wconv1, bconv1, bias1)
        h = jax.nn.relu(h)
        h = eve_conv(h, src, dst, wpool2, bpool2, wself2, weve2, wconv2, bconv2, bias2)
        return h

    def _L2_gnn_ref(x, edge_index, W1_l, W1_r, b1, W2_l, W2_r, b2):
        import jax, jax.numpy as jnp
        import numpy as np
        N_NODES = 100000
        N_EDGES = 12500
        D = 128

        def segment_mean(vals, seg_ids, num_segments):
            summed = jax.ops.segment_sum(vals, seg_ids, num_segments=num_segments)
            deg = jax.ops.segment_sum(jnp.ones((vals.shape[0],), vals.dtype), seg_ids, num_segments=num_segments)
            return summed / jnp.maximum(deg, 1.0)[:, None]

        def sage_conv(x, src, dst, W_l, W_r, b, num_nodes):
            agg = segment_mean(x[src], dst, num_nodes)
            return agg @ W_l.T + b + x @ W_r.T

        def swish(h):
            return h * jax.nn.sigmoid(h)
        src, dst = (edge_index[0], edge_index[1])
        n = x.shape[0]
        h = sage_conv(x, src, dst, W1_l, W1_r, b1, n)
        h = swish(h)
        out = sage_conv(h, src, dst, W2_l, W2_r, b2, n)
        return out

    def _L3_gnn_ref(x, edge_index, edge_attr, Wl, bl, Wr, br, We, att, bias, gamma, beta):
        import jax, jax.numpy as jnp
        import numpy as np
        N, E, D_IN, D_OUT, H, EDGE_DIM = (50000, 12500, 128, 128, 4, 16)
        C = D_OUT // H
        NEG_SLOPE = 0.2
        LN_EPS = 1e-05
        n = x.shape[0]
        src, dst = (edge_index[0], edge_index[1])
        xl = (x @ Wl + bl).reshape(n, H, C)
        xr = (x @ Wr + br).reshape(n, H, C)
        e_feat = (edge_attr @ We).reshape(-1, H, C)
        e = jax.nn.leaky_relu(xl[src] + xr[dst] + e_feat, negative_slope=NEG_SLOPE)
        logits = jnp.einsum('ehc,hc->eh', e, att)
        m = jax.ops.segment_max(logits, dst, num_segments=n)
        m = jnp.where(jnp.isfinite(m), m, 0.0)
        ex = jnp.exp(logits - m[dst])
        denom = jax.ops.segment_sum(ex, dst, num_segments=n)
        alpha = ex / (denom[dst] + 1e-16)
        out = jax.ops.segment_sum(alpha[..., None] * xl[src], dst, num_segments=n)
        out = out.reshape(n, H * C) + bias
        out = jax.nn.gelu(out, approximate=False)
        out = out + x
        mu = out.mean(-1, keepdims=True)
        var = jnp.mean((out - mu) ** 2, -1, keepdims=True)
        out = (out - mu) / jnp.sqrt(var + LN_EPS) * gamma + beta
        return out
    edge_index = jnp.stack([src, dst])
    x = _layernorm(x + _L0_gnn_ref(x, edge_index, edge_weight, L0_gnn_Ws, L0_gnn_bs, L0_gnn_gammas, L0_gnn_betas), axis=-1)
    x = _layernorm(x + _L1_gnn_ref(x, src, dst, L1_gnn_wpool1, L1_gnn_bpool1, L1_gnn_wself1, L1_gnn_weve1, L1_gnn_wconv1, L1_gnn_bconv1, L1_gnn_bias1, L1_gnn_wpool2, L1_gnn_bpool2, L1_gnn_wself2, L1_gnn_weve2, L1_gnn_wconv2, L1_gnn_bconv2, L1_gnn_bias2), axis=-1)
    x = _layernorm(x + _L2_gnn_ref(x, edge_index, L2_gnn_W1_l, L2_gnn_W1_r, L2_gnn_b1, L2_gnn_W2_l, L2_gnn_W2_r, L2_gnn_b2), axis=-1)
    x = _layernorm(x + _L3_gnn_ref(x, edge_index, edge_attr_16, L3_gnn_Wl, L3_gnn_bl, L3_gnn_Wr, L3_gnn_br, L3_gnn_We, L3_gnn_att, L3_gnn_bias, L3_gnn_gamma, L3_gnn_beta), axis=-1)
    return x

_drawn_inputs = setup_inputs


def setup_inputs(seed=0):
    import zlib

    import numpy as np

    out = dict(_drawn_inputs(seed))
    spreads = {'L0_gnn_bs': (0.0, 0.36),
     'L0_gnn_gammas': (1.0, 0.2),
     'L0_gnn_betas': (0.0, 0.1),
     'L1_gnn_bpool1': (0.0, 2.0),
     'L1_gnn_bias1': (0.0, 0.1),
     'L1_gnn_bpool2': (0.0, 0.1),
     'L1_gnn_bias2': (0.0, 0.1),
     'L2_gnn_b1': (0.0, 0.1),
     'L2_gnn_b2': (0.0, 0.1),
     'L3_gnn_bl': (0.0, 0.449),
     'L3_gnn_br': (0.0, 2.0),
     'L3_gnn_bias': (0.0, 0.301),
     'L3_gnn_gamma': (1.0, 0.2),
     'L3_gnn_beta': (0.0, 0.1)}
    factors = {'L3_gnn_Wr': 17.442}
    for name, (base, spread) in spreads.items():
        noise = np.random.default_rng([zlib.crc32(name.encode()), seed]).standard_normal(out[name].shape)
        drawn = base * np.exp(spread * noise) if base else spread * noise
        out[name] = jnp.asarray(drawn.astype(out[name].dtype))
    for name, factor in factors.items():
        out[name] = (out[name] * factor).astype(out[name].dtype)
    return out
```

```python
from contextlib import ExitStack

import concourse.bass as bass
from concourse import mybir

F32 = mybir.dt.float32
I32 = mybir.dt.int32
U8 = mybir.dt.uint8
ALU = mybir.AluOpType
ACT = mybir.ActivationFunctionType
AX = mybir.AxisListType

P = 128
D = 128
T = 8
H = 4
CH = P * T
HALF = CH // 2
BN_EPS = 1e-5
LN_EPS = 1e-5
BIG = 3.0e38
FAR = 1 << 20


class Shapes:

    def __init__(self, n_nodes, n_edges):
        self.n, self.e = n_nodes, n_edges
        self.node_chunks = -(-n_nodes // CH)
        self.edge_chunks = -(-n_edges // CH)
        self.edge_tiles = self.edge_chunks * T
        self.edges_padded = self.edge_chunks * CH
        self.last_nodes = n_nodes - (self.node_chunks - 1) * CH
        assert self.last_nodes % T == 0 and n_nodes < FAR
        self.last_rows = self.last_nodes // T

    def rows(self, c):
        return self.last_rows if isinstance(c, int) and c == self.node_chunks - 1 else P


def used_before(c, lag):
    return not isinstance(c, int) or c >= lag


def sweep(eng, chunks, full, step):
    step(0, 0, 0)
    step(1, 1, 0)
    with eng.Fori(1, full // 2) as q:
        step(2 * q, 0, q)
        step(2 * q + 1, 1, q)
    for c in range(full // 2 * 2, chunks):
        step(c, c % 2, c // 2)


def node_rows(t, c, sh):
    if isinstance(c, int):
        part = t[c * CH:c * CH + sh.rows(c) * T, :]
    else:
        part = t[bass.ds(c * CH, CH), :]
    return part.rearrange("(p j) f -> p j f", j=T)


class Phase:

    def __init__(self, nc, name):
        self.nc, self.name, self.stack, self.sems = nc, name, ExitStack(), []

    def __enter__(self):
        self.stack.__enter__()
        return self

    def __exit__(self, *a):
        self.nc.clear_and_free_semaphores(self.sems)
        self.nc.all_engine_barrier()
        return self.stack.__exit__(*a)

    def sb(self, name, shape, dt=F32):
        return self.stack.enter_context(self.nc.sbuf_tensor(f"{self.name}_{name}", shape, dt))

    def ps(self, name, shape):
        return self.stack.enter_context(self.nc.psum_tensor(f"{self.name}_{name}", shape, F32))

    def sem(self, name):
        s = self.nc.alloc_semaphore(f"{self.name}_{name}")
        self.sems.append(s)
        return s

    def pair(self, name):
        return [self.sem(f"{name}{b}") for b in range(2)]


def spread_slots(ap, shape):
    return ap.unsqueeze(1).to_broadcast(shape)


def spread_features(ap, shape):
    return ap.unsqueeze(2).to_broadcast(shape)


RSQRT_GUESS = 0x5F3759DF
RSQRT_STEPS = 11


def rsqrt(dve, y, x, tmp, step, base):
    yi = y.bitcast(I32)
    dve.tensor_scalar(yi, x.bitcast(I32), 1, None, ALU.logical_shift_right).then_inc(step, 1)
    dve.wait_ge(step, base + 1)
    dve.tensor_scalar(yi, yi, -1.0, float(RSQRT_GUESS), ALU.mult, ALU.add).then_inc(step, 1)
    for i in range(3):
        dve.wait_ge(step, base + 2 + 3 * i)
        dve.tensor_tensor(tmp, y, y, ALU.mult).then_inc(step, 1)
        dve.wait_ge(step, base + 3 + 3 * i)
        dve.scalar_tensor_tensor(out=tmp, in0=tmp, scalar=-0.5, in1=x, op0=ALU.mult, op1=ALU.mult).then_inc(step, 1)
        dve.wait_ge(step, base + 4 + 3 * i)
        dve.scalar_tensor_tensor(out=y, in0=tmp, scalar=1.5, in1=y, op0=ALU.add, op1=ALU.mult).then_inc(step, 1)
    dve.wait_ge(step, base + RSQRT_STEPS)



def load_constants(nc, a, k):
    turned = {"pool1": a["L1_gnn_wpool1"], "self1": a["L1_gnn_wself1"], "eve1": a["L1_gnn_weve1"],
              "pool2": a["L1_gnn_wpool2"], "self2": a["L1_gnn_wself2"], "eve2": a["L1_gnn_weve2"],
              "sage_l1": a["L2_gnn_W1_l"], "sage_r1": a["L2_gnn_W1_r"],
              "sage_l2": a["L2_gnn_W2_l"], "sage_r2": a["L2_gnn_W2_r"]}
    plain = {"gcn0": a["L0_gnn_Ws"][0], "gcn1": a["L0_gnn_Ws"][1], "gcn2": a["L0_gnn_Ws"][2],
             "gat_l": a["L3_gnn_Wl"], "gat_r": a["L3_gnn_Wr"], "gat_e": a["L3_gnn_We"]}
    columns = {"gamma0": a["L0_gnn_gammas"][0], "gamma1": a["L0_gnn_gammas"][1], "gamma2": a["L0_gnn_gammas"][2],
               "beta0": a["L0_gnn_betas"][0], "beta1": a["L0_gnn_betas"][1], "beta2": a["L0_gnn_betas"][2],
               "bpool1": a["L1_gnn_bpool1"], "bpool2": a["L1_gnn_bpool2"],
               "bl": a["L3_gnn_bl"], "br": a["L3_gnn_br"],
               "att": a["L3_gnn_att"].rearrange("h c -> (h c)")}
    rows = {"gcn_b0": a["L0_gnn_bs"][0], "gcn_b1": a["L0_gnn_bs"][1], "gcn_b2": a["L0_gnn_bs"][2],
            "eve_b1": a["L1_gnn_bias1"], "eve_b2": a["L1_gnn_bias2"],
            "sage_b1": a["L2_gnn_b1"], "sage_b2": a["L2_gnn_b2"],
            "gat_b": a["L3_gnn_bias"], "gat_gamma": a["L3_gnn_gamma"], "gat_beta": a["L3_gnn_beta"]}
    heads, width = a["L3_gnn_att"].shape
    with Phase(nc, "const") as ph:
        raw = {n: ph.sb(f"raw_{n}", [P, D]) for n in turned}
        relu_b = ph.sb("relu_b", [P, 2])
        relu_bm = ph.sb("relu_bm", [P, 2, P])
        att_cols = ph.sb("att_cols", [P, D])
        psum = [ph.ps(f"turn{i}", [P, 512]) for i in range(2)]
        eve_ps = ph.ps("eve", [P, 512])
        loaded = ph.sem("loaded")
        cleared = ph.sem("cleared")
        ident_made = ph.sem("ident_made")
        turned_ps = ph.sem("turned_ps")
        turned_sb = ph.sem("turned_sb")
        relu_done = ph.sem("relu_done")
        eve_const = ph.sem("eve_const")
        misc = ph.sem("misc")
        loads = [(raw[n][:, :], w) for n, w in turned.items()]
        loads += [(k[n][0:w.shape[0], :], w) for n, w in plain.items()]
        loads += [(k[n][:, 0:1], w.rearrange("(f o) -> f o", o=1)) for n, w in columns.items()]
        loads += [(k[n][:, :], w.partition_broadcast(P)) for n, w in rows.items()]
        for i in (1, 2):
            loads += [(k[f"wconv{i}"][:, :], a[f"L1_gnn_wconv{i}"].partition_broadcast(P)),
                      (k[f"bconv{i}"][:, :], a[f"L1_gnn_bconv{i}"].partition_broadcast(P))]
        with nc.Block() as block:
            @block.sync
            def _(sp):
                for out, src in loads:
                    sp.dma_start(out, src).then_inc(loaded, 16)

            @block.gpsimd
            def _(pool):
                pool.memset(k["ident"][:, :], 0.0).then_inc(cleared, 1)
                pool.memset(k["head_att"][:, :], 0.0).then_inc(cleared, 1)
                pool.memset(k["ones"][:, :], 1.0).then_inc(cleared, 1)
                pool.memset(k["zeros"][:, :], 0.0).then_inc(cleared, 1)
                pool.wait_ge(cleared, 4)
                pool.affine_select(out=k["ident"][:, :], in_=k["ident"][:, :], compare_op=ALU.not_equal,
                                   fill=1.0, base=0, pattern=[[-1, P]], channel_multiplier=1).then_inc(ident_made, 1)

            @block.tensor
            def _(pe):
                pe.wait_ge(loaded, 16 * len(loads))
                pe.wait_ge(ident_made, 1)
                for i, n in enumerate(turned):
                    if i >= 2:
                        pe.wait_ge(turned_sb, i - 1)
                    pe.transpose(psum[i % 2][:, 0:D], raw[n][:, :], k["ident"][:, :]).then_inc(turned_ps, 1)
                pe.wait_ge(relu_done, 2)
                pe.wait_ge(turned_sb, len(turned))
                for i in (1, 2):
                    pe.matmul(eve_ps[:, (i - 1) * D:i * D], relu_bm[:, i - 1, :], k[f"eve{i}"][:, :],
                              start=True, stop=True).then_inc(eve_const, 1)

            @block.vector
            def _(dve):
                for i, n in enumerate(turned):
                    dve.wait_ge(turned_ps, i + 1)
                    dve.tensor_copy(k[n][:, :], psum[i % 2][:, 0:D]).then_inc(turned_sb, 1)
                for i in (1, 2):
                    dve.tensor_scalar(relu_b[:, i - 1:i], k[f"bconv{i}"][:, :], 0.0, None, ALU.max).then_inc(misc, 1)
                dve.wait_ge(misc, 2)
                for i in (1, 2):
                    dve.tensor_scalar(relu_bm[:, i - 1, :], k["ones"][:, :], relu_b[:, i - 1:i], None,
                                      ALU.mult).then_inc(relu_done, 1)
                dve.wait_ge(eve_const, 2)
                for i in (1, 2):
                    dve.tensor_copy(k[f"eve_c{i}"][:, :], eve_ps[:, (i - 1) * D:i * D]).then_inc(misc, 1)
                dve.wait_ge(misc, 4)
                for i in (1, 2):
                    dve.tensor_tensor(k[f"eve_b{i}"][:, :], k[f"eve_b{i}"][:, :], k[f"eve_c{i}"][:, :],
                                      ALU.add).then_inc(misc, 1)
                dve.tensor_tensor(k["blr"][:, :], k["bl"][:, :], k["br"][:, :], ALU.add).then_inc(misc, 1)
                dve.tensor_scalar(att_cols[:, :], k["ones"][:, :], k["att"][:, 0:1], None, ALU.mult).then_inc(misc, 1)
                dve.wait_ge(misc, 8)
                for h in range(heads):
                    s = slice(h * width, (h + 1) * width)
                    dve.tensor_copy(k["head_att"][s, s], att_cols[s, s]).then_inc(misc, 1)
                dve.wait_ge(misc, 8 + heads)


def edge_rows_load(eng, out, src, count, sem):
    groups = count // (P * P)
    whole = count // P
    eng.dma_start(out[:, 0:groups, :], src[0:groups * P * P].rearrange("(g t e) -> t g e", t=P, e=P)).then_inc(sem, 16)
    n = 16
    left = whole - groups * P
    if left:
        eng.dma_start(out[0:left, groups, :], src[groups * P * P:whole * P].rearrange("(t e) -> t e", e=P)).then_inc(sem, 16)
        n += 16
    rest = count - whole * P
    if rest:
        eng.dma_start(out[left:left + 1, groups, 0:rest], src[whole * P:count].rearrange("(t e) -> t e", t=1)).then_inc(sem, 16)
        n += 16
    return n


def index_tables(nc, a, k, dram, sh):
    groups = -(-sh.edge_tiles // P)
    tail = sh.edge_tiles - (groups - 1) * P
    with Phase(nc, "index") as ph:
        ints = {n: ph.sb(f"int_{n}", [P, groups, P], I32) for n in ("src", "dst", "next")}
        flts = {n: ph.sb(f"flt_{n}", [P, groups, P]) for n in ("src", "dst", "next", "ew", "place")}
        same = ph.sb("same", [P, groups, P])
        zero = ph.sb("zero", [P, T, D])
        edge_pad = ph.sb("edge_pad", [1, CH], I32)
        bank = [ph.ps(f"bank{i}", [P, 512]) for i in range(4)]
        filled = ph.sem("filled")
        loaded = ph.sem("loaded")
        zeroed = ph.sem("zeroed")
        padded = ph.sem("padded")
        calc = ph.sem("calc")
        in_psum = ph.sem("in_psum")
        out_sb = ph.sem("out_sb")
        n_loaded = []
        with nc.Block() as block:
            @block.gpsimd
            def _(pool):
                pool.memset(ints["src"][:, :, :], 0).then_inc(filled, 1)
                pool.memset(ints["dst"][:, :, :], FAR).then_inc(filled, 1)
                pool.memset(ints["next"][:, :, :], 2 * FAR).then_inc(filled, 1)
                pool.memset(flts["ew"][:, :, :], 0.0).then_inc(filled, 1)
                pool.memset(edge_pad[:, :], FAR).then_inc(filled, 1)
                pool.memset(k["first_dst"][:, :], -1).then_inc(filled, 1)
                pool.memset(zero[:, :, :], 0.0).then_inc(filled, 1)

            @block.sync
            def _(sp):
                sp.wait_ge(filled, 7)
                n = edge_rows_load(sp, ints["src"], a["src"], sh.e, loaded)
                n += edge_rows_load(sp, ints["dst"], a["dst"], sh.e, loaded)
                n += edge_rows_load(sp, ints["next"], a["dst"][1:sh.e], sh.e - 1, loaded)
                n += edge_rows_load(sp, flts["ew"], a["edge_weight"], sh.e, loaded)
                n_loaded.append(n)
                dp = dram["dst_padded"]
                sp.dma_start(dp[0:1], k["first_dst"][0:1, 0:1]).then_inc(padded, 16)
                sp.dma_start(dp[1:sh.e + 1].rearrange("(a b) -> a b", a=16), a["dst"].rearrange("(a b) -> a b", a=16)).then_inc(padded, 16)
                rest = sh.edges_padded - sh.e
                sp.dma_start(dp[sh.e + 1:sh.e + 1 + rest], edge_pad[0:1, 0:rest]).then_inc(padded, 16)
                full = sh.node_chunks
                with sp.Fori(0, full) as c:
                    sp.dma_start(dram["node_sums"][bass.ds(c * CH, CH), :].rearrange("(p j) f -> p j f", j=T),
                                 zero[:, :, :]).then_inc(zeroed, 16)
                sp.dma_start(dram["degree"].rearrange("(p c) o -> p (c o)", p=P),
                             zero[:, :, :].rearrange("p j f -> p (j f)")[:, 0:full * T]).then_inc(zeroed, 16)
                sp.wait_ge(zeroed, 16 * (full + 1))
                sp.wait_ge(padded, 48)

            order = [("src", "src_idx"), ("place", "place_idx"), ("dst", "dst_idx"), ("ew", "ew_tab")]

            @block.vector
            def _(dve):
                dve.wait_ge(loaded, n_loaded[0])
                for n in ("src", "dst", "next"):
                    dve.tensor_copy(flts[n][:, :, :], ints[n][:, :, :]).then_inc(calc, 1)
                dve.wait_ge(calc, 3)
                dve.tensor_tensor(same[:, :, :], flts["dst"][:, :, :], flts["next"][:, :, :], ALU.is_equal).then_inc(calc, 1)
                dve.wait_ge(calc, 4)
                dve.scalar_tensor_tensor(out=flts["place"][:, :, :], in0=same[:, :, :], scalar=float(FAR),
                                         in1=flts["dst"][:, :, :], op0=ALU.mult, op1=ALU.add).then_inc(calc, 1)
                dve.wait_ge(calc, 5)
                dve.tensor_scalar(flts["dst"][:, :, :], flts["dst"][:, :, :], float(sh.n - 1), None, ALU.min).then_inc(calc, 1)
                for i, (n, out) in enumerate(order):
                    dve.wait_ge(in_psum, i + 1)
                    dve.tensor_copy(k[out][:, :], bank[i][:, 0:sh.edge_tiles]).then_inc(out_sb, 1)
                dve.wait_ge(out_sb, len(order))

            @block.tensor
            def _(pe):
                pe.wait_ge(calc, 6)
                for i, (n, _) in enumerate(order):
                    for g in range(groups):
                        rows = P if g < groups - 1 else tail
                        mm = pe.transpose(bank[i][:, g * P:g * P + rows], flts[n][0:rows, g, :], k["ident"][0:rows, 0:rows])
                    mm.then_inc(in_psum, 1)


def run_masks(nc, a, k, dram, sh):
    real = sh.e - (sh.edge_chunks - 1) * CH
    with Phase(nc, "runs") as ph:
        dst_all = [ph.sb(f"dst_all{b}", [P, CH + 1], I32) for b in range(2)]
        pairs = [ph.sb(f"pairs{b}", [2, CH]) for b in range(2)]
        sums = [ph.sb(f"sums{b}", [2, CH]) for b in range(2)]
        dst_in = ph.pair("dst_in")
        ew_in = ph.pair("ew_in")
        ones_set = ph.sem("ones_set")
        masked = ph.sem("masked")
        summed = ph.sem("summed")
        stored = ph.pair("stored")
        with nc.Block() as block:
            @block.gpsimd
            def _(pool):
                for b in range(2):
                    pool.memset(pairs[b][:, :], 1.0).then_inc(ones_set, 1)

            @block.sync
            def _(sp):
                sp.wait_ge(ones_set, 2)

                def step(c, b, q):
                    if used_before(c, 2):
                        sp.wait_ge(masked, c - 1)
                    at = c * CH
                    sp.dma_start(dst_all[b][:, :], dram["dst_padded"][bass.ds(at, CH + 1)].partition_broadcast(P)).then_inc(dst_in[b], 16)
                    if used_before(c, 2):
                        sp.wait_ge(summed, c - 1)
                    n = real if isinstance(c, int) and c == sh.edge_chunks - 1 else CH
                    sp.dma_start(pairs[b][0:1, 0:n], a["edge_weight"][bass.ds(at, n)].partition_broadcast(1)).then_inc(ew_in[b], 16)

                sweep(sp, sh.edge_chunks, sh.edge_chunks - 1, step)

            @block.vector
            def _(dve):
                def step(c, b, q):
                    dve.wait_ge(dst_in[b], 16 * q + 16)
                    dve.tensor_tensor(k["same_run"][:, bass.ds(c * CH, CH)], dst_all[b][:, 1:CH + 1], dst_all[b][:, 0:CH],
                                      ALU.is_equal).then_inc(masked, 1)
                    dve.wait_ge(masked, c + 1)
                    dve.wait_ge(ew_in[b], 16 * q + 16)
                    if used_before(c, 1):
                        dve.wait_ge(summed, c)
                    if used_before(c, 2):
                        dve.wait_ge(stored[b], 16 * q)
                    start = sums[1 - b][:, CH - 1:CH] if used_before(c, 1) else 0.0
                    dve.tensor_tensor_scan(sums[b][:, :], k["same_run"][0:2, bass.ds(c * CH, CH)], pairs[b][:, :],
                                           start, ALU.mult, ALU.add).then_inc(summed, 1)

                sweep(dve, sh.edge_chunks, sh.edge_chunks - 1, step)

            @block.scalar
            def _(act):
                def step(c, b, q):
                    act.wait_ge(summed, c + 1)
                    act.dma_start(dram["run_sums"][:, bass.ds(c * CH, CH)], sums[b][:, :]).then_inc(stored[b], 16)

                sweep(act, sh.edge_chunks, sh.edge_chunks - 1, step)
                act.wait_ge(stored[0], 16 * ((sh.edge_chunks + 1) // 2))
                act.wait_ge(stored[1], 16 * (sh.edge_chunks // 2))


def degrees(nc, k, dram, sh):
    groups = -(-sh.edge_tiles // P)
    tail = sh.edge_tiles - (groups - 1) * P
    rows_of = [P] * (groups - 1) + [tail]
    with Phase(nc, "deg") as ph:
        run = [ph.sb(f"run{i}", [P, groups, P]) for i in range(2)]
        deg_tab = ph.sb("deg_tab", [P, sh.edge_tiles])
        w_tab = ph.sb("w_tab", [P, sh.edge_tiles])
        w_rows = ph.sb("w_rows", [P, groups, P])
        pos = ph.sb("pos", [P, sh.node_chunks * T])
        root = ph.sb("root", [P, sh.node_chunks * T])
        root_tmp = ph.sb("root_tmp", [P, sh.node_chunks * T])
        root_step = ph.sem("root_step")
        deg_slot = ph.sb("deg_slot", [P, T])
        idx_slot = ph.sb("idx_slot", [P, T], I32)
        got = ph.sb("got", [P, T])
        bank = [ph.ps(f"bank{i}", [P, 512]) for i in range(3)]
        loaded = ph.sem("loaded")
        in_psum = ph.sem("in_psum")
        tabs = ph.sem("tabs")
        slots = ph.sem("slots")
        gate = ph.sem("gate")
        scattered = ph.sem("scattered")
        deg_in = ph.sem("deg_in")
        dinv_calc = ph.sem("dinv_calc")
        dinv_out = ph.sem("dinv_out")
        gathered = ph.sem("gathered")
        weighted = ph.sem("weighted")
        w_in_rows = ph.sem("w_in_rows")
        w_out = ph.sem("w_out")
        loads = []
        with nc.Block() as block:
            @block.sync
            def _(sp):
                n = 0
                for i in range(2):
                    n += edge_rows_load(sp, run[i], dram["run_sums"][i], sh.edges_padded, loaded)
                loads.append(n)
                sp.wait_ge(scattered, 16 * sh.edge_tiles)
                sp.dma_start(k["dinv"][:, :].rearrange("p (c j) -> p c j", j=T),
                             dram["degree"].rearrange("(c p j) o -> p c (j o)", p=P, j=T)).then_inc(deg_in, 16)
                sp.wait_ge(dinv_calc, 4)
                sp.dma_start(dram["dinv"].rearrange("(c p j) o -> p c (j o)", p=P, j=T),
                             k["dinv"][:, :].rearrange("p (c j) -> p c j", j=T)).then_inc(dinv_out, 16)
                sp.wait_ge(w_in_rows, groups)
                wr = dram["edge_w"]
                sp.dma_start(wr[0:(groups - 1) * P * P].rearrange("(g t e) -> t g e", t=P, e=P),
                             w_rows[:, 0:groups - 1, :]).then_inc(w_out, 16)
                sp.dma_start(wr[(groups - 1) * P * P:sh.edges_padded].rearrange("(t e) -> t e", e=P),
                             w_rows[0:tail, groups - 1, :]).then_inc(w_out, 16)
                sp.wait_ge(w_out, 32)

            @block.tensor
            def _(pe):
                pe.wait_ge(loaded, loads[0])
                for i in range(2):
                    for g, r in enumerate(rows_of):
                        mm = pe.transpose(bank[i][:, g * P:g * P + r], run[i][0:r, g, :], k["ident"][0:r, 0:r])
                    mm.then_inc(in_psum, 1)
                pe.wait_ge(weighted, sh.edge_chunks)
                for g, r in enumerate(rows_of):
                    if g:
                        pe.wait_ge(w_in_rows, g)
                    pe.transpose(bank[2][0:r, 0:P], w_tab[:, g * P:g * P + r], k["ident"][:, :]).then_inc(in_psum, 1)

            @block.vector
            def _(dve):
                dve.wait_ge(in_psum, 1)
                dve.tensor_copy(deg_tab[:, :], bank[0][:, 0:sh.edge_tiles]).then_inc(tabs, 1)
                dve.wait_ge(in_psum, 2)
                dve.reciprocal(k["inv_count"][:, :], bank[1][:, 0:sh.edge_tiles]).then_inc(tabs, 1)
                dve.wait_ge(deg_in, 16)
                dve.tensor_scalar(k["dinv"][:, :], k["dinv"][:, :], 1.0, None, ALU.add).then_inc(dinv_calc, 1)
                dve.wait_ge(dinv_calc, 1)
                dve.tensor_scalar(pos[:, :], k["dinv"][:, :], 0.0, None, ALU.is_gt).then_inc(dinv_calc, 1)
                dve.tensor_scalar(k["dinv2"][:, :], k["dinv"][:, :], 1e-12, None, ALU.max).then_inc(dinv_calc, 1)
                dve.wait_ge(dinv_calc, 3)
                rsqrt(dve, root[:, :], k["dinv2"][:, :], root_tmp[:, :], root_step, 0)
                dve.tensor_tensor(k["dinv"][:, :], root[:, :], pos[:, :], ALU.mult).then_inc(dinv_calc, 1)
                dve.wait_ge(dinv_calc, 4)
                dve.tensor_tensor(k["dinv2"][:, :], k["dinv"][:, :], k["dinv"][:, :], ALU.mult).then_inc(tabs, 1)
                with dve.Fori(0, sh.edge_chunks) as c:
                    dve.wait_ge(gathered, 16 * T * c + 16 * T)
                    dve.tensor_tensor(w_tab[:, bass.ds(c * T, T)], got[:, :], k["ew_tab"][:, bass.ds(c * T, T)],
                                      ALU.mult).then_inc(weighted, 1)
                for g, r in enumerate(rows_of):
                    dve.wait_ge(in_psum, 3 + g)
                    dve.tensor_copy(w_rows[0:r, g, :], bank[2][0:r, 0:P]).then_inc(w_in_rows, 1)
                dve.wait_ge(w_in_rows, groups)
                dve.wait_ge(tabs, 3)

            @block.gpsimd
            def _(pool):
                nodes_end = pool.to_reg(sh.n - 1)
                pool.wait_ge(tabs, 1)
                with pool.Fori(0, sh.edge_chunks) as c:
                    pool.tensor_copy(deg_slot[:, :], deg_tab[:, bass.ds(c * T, T)]).then_inc(slots, 1)
                    pool.tensor_copy(idx_slot[:, :], k["place_idx"][:, bass.ds(c * T, T)]).then_inc(slots, 1)
                    pool.wait_ge(slots, 2 * c + 2)
                    pool.sem_inc(gate, 1)
                    for t in range(T):
                        pool.indirect_dma_start(dram["degree"][:, :], bass.IndirectOffsetOnAxis(idx_slot[:, t:t + 1], 0),
                                                deg_slot[:, t:t + 1], None, bounds_check=nodes_end,
                                                oob_is_err=False).then_inc(scattered, 16)
                    pool.wait_ge(scattered, 16 * T * c + 16 * T)
                    pool.sem_inc(gate, 1)
                pool.wait_ge(dinv_out, 16)
                with pool.Fori(0, sh.edge_chunks) as c:
                    pool.tensor_copy(idx_slot[:, :], k["src_idx"][:, bass.ds(c * T, T)]).then_inc(slots, 1)
                    pool.wait_ge(slots, c + 2 * sh.edge_chunks + 1)
                    pool.sem_inc(gate, 1)
                    for t in range(T):
                        pool.indirect_dma_start(got[:, t:t + 1], None, dram["dinv"][:, :],
                                                bass.IndirectOffsetOnAxis(idx_slot[:, t:t + 1], 0)).then_inc(gathered, 16)
                    pool.wait_ge(weighted, c + 1)
                    pool.sem_inc(gate, 1)



class EdgePhase(Phase):

    def __init__(self, nc, name, k, dram, sh, table, both_ends=False):
        super().__init__(nc, name)
        self.k, self.dram, self.sh, self.table = k, dram, sh, table
        self.ends = [("src", "src_idx")] + ([("dst", "dst_idx")] if both_ends else [])

    def __enter__(self):
        super().__enter__()
        self.rows = {n: [self.sb(f"rows_{n}{b}", [P, T, D]) for b in range(2)] for n, _ in self.ends}
        self.idx = {n: [self.sb(f"idx_{n}{b}", [P, T], I32) for b in range(2)] for n, _ in self.ends}
        self.place = [self.sb(f"place{b}", [P, T], I32) for b in range(2)]
        self.result = [self.sb(f"result{b}", [P, T, D]) for b in range(2)]
        self.gate = self.sem("gate")
        self.slots = self.sem("slots")
        self.place_set = self.sem("place_set")
        self.gathered = self.pair("gathered")
        self.turned = self.sem("turned")
        self.result_ready = self.sem("result_ready")
        self.scattered = self.pair("scattered")
        return self

    def pool_program(self, pool):
        sh, k, n_ends = self.sh, self.k, len(self.ends)
        nodes_end = pool.to_reg(sh.n - 1)

        def gather(c, b, q):
            if used_before(c, 2):
                pool.wait_ge(self.turned, 2 * c - 2)
                pool.sem_inc(self.gate, 1)
            for n, tab in self.ends:
                pool.tensor_copy(self.idx[n][b][:, :], k[tab][:, bass.ds(c * T, T)]).then_inc(self.slots, 1)
            pool.wait_ge(self.slots, n_ends * c + n_ends)
            pool.sem_inc(self.gate, 1)
            for t in range(T):
                for n, _ in self.ends:
                    pool.indirect_dma_start(self.rows[n][b][:, t, :], None, self.table[:, :],
                                            bass.IndirectOffsetOnAxis(self.idx[n][b][:, t:t + 1], 0)).then_inc(self.gathered[b], 16)

        def scatter(c, b):
            pool.wait_ge(self.result_ready, 2 * c + 2)
            pool.sem_inc(self.gate, 1)
            pool.tensor_copy(self.place[b][:, :], k["place_idx"][:, bass.ds(c * T, T)]).then_inc(self.place_set, 1)
            pool.wait_ge(self.place_set, c + 1)
            pool.sem_inc(self.gate, 1)
            for t in range(T):
                pool.indirect_dma_start(self.dram["node_sums"][:, :], bass.IndirectOffsetOnAxis(self.place[b][:, t:t + 1], 0),
                                        self.result[b][:, t, :], None, bounds_check=nodes_end,
                                        oob_is_err=False).then_inc(self.scattered[b], 16)

        def step(c, b, q):
            gather(c, b, q)
            if used_before(c, 2):
                scatter(c - 2, b)

        sweep(pool, sh.edge_chunks, sh.edge_chunks - 1, step)
        for c in (sh.edge_chunks - 2, sh.edge_chunks - 1):
            scatter(c, c % 2)
        pool.wait_ge(self.scattered[0], 16 * T * ((sh.edge_chunks + 1) // 2))
        pool.wait_ge(self.scattered[1], 16 * T * (sh.edge_chunks // 2))

    def rows_landed(self, eng, b, q):
        n = 16 * T * len(self.ends)
        eng.wait_ge(self.gathered[b], n * q + n)

    def result_free(self, eng, c, b, q):
        if used_before(c, 2):
            eng.wait_ge(self.scattered[b], 16 * T * q)


def half_no(c, h):
    return 2 * c + (h + 1)


def tiles_of(h):
    return range(H * h, H * h + H)


def gcn_edges(nc, k, dram, sh, name, table, weight, scale_shift):
    with EdgePhase(nc, name, k, dram, sh, table) as ph:
        w_all = [ph.sb(f"w_all{b}", [P, CH]) for b in range(2)]
        hT = [ph.sb(f"hT{b}", [P, CH]) for b in range(2)]
        sums = [ph.sb(f"sums{b}", [P, CH]) for b in range(2)]
        turn_ps = [ph.ps(f"turn{h}", [P, HALF]) for h in range(2)]
        out_ps = [ph.ps(f"out{h}", [P, HALF]) for h in range(2)]
        w_in = ph.pair("w_in")
        normed = ph.sem("normed")
        weighted = ph.sem("weighted")
        summed = ph.sem("summed")
        multiplied = ph.sem("multiplied")
        with nc.Block() as block:
            @block.gpsimd
            def _(pool):
                ph.pool_program(pool)

            @block.sync
            def _(sp):
                def step(c, b, q):
                    if used_before(c, 2):
                        sp.wait_ge(weighted, 2 * c - 2)
                    sp.dma_start(w_all[b][:, :], dram["edge_w"][bass.ds(c * CH, CH)].partition_broadcast(P)).then_inc(w_in[b], 16)

                sweep(sp, sh.edge_chunks, sh.edge_chunks - 1, step)

            @block.tensor
            def _(pe):
                def step(c, b, q):
                    for h in range(2):
                        if h == 0:
                            ph.rows_landed(pe, b, q)
                        if used_before(c, 1):
                            pe.wait_ge(normed, 2 * c + h - 1)
                        for i, t in enumerate(tiles_of(h)):
                            mm = pe.transpose(turn_ps[h][:, i * P:(i + 1) * P], ph.rows["src"][b][:, t, :], k["ident"][:, :])
                        mm.then_inc(ph.turned, 1)
                    for h in range(2):
                        pe.wait_ge(summed, 2 * c + h + 1)
                        if used_before(c, 1):
                            pe.wait_ge(ph.result_ready, 2 * c + h - 1)
                        for i, t in enumerate(tiles_of(h)):
                            mm = pe.matmul(out_ps[h][:, i * D:(i + 1) * D], sums[b][:, t * P:(t + 1) * P], weight[:, :],
                                           start=True, stop=True)
                        mm.then_inc(multiplied, 1)

                sweep(pe, sh.edge_chunks, sh.edge_chunks - 1, step)

            @block.scalar
            def _(act):
                def step(c, b, q):
                    for h in range(2):
                        act.wait_ge(ph.turned, 2 * c + h + 1)
                        if used_before(c, 2):
                            act.wait_ge(summed, 2 * c + h - 3)
                        s = slice(h * HALF, (h + 1) * HALF)
                        if scale_shift is None:
                            act.activation(hT[b][:, s], turn_ps[h][:, :], ACT.Copy).then_inc(normed, 1)
                        else:
                            act.activation(hT[b][:, s], turn_ps[h][:, :], ACT.Identity, bias=scale_shift[:, 1:2],
                                           scale=scale_shift[:, 0:1]).then_inc(normed, 1)
                    for h in range(2):
                        act.wait_ge(multiplied, 2 * c + h + 1)
                        ph.result_free(act, c, b, q)
                        act.activation(ph.result[b][:, H * h:H * h + H, :].rearrange("p t f -> p (t f)"), out_ps[h][:, :],
                                       ACT.Copy).then_inc(ph.result_ready, 1)

                sweep(act, sh.edge_chunks, sh.edge_chunks - 1, step)

            @block.vector
            def _(dve):
                def step(c, b, q):
                    for h in range(2):
                        s = slice(h * HALF, (h + 1) * HALF)
                        dve.wait_ge(normed, 2 * c + h + 1)
                        if h == 0:
                            dve.wait_ge(w_in[b], 16 * q + 16)
                        dve.tensor_tensor(hT[b][:, s], hT[b][:, s], w_all[b][:, s], ALU.mult).then_inc(weighted, 1)
                        dve.wait_ge(weighted, 2 * c + h + 1)
                        if used_before(c, 2):
                            dve.wait_ge(multiplied, 2 * c + h - 3)
                        if used_before(c, 1) or h:
                            dve.wait_ge(summed, 2 * c + h)
                        start = sums[b][:, HALF - 1:HALF] if h else sums[1 - b][:, CH - 1:CH] if used_before(c, 1) else 0.0
                        dve.tensor_tensor_scan(sums[b][:, s], k["same_run"][:, bass.ds(c * CH + h * HALF, HALF)], hT[b][:, s],
                                               start, ALU.mult, ALU.add).then_inc(summed, 1)

                sweep(dve, sh.edge_chunks, sh.edge_chunks - 1, step)


def eve_edges(nc, k, dram, sh, name, table, no):
    wpool, weve, bpool = k[f"pool{no}"], k[f"eve{no}"], k[f"bpool{no}"]
    wconv, bconv, const = k[f"wconv{no}"], k[f"bconv{no}"], k[f"eve_c{no}"]
    with EdgePhase(nc, name, k, dram, sh, table) as ph:
        xT = [ph.sb(f"xT{b}", [P, CH]) for b in range(2)]
        pT = [ph.sb(f"pT{b}", [P, CH]) for b in range(2)]
        begin = [ph.sb(f"begin{b}", [P, CH]) for b in range(2)]
        hi = [ph.sb(f"hi{b}", [P, CH]) for b in range(2)]
        lo = [ph.sb(f"lo{b}", [P, CH]) for b in range(2)]
        mix = [ph.sb(f"mix{b}", [P, CH]) for b in range(2)]
        turn_ps = [ph.ps(f"turn{h}", [P, HALF]) for h in range(2)]
        pool_ps = [ph.ps(f"pool{h}", [P, HALF]) for h in range(2)]
        out_ps = [ph.ps(f"out{h}", [P, HALF]) for h in range(2)]
        copied = ph.sem("copied")
        pooled_ps = ph.sem("pooled_ps")
        pooled = ph.sem("pooled")
        begun = ph.sem("begun")
        hi_done = ph.sem("hi_done")
        lo_done = ph.sem("lo_done")
        lo_scaled = ph.sem("lo_scaled")
        mixed = ph.sem("mixed")
        mix_relu = ph.sem("mix_relu")
        multiplied = ph.sem("multiplied")
        with nc.Block() as block:
            @block.gpsimd
            def _(pool):
                ph.pool_program(pool)

            @block.tensor
            def _(pe):
                def step(c, b, q):
                    for h in range(2):
                        if h == 0:
                            ph.rows_landed(pe, b, q)
                        if used_before(c, 1):
                            pe.wait_ge(copied, 2 * c + h - 1)
                        for i, t in enumerate(tiles_of(h)):
                            mm = pe.transpose(turn_ps[h][:, i * P:(i + 1) * P], ph.rows["src"][b][:, t, :], k["ident"][:, :])
                        mm.then_inc(ph.turned, 1)
                    for h in range(2):
                        pe.wait_ge(copied, 2 * c + h + 1)
                        if used_before(c, 1):
                            pe.wait_ge(pooled, 2 * c + h - 1)
                        pe.matmul(pool_ps[h][:, :], wpool[:, :], xT[b][:, h * HALF:(h + 1) * HALF], start=True,
                                  stop=True).then_inc(pooled_ps, 1)
                    for h in range(2):
                        pe.wait_ge(mix_relu, 2 * c + h + 1)
                        if used_before(c, 1):
                            pe.wait_ge(ph.result_ready, 2 * c + h - 1)
                        for i, t in enumerate(tiles_of(h)):
                            mm = pe.matmul(out_ps[h][:, i * D:(i + 1) * D], mix[b][:, t * P:(t + 1) * P], weve[:, :],
                                           start=True, stop=True)
                        mm.then_inc(multiplied, 1)

                sweep(pe, sh.edge_chunks, sh.edge_chunks - 1, step)

            @block.scalar
            def _(act):
                def step(c, b, q):
                    if used_before(c, 2):
                        act.wait_ge(lo_done, 2 * c - 2)
                    act.sem_inc(ph.gate, 1)
                    act.activation(begin[b][:, :], k["same_run"][:, bass.ds(c * CH, CH)], ACT.Copy, bias=BIG,
                                   scale=-BIG).then_inc(begun, 1)
                    for h in range(2):
                        s = slice(h * HALF, (h + 1) * HALF)
                        act.wait_ge(ph.turned, 2 * c + h + 1)
                        if used_before(c, 2):
                            act.wait_ge(pooled_ps, 2 * c + h - 3)
                        act.activation(xT[b][:, s], turn_ps[h][:, :], ACT.Copy).then_inc(copied, 1)
                    for h in range(2):
                        s = slice(h * HALF, (h + 1) * HALF)
                        act.wait_ge(pooled_ps, 2 * c + h + 1)
                        if used_before(c, 2):
                            act.wait_ge(lo_done, 2 * c + h - 3)
                        act.activation(pT[b][:, s], pool_ps[h][:, :], ACT.Relu, bias=bpool[:, 0:1]).then_inc(pooled, 1)
                    for h in range(2):
                        s = slice(h * HALF, (h + 1) * HALF)
                        act.wait_ge(lo_done, 2 * c + h + 1)
                        if used_before(c, 2):
                            act.wait_ge(multiplied, 2 * c + h - 3)
                        act.activation(mix[b][:, s], lo[b][:, s], ACT.Identity, bias=bconv[:, 0:1],
                                       scale=wconv[:, 1:2]).then_inc(lo_scaled, 1)
                    for h in range(2):
                        s = slice(h * HALF, (h + 1) * HALF)
                        act.wait_ge(mixed, 2 * c + h + 1)
                        act.activation(mix[b][:, s], mix[b][:, s], ACT.Relu).then_inc(mix_relu, 1)

                sweep(act, sh.edge_chunks, sh.edge_chunks - 1, step)

            @block.vector
            def _(dve):
                def step(c, b, q):
                    for h in range(2):
                        s = slice(h * HALF, (h + 1) * HALF)
                        at = bass.ds(c * CH + h * HALF, HALF)
                        dve.wait_ge(pooled, 2 * c + h + 1)
                        if h == 0:
                            dve.wait_ge(begun, c + 1)
                        if used_before(c, 2):
                            dve.wait_ge(mixed, 2 * c + h - 3)
                        if used_before(c, 1) or h:
                            dve.wait_ge(hi_done, 2 * c + h)
                            dve.wait_ge(lo_done, 2 * c + h)
                        go_on = (lambda z: z[b][:, HALF - 1:HALF] if h else z[1 - b][:, CH - 1:CH] if used_before(c, 1) else 0.0)
                        dve.tensor_tensor_scan(hi[b][:, s], k["same_run"][:, at], pT[b][:, s], go_on(hi), ALU.mult,
                                               ALU.max).then_inc(hi_done, 1)
                        if used_before(c, 2):
                            dve.wait_ge(lo_scaled, 2 * c + h - 3)
                        dve.tensor_tensor_scan(lo[b][:, s], begin[b][:, s], pT[b][:, s], go_on(lo), ALU.add,
                                               ALU.min).then_inc(lo_done, 1)
                    for h in range(2):
                        s = slice(h * HALF, (h + 1) * HALF)
                        dve.wait_ge(lo_scaled, 2 * c + h + 1)
                        dve.wait_ge(hi_done, 2 * c + h + 1)
                        dve.scalar_tensor_tensor(out=mix[b][:, s], in0=hi[b][:, s], scalar=wconv[:, 0:1], in1=mix[b][:, s],
                                                 op0=ALU.mult, op1=ALU.add).then_inc(mixed, 1)
                    for h in range(2):
                        dve.wait_ge(multiplied, 2 * c + h + 1)
                        ph.result_free(dve, c, b, q)
                        dve.tensor_tensor(ph.result[b][:, H * h:H * h + H, :], out_ps[h][:, :].rearrange("p (t f) -> p t f", f=D),
                                          spread_slots(const[:, :], [P, H, D]), ALU.subtract).then_inc(ph.result_ready, 1)

                sweep(dve, sh.edge_chunks, sh.edge_chunks - 1, step)


def sage_edges(nc, k, dram, sh, name, table, weight):
    with EdgePhase(nc, name, k, dram, sh, table) as ph:
        sums = [ph.sb(f"sums{b}", [P, CH]) for b in range(2)]
        turn_ps = [ph.ps(f"turn{h}", [P, HALF]) for h in range(2)]
        out_ps = [ph.ps(f"out{h}", [P, HALF]) for h in range(2)]
        summed = ph.sem("summed")
        multiplied = ph.sem("multiplied")
        with nc.Block() as block:
            @block.gpsimd
            def _(pool):
                ph.pool_program(pool)

            @block.tensor
            def _(pe):
                def step(c, b, q):
                    for h in range(2):
                        if h == 0:
                            ph.rows_landed(pe, b, q)
                        if used_before(c, 1):
                            pe.wait_ge(summed, 2 * c + h - 1)
                        for i, t in enumerate(tiles_of(h)):
                            mm = pe.transpose(turn_ps[h][:, i * P:(i + 1) * P], ph.rows["src"][b][:, t, :], k["ident"][:, :])
                        mm.then_inc(ph.turned, 1)
                    for h in range(2):
                        pe.wait_ge(summed, 2 * c + h + 1)
                        if used_before(c, 1):
                            pe.wait_ge(ph.result_ready, 2 * c + h - 1)
                        for i, t in enumerate(tiles_of(h)):
                            mm = pe.matmul(out_ps[h][:, i * D:(i + 1) * D], sums[b][:, t * P:(t + 1) * P], weight[:, :],
                                           start=True, stop=True)
                        mm.then_inc(multiplied, 1)

                sweep(pe, sh.edge_chunks, sh.edge_chunks - 1, step)

            @block.vector
            def _(dve):
                def step(c, b, q):
                    for h in range(2):
                        s = slice(h * HALF, (h + 1) * HALF)
                        dve.wait_ge(ph.turned, 2 * c + h + 1)
                        if used_before(c, 2):
                            dve.wait_ge(multiplied, 2 * c + h - 3)
                        if used_before(c, 1) or h:
                            dve.wait_ge(summed, 2 * c + h)
                        start = sums[b][:, HALF - 1:HALF] if h else sums[1 - b][:, CH - 1:CH] if used_before(c, 1) else 0.0
                        dve.tensor_tensor_scan(sums[b][:, s], k["same_run"][:, bass.ds(c * CH + h * HALF, HALF)],
                                               turn_ps[h][:, :], start, ALU.mult, ALU.add).then_inc(summed, 1)
                    for h in range(2):
                        dve.wait_ge(multiplied, 2 * c + h + 1)
                        ph.result_free(dve, c, b, q)
                        dve.tensor_tensor(ph.result[b][:, H * h:H * h + H, :], out_ps[h][:, :].rearrange("p (t f) -> p t f", f=D),
                                          spread_features(k["inv_count"][:, bass.ds(c * T + h * H, H)], [P, H, D]),
                                          ALU.mult).then_inc(ph.result_ready, 1)

                sweep(dve, sh.edge_chunks, sh.edge_chunks - 1, step)


def gat_edges(nc, a, k, dram, sh, name, table):
    n_attr = a["edge_attr_16"].shape[1]
    real = sh.e - (sh.edge_chunks - 1) * CH
    with EdgePhase(nc, name, k, dram, sh, table, both_ends=True) as ph:
        attr = [ph.sb(f"attr{b}", [P, T, n_attr]) for b in range(2)]
        sT = [ph.sb(f"sT{h}", [P, HALF]) for h in range(2)]
        dT = [ph.sb(f"dT{h}", [P, HALF]) for h in range(2)]
        eT = [ph.sb(f"eT{h}", [n_attr, HALF]) for h in range(2)]
        val = [ph.sb(f"val{h}", [P, HALF]) for h in range(2)]
        pre = [ph.sb(f"pre{h}", [P, HALF]) for h in range(2)]
        top = [ph.sb(f"top{h}", [P, HALF + 1]) for h in range(2)]
        begin = [ph.sb(f"begin{h}", [P, HALF]) for h in range(2)]
        fall = [ph.sb(f"fall{h}", [P, HALF]) for h in range(2)]
        prob = [ph.sb(f"prob{h}", [P, HALF]) for h in range(2)]
        num = [ph.sb(f"num{h}", [P, HALF]) for h in range(2)]
        den = [ph.sb(f"den{h}", [P, HALF]) for h in range(2)]
        mean = [ph.sb(f"mean{h}", [P, HALF]) for h in range(2)]
        src_ps = ph.ps("src", [P, HALF])
        dst_ps = ph.ps("dst", [P, HALF])
        attr_ps = ph.ps("attr", [P, HALF])
        val_ps = ph.ps("val", [P, HALF])
        pre_ps = ph.ps("pre", [P, HALF])
        logit_ps = ph.ps("logit", [P, HALF])
        out_ps = ph.ps("out", [P, HALF])
        attr_in = ph.pair("attr_in")
        attr_set = ph.sem("attr_set")
        in_sb = ph.sem("in_sb")
        val_mm = ph.sem("val_mm")
        pre_mm = ph.sem("pre_mm")
        val_set = ph.sem("val_set")
        pre_set = ph.sem("pre_set")
        leaky = ph.sem("leaky")
        logits = ph.sem("logits")
        begun = ph.sem("begun")
        topped = ph.sem("topped")
        diffs = ph.sem("diffs")
        lowered = ph.sem("lowered")
        exps = ph.sem("exps")
        probs_v = ph.sem("probs_v")
        num_done = ph.sem("num_done")
        den_done = ph.sem("den_done")
        guarded = ph.sem("guarded")
        divided = ph.sem("divided")
        multiplied = ph.sem("multiplied")
        top_set = ph.sem("top_set")
        with nc.Block() as block:
            @block.gpsimd
            def _(pool):
                pool.memset(attr[(sh.edge_chunks - 1) % 2][:, :, :], 0.0).then_inc(attr_set, 1)
                ph.pool_program(pool)

            @block.sync
            def _(sp):
                sp.wait_ge(attr_set, 1)

                def step(c, b, q):
                    if used_before(c, 2):
                        sp.wait_ge(ph.turned, 2 * c - 2)
                    ea = a["edge_attr_16"]
                    if isinstance(c, int) and c == sh.edge_chunks - 1:
                        whole, left = real // P, real % P
                        sp.dma_start(attr[b][:, 0:whole, :], ea[c * CH:c * CH + whole * P, :].rearrange("(t p) d -> p t d", p=P)).then_inc(attr_in[b], 16)
                        sp.dma_start(attr[b][0:left, whole, :], ea[c * CH + whole * P:sh.e, :]).then_inc(attr_in[b], 16)
                    else:
                        sp.dma_start(attr[b][:, :, :], ea[bass.ds(c * CH, CH), :].rearrange("(t p) d -> p t d", p=P)).then_inc(attr_in[b], 16)

                sweep(sp, sh.edge_chunks, sh.edge_chunks - 1, step)

            @block.tensor
            def _(pe):
                def front(c, b, q, h):
                    if h == 0:
                        ph.rows_landed(pe, b, q)
                        last = isinstance(c, int) and c == sh.edge_chunks - 1
                        pe.wait_ge(attr_in[b], 16 * q + 16 + (16 if last else 0))
                    if used_before(c, 1) or h:
                        pe.wait_ge(in_sb, 3 * (2 * c + h))
                    for i, t in enumerate(tiles_of(h)):
                        pe.transpose(src_ps[:, i * P:(i + 1) * P], ph.rows["src"][b][:, t, :], k["ident"][:, :])
                        pe.transpose(dst_ps[:, i * P:(i + 1) * P], ph.rows["dst"][b][:, t, :], k["ident"][:, :])
                        mm = pe.transpose(attr_ps[0:n_attr, i * P:(i + 1) * P], attr[b][:, t, :], k["ident"][:, :])
                    mm.then_inc(ph.turned, 1)
                    pe.wait_ge(in_sb, 3 * (2 * c + h) + 3)
                    if used_before(c, 1) or h:
                        pe.wait_ge(val_set, 2 * c + h)
                    pe.matmul(val_ps[:, :], k["gat_l"][:, :], sT[h][:, :], start=True, stop=True).then_inc(val_mm, 1)
                    if used_before(c, 1) or h:
                        pe.wait_ge(pre_set, 2 * c + h)
                    pe.matmul(pre_ps[:, :], k["gat_l"][:, :], sT[h][:, :], start=True, stop=False)
                    pe.matmul(pre_ps[:, :], k["gat_r"][:, :], dT[h][:, :], start=False, stop=False)
                    pe.matmul(pre_ps[:, :], k["gat_e"][0:n_attr, :], eT[h][:, :], start=False, stop=True).then_inc(pre_mm, 1)
                    pe.wait_ge(leaky, 2 * c + h + 1)
                    if used_before(c, 1) or h:
                        pe.wait_ge(lowered, 2 * c + h)
                    pe.matmul(logit_ps[:, :], k["head_att"][:, :], pre[h][:, :], start=True, stop=True).then_inc(logits, 1)

                def back(c, b, q, h):
                    pe.wait_ge(divided, 2 * c + h + 1)
                    if used_before(c, 1) or h:
                        pe.wait_ge(ph.result_ready, 2 * c + h)
                    for i in range(H):
                        mm = pe.transpose(out_ps[:, i * P:(i + 1) * P], mean[h][:, i * P:(i + 1) * P], k["ident"][:, :])
                    mm.then_inc(multiplied, 1)

                def step(c, b, q):
                    front(c, b, q, 0)
                    front(c, b, q, 1)
                    back(c, b, q, 0)
                    back(c, b, q, 1)

                sweep(pe, sh.edge_chunks, sh.edge_chunks - 1, step)

            @block.scalar
            def _(act):
                def step(c, b, q):
                    for h in range(2):
                        act.wait_ge(ph.turned, 2 * c + h + 1)
                        if used_before(c, 1):
                            act.wait_ge(pre_mm, 2 * c + h - 1)
                        act.activation(sT[h][:, :], src_ps[:, :], ACT.Copy).then_inc(in_sb, 1)
                        act.activation(dT[h][:, :], dst_ps[:, :], ACT.Copy).then_inc(in_sb, 1)
                        act.activation(eT[h][:, :], attr_ps[0:n_attr, :], ACT.Copy).then_inc(in_sb, 1)
                        act.wait_ge(val_mm, 2 * c + h + 1)
                        if used_before(c, 1):
                            act.wait_ge(probs_v, 2 * c + h - 1)
                        act.activation(val[h][:, :], val_ps[:, :], ACT.Identity, bias=k["bl"][:, 0:1]).then_inc(val_set, 1)
                        act.wait_ge(pre_mm, 2 * c + h + 1)
                        if used_before(c, 1):
                            act.wait_ge(logits, 2 * c + h - 1)
                        act.activation(pre[h][:, :], pre_ps[:, :], ACT.Identity, bias=k["blr"][:, 0:1]).then_inc(pre_set, 1)
                        if used_before(c, 1):
                            act.wait_ge(diffs, 2 * c + h - 1)
                            act.sem_inc(ph.gate, 1)
                        act.activation(begin[h][:, :], k["same_run"][:, bass.ds(c * CH + h * HALF, HALF)], ACT.Copy,
                                       bias=-BIG, scale=BIG).then_inc(begun, 1)
                    for h in range(2):
                        act.wait_ge(lowered, 2 * c + h + 1)
                        act.activation(fall[h][:, :], fall[h][:, :], ACT.Exp).then_inc(exps, 1)
                        act.activation(prob[h][:, :], prob[h][:, :], ACT.Exp).then_inc(exps, 1)
                    for h in range(2):
                        act.wait_ge(multiplied, 2 * c + h + 1)
                        ph.result_free(act, c, b, q)
                        act.activation(ph.result[b][:, H * h:H * h + H, :].rearrange("p t f -> p (t f)"), out_ps[:, :],
                                       ACT.Copy).then_inc(ph.result_ready, 1)

                sweep(act, sh.edge_chunks, sh.edge_chunks - 1, step)

            @block.vector
            def _(dve):
                dve.memset(top[1][:, HALF:HALF + 1], 0.0).then_inc(top_set, 1)
                dve.wait_ge(top_set, 1)

                def front(c, b, q, h):
                    dve.wait_ge(pre_set, 2 * c + h + 1)
                    dve.scalar_tensor_tensor(out=pre[h][:, :], in0=pre[h][:, :], scalar=0.2, in1=pre[h][:, :], op0=ALU.mult,
                                             op1=ALU.max).then_inc(leaky, 1)
                    if used_before(c, 1):
                        dve.wait_ge(diffs, 2 * c + h - 1)
                        dve.wait_ge(exps, 2 * (2 * c + h - 1))
                    if used_before(c, 1) or h:
                        dve.wait_ge(topped, 2 * c + h)
                    dve.tensor_copy(top[h][:, 0:1], top[1 - h][:, HALF:HALF + 1]).then_inc(top_set, 1)
                    dve.wait_ge(top_set, 2 * c + h + 2)
                    dve.wait_ge(logits, 2 * c + h + 1)
                    dve.wait_ge(begun, 2 * c + h + 1)
                    dve.tensor_tensor_scan(top[h][:, 1:HALF + 1], begin[h][:, :], logit_ps[:, :], top[h][:, 0:1], ALU.add,
                                           ALU.max).then_inc(topped, 1)
                    if used_before(c, 1):
                        dve.wait_ge(num_done, 2 * c + h - 1)
                        dve.wait_ge(den_done, 2 * c + h - 1)
                    dve.wait_ge(topped, 2 * c + h + 1)
                    dve.tensor_tensor(fall[h][:, :], top[h][:, 0:HALF], begin[h][:, :], ALU.add).then_inc(diffs, 1)
                    dve.wait_ge(diffs, 2 * c + h + 1)
                    dve.tensor_tensor(prob[h][:, :], logit_ps[:, :], top[h][:, 1:HALF + 1], ALU.subtract)
                    dve.tensor_tensor(fall[h][:, :], fall[h][:, :], top[h][:, 1:HALF + 1], ALU.subtract).then_inc(lowered, 1)

                def back(c, b, q, h):
                    dve.wait_ge(exps, 2 * (2 * c + h + 1))
                    go_on = (lambda z: z[1 - h][:, HALF - 1:HALF] if h or used_before(c, 1) else 0.0)
                    if used_before(c, 1) or h:
                        dve.wait_ge(den_done, 2 * c + h)
                        dve.wait_ge(num_done, 2 * c + h)
                    if used_before(c, 1):
                        dve.wait_ge(divided, 2 * c + h - 1)
                    dve.tensor_tensor_scan(den[h][:, :], fall[h][:, :], prob[h][:, :], go_on(den), ALU.mult,
                                           ALU.add).then_inc(den_done, 1)
                    dve.tensor_tensor(val[h][:, :], val[h][:, :], prob[h][:, :], ALU.mult).then_inc(probs_v, 1)
                    dve.wait_ge(probs_v, 2 * c + h + 1)
                    dve.tensor_tensor_scan(num[h][:, :], fall[h][:, :], val[h][:, :], go_on(num), ALU.mult,
                                           ALU.add).then_inc(num_done, 1)
                    dve.wait_ge(num_done, 2 * c + h + 1)
                    dve.wait_ge(den_done, 2 * c + h + 1)
                    if used_before(c, 1):
                        dve.wait_ge(multiplied, 2 * c + h - 1)
                    dve.tensor_scalar(mean[h][:, :], den[h][:, :], 1e-16, None, ALU.add).then_inc(guarded, 1)
                    dve.wait_ge(guarded, 2 * (2 * c + h) + 1)
                    dve.reciprocal(mean[h][:, :], mean[h][:, :]).then_inc(guarded, 1)
                    dve.wait_ge(guarded, 2 * (2 * c + h) + 2)
                    dve.tensor_tensor(mean[h][:, :], num[h][:, :], mean[h][:, :], ALU.mult).then_inc(divided, 1)

                def step(c, b, q):
                    front(c, b, q, 0)
                    front(c, b, q, 1)
                    back(c, b, q, 0)
                    back(c, b, q, 1)

                sweep(dve, sh.edge_chunks, sh.edge_chunks - 1, step)



class LayerNorm:
    STEPS = 7 + RSQRT_STEPS

    def __init__(self, ph, name):
        self.stats = [ph.sb(f"{name}_stats{b}", [P, T, 6]) for b in range(2)]
        self.tmp = [ph.sb(f"{name}_tmp{b}", [P, 3, T]) for b in range(2)]
        self.scale = [ph.sb(f"{name}_scale{b}", [P, T]) for b in range(2)]
        self.shift = [ph.sb(f"{name}_shift{b}", [P, T]) for b in range(2)]
        self.step = ph.sem(f"{name}_step")
        self.ready = ph.sem(f"{name}_ready")

    def on_vector(self, dve, z, n, c, b):
        base = c * self.STEPS
        s, t = self.stats[b], self.tmp[b]
        for j in range(T):
            ins = dve.bn_stats(s[0:n, j, :], z[0:n, j, :])
        ins.then_inc(self.step, 1)
        dve.wait_ge(self.step, base + 1)
        me, mo, ve, vo = (s[0:n, :, i] for i in (1, 4, 2, 5))
        dve.tensor_tensor(t[0:n, 0, :], me, mo, ALU.subtract).then_inc(self.step, 1)
        dve.tensor_tensor(t[0:n, 1, :], ve, vo, ALU.add).then_inc(self.step, 1)
        dve.tensor_tensor(t[0:n, 2, :], me, mo, ALU.add).then_inc(self.step, 1)
        dve.wait_ge(self.step, base + 4)
        dve.scalar_tensor_tensor(out=t[0:n, 0, :], in0=t[0:n, 0, :], scalar=D / 4.0, in1=t[0:n, 0, :], op0=ALU.mult,
                                 op1=ALU.mult).then_inc(self.step, 1)
        dve.wait_ge(self.step, base + 5)
        dve.tensor_tensor(t[0:n, 1, :], t[0:n, 1, :], t[0:n, 0, :], ALU.add).then_inc(self.step, 1)
        dve.wait_ge(self.step, base + 6)
        dve.tensor_scalar(t[0:n, 1, :], t[0:n, 1, :], 1.0 / D, LN_EPS, ALU.mult, ALU.add).then_inc(self.step, 1)
        dve.wait_ge(self.step, base + 7)
        scale = self.scale[b][0:n, :]
        rsqrt(dve, scale, t[0:n, 1, :], t[0:n, 0, :], self.step, base + 7)
        dve.scalar_tensor_tensor(out=self.shift[b][0:n, :], in0=t[0:n, 2, :], scalar=-0.5, in1=scale,
                                 op0=ALU.mult, op1=ALU.mult).then_inc(self.ready, 1)

    def apply(self, act, out, z, n, c, b, done):
        act.wait_ge(self.ready, c + 1)
        for j in range(T):
            ins = act.activation(out[0:n, j, :], z[0:n, j, :], ACT.Identity, bias=self.shift[b][0:n, j:j + 1],
                                 scale=self.scale[b][0:n, j:j + 1])
        ins.then_inc(done, 1)


class NodePhase(Phase):

    def __init__(self, nc, name, sh, streams, out):
        super().__init__(nc, name)
        self.sh, self.streams, self.out_dram = sh, streams, out

    def __enter__(self):
        super().__enter__()
        self.buf = {n: [self.sb(f"in_{n}{b}", [P, T, D]) for b in range(2)] for n in self.streams}
        self.landed = {n: self.pair(f"landed_{n}") for n in self.streams}
        self.out_ready = self.sem("out_ready")
        self.stored = self.pair("stored")
        return self

    def load_program(self, sp, free):
        def step(c, b, q):
            n = self.sh.rows(c)
            for name, src in self.streams.items():
                if used_before(c, 2):
                    for sem, per in free[name]:
                        sp.wait_ge(sem, per * (c - 1))
                sp.dma_start(self.buf[name][b][0:n, :, :], node_rows(src, c, self.sh)).then_inc(self.landed[name][b], 16)

        self.node_sweep(sp, step)

    def node_sweep(self, eng, step):
        sweep(eng, self.sh.node_chunks, self.sh.node_chunks - 1, step)

    def have(self, eng, name, b, q):
        eng.wait_ge(self.landed[name][b], 16 * q + 16)

    def store(self, eng, out, c, b):
        n = self.sh.rows(c)
        eng.wait_ge(self.out_ready, c + 1)
        eng.dma_start(node_rows(self.out_dram, c, self.sh), out[b][0:n, :, 0:D]).then_inc(self.stored[b], 16)

    def out_free(self, eng, c, b, q):
        if used_before(c, 2):
            eng.wait_ge(self.stored[b], 16 * q)

    def all_stored(self, eng):
        eng.wait_ge(self.stored[0], 16 * ((self.sh.node_chunks + 1) // 2))
        eng.wait_ge(self.stored[1], 16 * (self.sh.node_chunks // 2))


def own_product(ph, pe, k, x, weight, turn_ps, out_ps, turned, in_sb, out_read, multiplied, hT, c, b, q, between=None):
    n = ph.sh.rows(c)
    for h in range(2):
        if h == 0:
            ph.have(pe, x, b, q)
        if used_before(c, 1):
            pe.wait_ge(in_sb, 2 * c + h - 1)
        for i, t in enumerate(tiles_of(h)):
            mm = pe.transpose(turn_ps[h][:, i * P:i * P + n], ph.buf[x][b][0:n, t, :], k["ident"][0:n, 0:n])
        mm.then_inc(turned, 1)
    if between:
        between()
    for h in range(2):
        pe.wait_ge(in_sb, 2 * c + h + 1)
        if used_before(c, 2):
            pe.wait_ge(out_read, 2 * c + h - 3)
        for i, t in enumerate(tiles_of(h)):
            mm = pe.matmul(out_ps[b][h][0:n, i * D:(i + 1) * D], hT[b][:, t * P:t * P + n], weight[:, :], start=True, stop=True)
        mm.then_inc(multiplied, 1)


def turned_to_sbuf(act, ph, turn_ps, turned, multiplied, in_sb, hT, c, b, scale_shift=None):
    n = ph.sh.rows(c)
    for h in range(2):
        act.wait_ge(turned, 2 * c + h + 1)
        if used_before(c, 2):
            act.wait_ge(multiplied, 2 * c + h - 3)
        out = hT[b][:, h * HALF:(h + 1) * HALF].rearrange("p (t n) -> p t n", n=P)[:, :, 0:n]
        src = turn_ps[h][:, :].rearrange("p (t n) -> p t n", n=P)[:, :, 0:n]
        if scale_shift is None:
            act.activation(out, src, ACT.Copy).then_inc(in_sb, 1)
        else:
            act.activation(out, src, ACT.Identity, bias=scale_shift[:, 1:2], scale=scale_shift[:, 0:1]).then_inc(in_sb, 1)


def gcn_nodes(nc, k, dram, sh, name, no, table, x0, out, scale_shift, next_scale_shift, as_rows=None):
    first, last = no == 0, no == 2
    streams = {"y": table, "sums": dram["node_sums"]}
    if not first:
        streams["x0"] = x0
    res = "y" if first else "x0"
    weight, bias = k[f"gcn{no}"], k[f"gcn_b{no}"]
    with NodePhase(nc, name, sh, streams, out) as ph:
        hT = [ph.sb(f"hT{b}", [P, CH]) for b in range(2)]
        res_b = [ph.sb(f"res_b{b}", [P, T, D]) for b in range(2)]
        acc = [ph.sb(f"acc{b}", [P, T, D]) for b in range(2)]
        y1 = [ph.sb(f"y1{b}", [P, T, D + 1]) for b in range(2)]
        small = ph.sb("small", [P, 8])
        diag = ph.sb("diag", [P, D])
        turn_ps = [ph.ps(f"turn{h}", [P, HALF]) for h in range(2)]
        out_ps = [[ph.ps(f"out{b}{h}", [P, HALF]) for h in range(2)] for b in range(2)]
        gram = ph.ps("gram", [P, 512])
        turned, in_sb, multiplied = ph.sem("turned"), ph.sem("in_sb"), ph.sem("multiplied")
        ones_set = ph.sem("ones_set")
        res_done, sums_done = ph.sem("res_done"), ph.sem("sums_done")
        own_done, added, finished = ph.sem("own_done"), ph.sem("added"), ph.sem("finished")
        gram_done = ph.sem("gram_done")
        bn_step, root_step = ph.sem("bn_step"), ph.sem("root_step")
        rows_ps = ph.sem("rows_ps")
        with nc.Block() as block:
            @block.sync
            def _(sp):
                free = {"y": [(turned, 2)], "sums": [(sums_done, 1)]}
                if first:
                    free["y"].append((res_done, 1))
                else:
                    free["x0"] = [(res_done, 1)]
                free["sums"] = [(added, 2)]
                ph.load_program(sp, free)

            @block.gpsimd
            def _(pool):
                for b in range(2):
                    pool.memset(y1[b][:, :, D:D + 1], 1.0).then_inc(ones_set, 1)

                def step(c, b, q):
                    n = sh.rows(c)
                    if used_before(c, 2):
                        pool.wait_ge(finished, 2 * (c - 1))
                        pool.sem_inc(rows_ps, 1)
                    ph.have(pool, res, b, q)
                    pool.tensor_tensor(res_b[b][0:n, :, :], ph.buf[res][b][0:n, :, :], spread_slots(bias[0:n, :], [n, T, D]),
                                       ALU.add).then_inc(res_done, 1)
                    ph.have(pool, "sums", b, q)
                    pool.tensor_tensor(ph.buf["sums"][b][0:n, :, :], ph.buf["sums"][b][0:n, :, :],
                                       spread_features(k["dinv"][0:n, bass.ds(c * T, T)], [n, T, D]), ALU.mult).then_inc(sums_done, 1)

                ph.node_sweep(pool, step)

            @block.tensor
            def _(pe):
                pe.matmul(gram[:, 0:D + 1], k["zeros"][:, 0:P], k["zeros"][:, 0:D + 1], start=True, stop=False,
                          skip_group_check=True)

                def add_gram(c, b):
                    n = sh.rows(c)
                    pe.wait_ge(ph.out_ready, c + 1)
                    for t in range(T):
                        mm = pe.matmul(gram[:, 0:D + 1], y1[b][0:n, t, 0:D], y1[b][0:n, t, :], start=False, stop=False,
                                       skip_group_check=True)
                    mm.then_inc(gram_done, 1)

                def step(c, b, q):
                    own_product(ph, pe, k, "y", weight, turn_ps, out_ps, turned, in_sb, own_done, multiplied, hT, c, b, q,
                                between=(lambda: add_gram(c - 1, 1 - b)) if used_before(c, 1) else None)

                pe.wait_ge(ones_set, 2)
                ph.node_sweep(pe, step)
                last_c = sh.node_chunks - 1
                add_gram(last_c, last_c % 2)
                if last:
                    pe.wait_ge(bn_step, 12)
                    for i in range(2):
                        pe.matmul(turn_ps[0][:, i * D:(i + 1) * D], as_rows[2][:, i, :], k["ident"][:, :], start=True,
                                  stop=True).then_inc(gram_done, 1)

            @block.scalar
            def _(act):
                def step(c, b, q):
                    n = sh.rows(c)
                    turned_to_sbuf(act, ph, turn_ps, turned, multiplied, in_sb, hT, c, b, scale_shift)
                    if used_before(c, 1):
                        ph.store(act, y1, c - 1, 1 - b)
                    if last:
                        return
                    for h in range(2):
                        act.wait_ge(finished, 2 * c + h + 1)
                        ph.out_free(act, c, b, q)
                        if used_before(c, 2):
                            act.wait_ge(gram_done, c - 1)
                        t = slice(H * h, H * h + H)
                        ins = act.activation(y1[b][0:n, t, 0:D], acc[b][0:n, t, :], ACT.Relu)
                    ins.then_inc(ph.out_ready, 1)

                ph.node_sweep(act, step)
                last_c = sh.node_chunks - 1
                ph.store(act, y1, last_c, last_c % 2)
                ph.all_stored(act)

            @block.vector
            def _(dve):
                def step(c, b, q):
                    n = sh.rows(c)
                    for h in range(2):
                        t = slice(H * h, H * h + H)
                        dve.wait_ge(multiplied, 2 * c + h + 1)
                        if used_before(c, 2):
                            if last:
                                dve.wait_ge(finished, 2 * c + h - 3)
                            else:
                                dve.wait_ge(ph.out_ready, c - 1)
                        dve.tensor_tensor(acc[b][0:n, t, :], out_ps[b][h][0:n, :].rearrange("p (t f) -> p t f", f=D),
                                          spread_features(k["dinv2"][0:n, bass.ds(c * T + h * H, H)], [n, H, D]),
                                          ALU.mult).then_inc(own_done, 1)
                    dve.wait_ge(sums_done, c + 1)
                    for h in range(2):
                        t = slice(H * h, H * h + H)
                        dve.wait_ge(own_done, 2 * c + h + 1)
                        dve.tensor_tensor(acc[b][0:n, t, :], acc[b][0:n, t, :], ph.buf["sums"][b][0:n, t, :],
                                          ALU.add).then_inc(added, 1)
                    dve.wait_ge(res_done, c + 1)
                    if last:
                        ph.out_free(dve, c, b, q)
                        if used_before(c, 2):
                            dve.wait_ge(gram_done, c - 1)
                    for h in range(2):
                        t = slice(H * h, H * h + H)
                        dve.wait_ge(added, 2 * c + h + 1)
                        out = y1[b][0:n, t, 0:D] if last else acc[b][0:n, t, :]
                        ins = dve.tensor_tensor(out, acc[b][0:n, t, :], res_b[b][0:n, t, :], ALU.add)
                        ins.then_inc(finished, 1)
                    if last:
                        dve.wait_ge(finished, 2 * c + 2)
                        dve.sem_inc(ph.out_ready, 1)

                ph.node_sweep(dve, step)
                gamma, beta = k[f"gamma{no}"], k[f"beta{no}"]
                mean, sq, var, m2, root = (small[:, i:i + 1] for i in range(5))
                ss = next_scale_shift
                dve.wait_ge(gram_done, sh.node_chunks)
                dve.tensor_tensor(diag[:, :], gram[:, 0:D], k["ident"][:, :], ALU.mult).then_inc(bn_step, 1)
                dve.tensor_scalar(mean, gram[:, D:D + 1], 1.0 / sh.n, None, ALU.mult).then_inc(bn_step, 1)
                dve.wait_ge(bn_step, 2)
                dve.tensor_reduce(sq, diag[:, :], AX.X, ALU.add).then_inc(bn_step, 1)
                dve.tensor_tensor(m2, mean, mean, ALU.mult).then_inc(bn_step, 1)
                dve.wait_ge(bn_step, 4)
                dve.scalar_tensor_tensor(out=var, in0=sq, scalar=1.0 / sh.n, in1=m2, op0=ALU.mult, op1=ALU.subtract).then_inc(bn_step, 1)
                dve.wait_ge(bn_step, 5)
                dve.tensor_scalar(var, var, 0.0, BN_EPS, ALU.max, ALU.add).then_inc(bn_step, 1)
                dve.wait_ge(bn_step, 6)
                rsqrt(dve, root, var, sq, root_step, 0)
                dve.tensor_tensor(ss[:, 0:1], root, gamma[:, :], ALU.mult).then_inc(bn_step, 1)
                dve.wait_ge(bn_step, 7)
                dve.tensor_tensor(m2, mean, ss[:, 0:1], ALU.mult).then_inc(bn_step, 1)
                dve.wait_ge(bn_step, 8)
                dve.tensor_tensor(ss[:, 1:2], beta[:, :], m2, ALU.subtract).then_inc(bn_step, 1)
                dve.wait_ge(bn_step, 9)
                if last:
                    for i in range(2):
                        dve.tensor_scalar(as_rows[2][:, i, :], k["ones"][:, :], ss[:, i:i + 1], None, ALU.mult).then_inc(bn_step, 1)
                    dve.wait_ge(bn_step, 11)
                    dve.sem_inc(bn_step, 1)
                    dve.wait_ge(gram_done, sh.node_chunks + 2)
                    for i in range(2):
                        dve.tensor_copy(as_rows[i][:, :], turn_ps[0][:, i * D:(i + 1) * D]).then_inc(bn_step, 1)
                    dve.wait_ge(bn_step, 14)


def norm_nodes(nc, k, dram, sh, name, table, x0, out, scale_row, shift_row):
    with NodePhase(nc, name, sh, {"y": table, "x0": x0}, out) as ph:
        z = [ph.sb(f"z{b}", [P, T, D]) for b in range(2)]
        o = [ph.sb(f"o{b}", [P, T, D]) for b in range(2)]
        ln = LayerNorm(ph, "ln")
        shifted, scaled, z_done = ph.sem("shifted"), ph.sem("scaled"), ph.sem("z_done")
        with nc.Block() as block:
            @block.sync
            def _(sp):
                ph.load_program(sp, {"y": [(scaled, 1)], "x0": [(z_done, 1)]})

            @block.gpsimd
            def _(pool):
                def step(c, b, q):
                    n = sh.rows(c)
                    x = ph.buf["x0"][b][0:n, :, :]
                    ph.have(pool, "x0", b, q)
                    pool.tensor_tensor(x, x, spread_slots(shift_row[0:n, :], [n, T, D]), ALU.add).then_inc(shifted, 1)

                ph.node_sweep(pool, step)

            @block.vector
            def _(dve):
                def step(c, b, q):
                    n = sh.rows(c)
                    ph.have(dve, "y", b, q)
                    if used_before(c, 2):
                        dve.wait_ge(ph.out_ready, c - 1)
                    dve.tensor_tensor(z[b][0:n, :, :], ph.buf["y"][b][0:n, :, :], spread_slots(scale_row[0:n, :], [n, T, D]),
                                      ALU.mult).then_inc(scaled, 1)
                    dve.wait_ge(scaled, c + 1)
                    dve.wait_ge(shifted, c + 1)
                    dve.tensor_tensor(z[b][0:n, :, :], z[b][0:n, :, :], ph.buf["x0"][b][0:n, :, :], ALU.add).then_inc(z_done, 1)
                    dve.wait_ge(z_done, c + 1)
                    ln.on_vector(dve, z[b], n, c, b)

                ph.node_sweep(dve, step)

            @block.scalar
            def _(act):
                def step(c, b, q):
                    n = sh.rows(c)
                    ph.out_free(act, c, b, q)
                    ln.apply(act, o[b], z[b], n, c, b, ph.out_ready)
                    ph.store(act, o, c, b)

                ph.node_sweep(act, step)
                ph.all_stored(act)


def linear_nodes(nc, k, dram, sh, name, table, weight, bias, out, finish, x0=None):
    streams = {"y": table, "sums": dram["node_sums"]}
    if x0 is not None:
        streams["x0"] = x0
    with NodePhase(nc, name, sh, streams, out) as ph:
        hT = [ph.sb(f"hT{b}", [P, CH]) for b in range(2)]
        z = [ph.sb(f"z{b}", [P, T, D]) for b in range(2)]
        o = [ph.sb(f"o{b}", [P, T, D]) for b in range(2)]
        turn_ps = [ph.ps(f"turn{h}", [P, HALF]) for h in range(2)]
        out_ps = [[ph.ps(f"out{b}{h}", [P, HALF]) for h in range(2)] for b in range(2)]
        turned, in_sb, multiplied = ph.sem("turned"), ph.sem("in_sb"), ph.sem("multiplied")
        biased, summed = ph.sem("biased"), ph.sem("summed")
        gated = ph.sem("gated")
        residual = ph.sem("residual")
        ln = LayerNorm(ph, "ln") if finish == "norm" else None
        with nc.Block() as block:
            @block.sync
            def _(sp):
                free = {"y": [(turned, 2)], "sums": [(summed, 2)]}
                if x0 is not None:
                    free["x0"] = [(residual, 1)]
                ph.load_program(sp, free)

            @block.gpsimd
            def _(pool):
                def step(c, b, q):
                    n = sh.rows(c)
                    g = ph.buf["sums"][b][0:n, :, :]
                    ph.have(pool, "sums", b, q)
                    pool.tensor_tensor(g, g, spread_slots(bias[0:n, :], [n, T, D]), ALU.add).then_inc(biased, 1)
                    if x0 is not None:
                        pool.wait_ge(biased, 2 * c + 1)
                        ph.have(pool, "x0", b, q)
                        pool.tensor_tensor(g, g, ph.buf["x0"][b][0:n, :, :], ALU.add).then_inc(biased, 1)
                        pool.wait_ge(biased, 2 * c + 2)
                        pool.sem_inc(residual, 1)

                ph.node_sweep(pool, step)

            @block.tensor
            def _(pe):
                def step(c, b, q):
                    own_product(ph, pe, k, "y", weight, turn_ps, out_ps, turned, in_sb, summed, multiplied, hT, c, b, q)

                ph.node_sweep(pe, step)

            @block.vector
            def _(dve):
                per = 1 if x0 is None else 2

                def step(c, b, q):
                    n = sh.rows(c)
                    dve.wait_ge(biased, per * c + per)
                    for h in range(2):
                        t = slice(H * h, H * h + H)
                        dve.wait_ge(multiplied, 2 * c + h + 1)
                        if used_before(c, 2) and h == 0:
                            dve.wait_ge(ph.out_ready, c - 1)
                        dve.tensor_tensor(z[b][0:n, t, :], out_ps[b][h][0:n, :].rearrange("p (t f) -> p t f", f=D),
                                          ph.buf["sums"][b][0:n, t, :], ALU.add).then_inc(summed, 1)
                    if finish == "norm":
                        dve.wait_ge(summed, 2 * c + 2)
                        ln.on_vector(dve, z[b], n, c, b)
                    if finish == "swish":
                        dve.wait_ge(gated, c + 1)
                        dve.tensor_tensor(o[b][0:n, :, :], o[b][0:n, :, :], z[b][0:n, :, :], ALU.mult).then_inc(ph.out_ready, 1)

                ph.node_sweep(dve, step)

            @block.scalar
            def _(act):
                def step(c, b, q):
                    n = sh.rows(c)
                    turned_to_sbuf(act, ph, turn_ps, turned, multiplied, in_sb, hT, c, b)
                    if used_before(c, 1):
                        ph.store(act, o, c - 1, 1 - b)
                    ph.out_free(act, c, b, q)
                    if finish == "norm":
                        ln.apply(act, o[b], z[b], n, c, b, ph.out_ready)
                    else:
                        act.wait_ge(summed, 2 * c + 2)
                        f, done = (ACT.Relu, ph.out_ready) if finish == "relu" else (ACT.Sigmoid, gated)
                        act.activation(o[b][0:n, :, :], z[b][0:n, :, :], f).then_inc(done, 1)

                ph.node_sweep(act, step)
                last_c = sh.node_chunks - 1
                ph.store(act, o, last_c, last_c % 2)
                ph.all_stored(act)


def gat_nodes(nc, k, dram, sh, name, table, out):
    with NodePhase(nc, name, sh, {"sums": dram["node_sums"], "x": table}, out) as ph:
        act_out = [ph.sb(f"gelu{b}", [P, T, D]) for b in range(2)]
        x_beta = [ph.sb(f"x_beta{b}", [P, T, D]) for b in range(2)]
        z1 = [ph.sb(f"z1{b}", [P, T, D]) for b in range(2)]
        z2 = [ph.sb(f"z2{b}", [P, T, D]) for b in range(2)]
        o = [ph.sb(f"o{b}", [P, T, D]) for b in range(2)]
        ln1, ln2 = LayerNorm(ph, "ln1"), LayerNorm(ph, "ln2")
        biased, beta_added, gelu_done = ph.sem("biased"), ph.sem("beta_added"), ph.sem("gelu_done")
        z1_done, normed, scaled, z2_done = ph.sem("z1_done"), ph.sem("normed"), ph.sem("scaled"), ph.sem("z2_done")
        gate = ph.sem("gate")
        with nc.Block() as block:
            @block.sync
            def _(sp):
                ph.load_program(sp, {"sums": [(gelu_done, 1)], "x": [(z1_done, 1), (beta_added, 1)]})

            @block.gpsimd
            def _(pool):
                def scale(c, b):
                    n = sh.rows(c)
                    z = z2[b][0:n, :, :]
                    pool.wait_ge(normed, c + 1)
                    pool.tensor_tensor(z, z, spread_slots(k["gat_gamma"][0:n, :], [n, T, D]), ALU.mult).then_inc(scaled, 1)

                def step(c, b, q):
                    n = sh.rows(c)
                    g = ph.buf["sums"][b][0:n, :, :]
                    ph.have(pool, "sums", b, q)
                    pool.tensor_tensor(g, g, spread_slots(k["gat_b"][0:n, :], [n, T, D]), ALU.add).then_inc(biased, 1)
                    ph.have(pool, "x", b, q)
                    if used_before(c, 2):
                        pool.wait_ge(z2_done, c - 1)
                    pool.tensor_tensor(x_beta[b][0:n, :, :], ph.buf["x"][b][0:n, :, :],
                                       spread_slots(k["gat_beta"][0:n, :], [n, T, D]), ALU.add).then_inc(beta_added, 1)
                    if used_before(c, 1):
                        scale(c - 1, 1 - b)

                ph.node_sweep(pool, step)
                last_c = sh.node_chunks - 1
                scale(last_c, last_c % 2)

            @block.scalar
            def _(act):
                def second(c, b, q):
                    n = sh.rows(c)
                    ph.out_free(act, c, b, q)
                    ln2.apply(act, o[b], z2[b], n, c, b, ph.out_ready)
                    ph.store(act, o, c, b)

                def step(c, b, q):
                    n = sh.rows(c)
                    act.wait_ge(biased, c + 1)
                    if used_before(c, 2):
                        act.wait_ge(z1_done, c - 1)
                    act.activation(act_out[b][0:n, :, :], ph.buf["sums"][b][0:n, :, :], ACT.Gelu).then_inc(gelu_done, 1)
                    if used_before(c, 1):
                        second(c - 1, 1 - b, q if b else q - 1)
                    ln1.apply(act, z2[b], z1[b], n, c, b, normed)

                ph.node_sweep(act, step)
                last_c = sh.node_chunks - 1
                second(last_c, last_c % 2, last_c // 2)
                ph.all_stored(act)

            @block.vector
            def _(dve):
                def second(c, b):
                    n = sh.rows(c)
                    dve.wait_ge(scaled, c + 1)
                    dve.tensor_tensor(z2[b][0:n, :, :], z2[b][0:n, :, :], x_beta[b][0:n, :, :], ALU.add).then_inc(z2_done, 1)
                    dve.wait_ge(z2_done, c + 1)
                    ln2.on_vector(dve, z2[b], n, c, b)

                def step(c, b, q):
                    n = sh.rows(c)
                    dve.wait_ge(gelu_done, c + 1)
                    ph.have(dve, "x", b, q)
                    if used_before(c, 2):
                        dve.wait_ge(normed, c - 1)
                    dve.tensor_tensor(z1[b][0:n, :, :], act_out[b][0:n, :, :], ph.buf["x"][b][0:n, :, :], ALU.add).then_inc(z1_done, 1)
                    dve.wait_ge(z1_done, c + 1)
                    ln1.on_vector(dve, z1[b], n, c, b)
                    if used_before(c, 1):
                        second(c - 1, 1 - b)

                ph.node_sweep(dve, step)
                last_c = sh.node_chunks - 1
                second(last_c, last_c % 2)



def build(nc, a, out):
    sh = Shapes(a["x"].shape[0], a["src"].shape[0])
    nodes_padded = sh.node_chunks * CH

    def scratch(name, shape, dt=F32):
        return nc.dram_tensor(name, shape, dt, kind="Internal")

    dram = {"node_sums": scratch("node_sums", [nodes_padded, D]).ap(),
            "degree": scratch("degree", [nodes_padded, 1]).ap(),
            "dinv": scratch("dinv", [nodes_padded, 1]).ap(),
            "dst_padded": scratch("dst_padded", [sh.edges_padded + 1], I32).ap(),
            "run_sums": scratch("run_sums", [2, sh.edges_padded]).ap(),
            "edge_w": scratch("edge_w", [sh.edges_padded]).ap()}
    rows_a, rows_b, rows_c = (scratch(f"node_rows_{i}", [sh.n, D]).ap() for i in "abc")

    with ExitStack() as ctx:
        k = {}

        def keep(name, shape, dt=F32):
            k[name] = ctx.enter_context(nc.sbuf_tensor(f"k_{name}", shape, dt))

        for n in ("pool1", "self1", "eve1", "pool2", "self2", "eve2", "sage_l1", "sage_r1", "sage_l2", "sage_r2",
                  "gcn0", "gcn1", "gcn2", "gat_l", "gat_r", "gat_e", "ident", "ones", "head_att",
                  "gcn_b0", "gcn_b1", "gcn_b2", "eve_b1", "eve_b2", "eve_c1", "eve_c2", "sage_b1", "sage_b2",
                  "gat_b", "gat_gamma", "gat_beta", "bn_scale_row", "bn_shift_row"):
            keep(n, [P, D])
        keep("zeros", [P, D + 1])
        keep("bn_cols", [P, 2, D])
        for n in ("gamma0", "gamma1", "gamma2", "beta0", "beta1", "beta2", "bpool1", "bpool2", "bl", "br", "blr", "att",
                  "bconv1", "bconv2"):
            keep(n, [P, 1])
        for n in ("wconv1", "wconv2", "bn1", "bn2", "bn3"):
            keep(n, [P, 2])
        keep("first_dst", [1, 1], I32)
        for n in ("src_idx", "place_idx", "dst_idx"):
            keep(n, [P, sh.edge_tiles], I32)
        for n in ("ew_tab", "inv_count"):
            keep(n, [P, sh.edge_tiles])
        for n in ("dinv", "dinv2"):
            keep(n, [P, sh.node_chunks * T])
        keep("same_run", [P, sh.edges_padded], U8)

        load_constants(nc, a, k)
        index_tables(nc, a, k, dram, sh)
        run_masks(nc, a, k, dram, sh)
        degrees(nc, k, dram, sh)

        x = a["x"]
        gcn_edges(nc, k, dram, sh, "e0", x, k["gcn0"], None)
        gcn_nodes(nc, k, dram, sh, "n0", 0, x, x, rows_a, None, k["bn1"])
        gcn_edges(nc, k, dram, sh, "e1", rows_a, k["gcn1"], k["bn1"])
        gcn_nodes(nc, k, dram, sh, "n1", 1, rows_a, x, rows_b, k["bn1"], k["bn2"])
        gcn_edges(nc, k, dram, sh, "e2", rows_b, k["gcn2"], k["bn2"])
        gcn_nodes(nc, k, dram, sh, "n2", 2, rows_b, x, rows_a, k["bn2"], k["bn3"],
                  as_rows=(k["bn_scale_row"], k["bn_shift_row"], k["bn_cols"]))
        norm_nodes(nc, k, dram, sh, "n3", rows_a, x, rows_b, k["bn_scale_row"], k["bn_shift_row"])
        eve_edges(nc, k, dram, sh, "e4", rows_b, 1)
        linear_nodes(nc, k, dram, sh, "n4", rows_b, k["self1"], k["eve_b1"], rows_a, "relu")
        eve_edges(nc, k, dram, sh, "e5", rows_a, 2)
        linear_nodes(nc, k, dram, sh, "n5", rows_a, k["self2"], k["eve_b2"], rows_c, "norm", x0=rows_b)
        sage_edges(nc, k, dram, sh, "e6", rows_c, k["sage_l1"])
        linear_nodes(nc, k, dram, sh, "n6", rows_c, k["sage_r1"], k["sage_b1"], rows_a, "swish")
        sage_edges(nc, k, dram, sh, "e7", rows_a, k["sage_l2"])
        linear_nodes(nc, k, dram, sh, "n7", rows_a, k["sage_r2"], k["sage_b2"], rows_b, "norm", x0=rows_c)
        gat_edges(nc, a, k, dram, sh, "e8", rows_b)
        gat_nodes(nc, k, dram, sh, "n8", rows_b, out)


def kernel(**inputs):
    import numpy as _np
    import concourse.bacc as _bacc
    from concourse import mybir as _mybir
    from concourse.bass_utils import run_bass_kernel_spmd as _run

    nc = _bacc.Bacc("TRN2", target_bir_lowering=False, num_devices=1)
    arrays, args = {}, {}
    for name, value in inputs.items():
        v = _np.ascontiguousarray(value)
        arrays[f"in_{name}_dram"] = v
        args[name] = nc.dram_tensor(f"in_{name}_dram", v.shape, _mybir.dt.from_np(v.dtype), kind="ExternalInput").ap()
    out = nc.dram_tensor("out_0_dram", args["x"].shape, _mybir.dt.float32, kind="ExternalOutput").ap()
    build(nc, args, out)
    r = _run(nc, [arrays], core_ids=[0])
    return r.results[0]["out_0_dram"]
```

```python
from contextlib import ExitStack

import concourse.bass as bass
from concourse import mybir

F32 = mybir.dt.float32
I32 = mybir.dt.int32
U8 = mybir.dt.uint8
ALU = mybir.AluOpType
ACT = mybir.ActivationFunctionType
AX = mybir.AxisListType

P = 128
D = 128
T = 8
H = 4
CH = P * T
HALF = CH // 2
BN_EPS = 1e-5
LN_EPS = 1e-5
BIG = 3.0e38
FAR = 1 << 20


class Shapes:

    def __init__(self, n_nodes, n_edges):
        self.n, self.e = n_nodes, n_edges
        self.node_chunks = -(-n_nodes // CH)
        self.edge_chunks = -(-n_edges // CH)
        self.edge_tiles = self.edge_chunks * T
        self.edges_padded = self.edge_chunks * CH
        self.node_pairs, self.edge_pairs = self.node_chunks // 2, self.edge_chunks // 2
        assert self.node_chunks % 2 == 0 and self.edge_chunks % 2 == 1 and self.edge_pairs > 2
        self.last_nodes = n_nodes - (self.node_chunks - 1) * CH
        assert self.last_nodes % T == 0 and n_nodes < FAR
        self.last_rows = self.last_nodes // T

    def rows(self, c):
        return self.last_rows if isinstance(c, int) and c == self.node_chunks - 1 else P


def used_before(c, lag):
    return not isinstance(c, int) or c >= lag


def sweep(eng, chunks, full, step):
    step(0, 0, 0)
    step(1, 1, 0)
    with eng.Fori(1, full // 2) as q:
        step(2 * q, 0, q)
        step(2 * q + 1, 1, q)
    for c in range(full // 2 * 2, chunks):
        step(c, c % 2, c // 2)


def node_rows(t, c, sh):
    if isinstance(c, int):
        part = t[c * CH:c * CH + sh.rows(c) * T, :]
    else:
        part = t[bass.ds(c * CH, CH), :]
    return part.rearrange("(p j) f -> p j f", j=T)


class Phase:

    def __init__(self, nc, name):
        self.nc, self.name, self.stack, self.sems = nc, name, ExitStack(), []

    def __enter__(self):
        self.stack.__enter__()
        return self

    def __exit__(self, *a):
        self.nc.clear_and_free_semaphores(self.sems)
        self.nc.all_engine_barrier()
        return self.stack.__exit__(*a)

    def sb(self, name, shape, dt=F32):
        return self.stack.enter_context(self.nc.sbuf_tensor(f"{self.name}_{name}", shape, dt))

    def ps(self, name, shape):
        return self.stack.enter_context(self.nc.psum_tensor(f"{self.name}_{name}", shape, F32))

    def sem(self, name):
        s = self.nc.alloc_semaphore(f"{self.name}_{name}")
        self.sems.append(s)
        return s

    def pair(self, name):
        return [self.sem(f"{name}{b}") for b in range(2)]


def spread_slots(ap, shape):
    return ap.unsqueeze(1).to_broadcast(shape)


def spread_features(ap, shape):
    return ap.unsqueeze(2).to_broadcast(shape)


RSQRT_GUESS = 0x5F3759DF
RSQRT_STEPS = 11


def rsqrt(dve, y, x, tmp, step, base):
    yi = y.bitcast(I32)
    dve.tensor_scalar(yi, x.bitcast(I32), 1, None, ALU.logical_shift_right).then_inc(step, 1)
    dve.wait_ge(step, base + 1)
    dve.tensor_scalar(yi, yi, -1.0, float(RSQRT_GUESS), ALU.mult, ALU.add).then_inc(step, 1)
    for i in range(3):
        dve.wait_ge(step, base + 2 + 3 * i)
        dve.tensor_tensor(tmp, y, y, ALU.mult).then_inc(step, 1)
        dve.wait_ge(step, base + 3 + 3 * i)
        dve.scalar_tensor_tensor(out=tmp, in0=tmp, scalar=-0.5, in1=x, op0=ALU.mult, op1=ALU.mult).then_inc(step, 1)
        dve.wait_ge(step, base + 4 + 3 * i)
        dve.scalar_tensor_tensor(out=y, in0=tmp, scalar=1.5, in1=y, op0=ALU.add, op1=ALU.mult).then_inc(step, 1)
    dve.wait_ge(step, base + RSQRT_STEPS)



def load_constants(nc, a, k):
    turned = {"pool1": a["L1_gnn_wpool1"], "self1": a["L1_gnn_wself1"], "eve1": a["L1_gnn_weve1"],
              "pool2": a["L1_gnn_wpool2"], "self2": a["L1_gnn_wself2"], "eve2": a["L1_gnn_weve2"],
              "sage_l1": a["L2_gnn_W1_l"], "sage_r1": a["L2_gnn_W1_r"],
              "sage_l2": a["L2_gnn_W2_l"], "sage_r2": a["L2_gnn_W2_r"]}
    plain = {"gcn0": a["L0_gnn_Ws"][0], "gcn1": a["L0_gnn_Ws"][1], "gcn2": a["L0_gnn_Ws"][2],
             "gat_l": a["L3_gnn_Wl"], "gat_r": a["L3_gnn_Wr"], "gat_e": a["L3_gnn_We"]}
    columns = {"gamma0": a["L0_gnn_gammas"][0], "gamma1": a["L0_gnn_gammas"][1], "gamma2": a["L0_gnn_gammas"][2],
               "beta0": a["L0_gnn_betas"][0], "beta1": a["L0_gnn_betas"][1], "beta2": a["L0_gnn_betas"][2],
               "bpool1": a["L1_gnn_bpool1"], "bpool2": a["L1_gnn_bpool2"],
               "bl": a["L3_gnn_bl"], "br": a["L3_gnn_br"],
               "att": a["L3_gnn_att"].rearrange("h c -> (h c)")}
    rows = {"gcn_b0": a["L0_gnn_bs"][0], "gcn_b1": a["L0_gnn_bs"][1], "gcn_b2": a["L0_gnn_bs"][2],
            "eve_b1": a["L1_gnn_bias1"], "eve_b2": a["L1_gnn_bias2"],
            "sage_b1": a["L2_gnn_b1"], "sage_b2": a["L2_gnn_b2"],
            "gat_b": a["L3_gnn_bias"], "gat_gamma": a["L3_gnn_gamma"], "gat_beta": a["L3_gnn_beta"]}
    heads, width = a["L3_gnn_att"].shape
    with Phase(nc, "const") as ph:
        raw = {n: ph.sb(f"raw_{n}", [P, D]) for n in turned}
        relu_b = ph.sb("relu_b", [P, 2])
        relu_bm = ph.sb("relu_bm", [P, 2, P])
        att_cols = ph.sb("att_cols", [P, D])
        psum = [ph.ps(f"turn{i}", [P, 512]) for i in range(2)]
        eve_ps = ph.ps("eve", [P, 512])
        loaded = ph.sem("loaded")
        cleared = ph.sem("cleared")
        ident_made = ph.sem("ident_made")
        turned_ps = ph.sem("turned_ps")
        turned_sb = ph.sem("turned_sb")
        relu_done = ph.sem("relu_done")
        eve_const = ph.sem("eve_const")
        misc = ph.sem("misc")
        loads = [(raw[n][:, :], w) for n, w in turned.items()]
        loads += [(k[n][0:w.shape[0], :], w) for n, w in plain.items()]
        loads += [(k[n][:, 0:1], w.rearrange("(f o) -> f o", o=1)) for n, w in columns.items()]
        loads += [(k[n][:, :], w.partition_broadcast(P)) for n, w in rows.items()]
        for i in (1, 2):
            loads += [(k[f"wconv{i}"][:, :], a[f"L1_gnn_wconv{i}"].partition_broadcast(P)),
                      (k[f"bconv{i}"][:, :], a[f"L1_gnn_bconv{i}"].partition_broadcast(P))]
        with nc.Block() as block:
            @block.sync
            def _(sp):
                for out, src in loads:
                    sp.dma_start(out, src).then_inc(loaded, 16)

            @block.gpsimd
            def _(pool):
                pool.memset(k["ident"][:, :], 0.0).then_inc(cleared, 1)
                pool.memset(k["head_att"][:, :], 0.0).then_inc(cleared, 1)
                pool.memset(k["ones"][:, :], 1.0).then_inc(cleared, 1)
                pool.memset(k["zeros"][:, :], 0.0).then_inc(cleared, 1)
                pool.wait_ge(cleared, 4)
                pool.affine_select(out=k["ident"][:, :], in_=k["ident"][:, :], compare_op=ALU.not_equal,
                                   fill=1.0, base=0, pattern=[[-1, P]], channel_multiplier=1).then_inc(ident_made, 1)

            @block.tensor
            def _(pe):
                pe.wait_ge(loaded, 16 * len(loads))
                pe.wait_ge(ident_made, 1)
                for i, n in enumerate(turned):
                    if i >= 2:
                        pe.wait_ge(turned_sb, i - 1)
                    pe.transpose(psum[i % 2][:, 0:D], raw[n][:, :], k["ident"][:, :]).then_inc(turned_ps, 1)
                pe.wait_ge(relu_done, 2)
                pe.wait_ge(turned_sb, len(turned))
                for i in (1, 2):
                    pe.matmul(eve_ps[:, (i - 1) * D:i * D], relu_bm[:, i - 1, :], k[f"eve{i}"][:, :],
                              start=True, stop=True).then_inc(eve_const, 1)

            @block.vector
            def _(dve):
                for i, n in enumerate(turned):
                    dve.wait_ge(turned_ps, i + 1)
                    dve.tensor_copy(k[n][:, :], psum[i % 2][:, 0:D]).then_inc(turned_sb, 1)
                for i in (1, 2):
                    dve.tensor_scalar(relu_b[:, i - 1:i], k[f"bconv{i}"][:, :], 0.0, None, ALU.max).then_inc(misc, 1)
                dve.wait_ge(misc, 2)
                for i in (1, 2):
                    dve.tensor_scalar(relu_bm[:, i - 1, :], k["ones"][:, :], relu_b[:, i - 1:i], None,
                                      ALU.mult).then_inc(relu_done, 1)
                dve.wait_ge(eve_const, 2)
                for i in (1, 2):
                    dve.tensor_copy(k[f"eve_c{i}"][:, :], eve_ps[:, (i - 1) * D:i * D]).then_inc(misc, 1)
                dve.wait_ge(misc, 4)
                for i in (1, 2):
                    dve.tensor_tensor(k[f"eve_b{i}"][:, :], k[f"eve_b{i}"][:, :], k[f"eve_c{i}"][:, :],
                                      ALU.add).then_inc(misc, 1)
                dve.tensor_tensor(k["blr"][:, :], k["bl"][:, :], k["br"][:, :], ALU.add).then_inc(misc, 1)
                dve.tensor_scalar(att_cols[:, :], k["ones"][:, :], k["att"][:, 0:1], None, ALU.mult).then_inc(misc, 1)
                dve.wait_ge(misc, 8)
                for h in range(heads):
                    s = slice(h * width, (h + 1) * width)
                    dve.tensor_copy(k["head_att"][s, s], att_cols[s, s]).then_inc(misc, 1)
                dve.wait_ge(misc, 8 + heads)


def edge_rows_load(eng, out, src, count, sem):
    groups = count // (P * P)
    whole = count // P
    eng.dma_start(out[:, 0:groups, :], src[0:groups * P * P].rearrange("(g t e) -> t g e", t=P, e=P)).then_inc(sem, 16)
    n = 16
    left = whole - groups * P
    if left:
        eng.dma_start(out[0:left, groups, :], src[groups * P * P:whole * P].rearrange("(t e) -> t e", e=P)).then_inc(sem, 16)
        n += 16
    rest = count - whole * P
    if rest:
        eng.dma_start(out[left:left + 1, groups, 0:rest], src[whole * P:count].rearrange("(t e) -> t e", t=1)).then_inc(sem, 16)
        n += 16
    return n


def index_tables(nc, a, k, dram, sh):
    groups = -(-sh.edge_tiles // P)
    tail = sh.edge_tiles - (groups - 1) * P
    with Phase(nc, "index") as ph:
        ints = {n: ph.sb(f"int_{n}", [P, groups, P], I32) for n in ("src", "dst", "next")}
        flts = {n: ph.sb(f"flt_{n}", [P, groups, P]) for n in ("src", "dst", "next", "ew", "place")}
        same = ph.sb("same", [P, groups, P])
        zero = ph.sb("zero", [P, T, D])
        edge_pad = ph.sb("edge_pad", [1, CH], I32)
        bank = [ph.ps(f"bank{i}", [P, 512]) for i in range(4)]
        filled = ph.sem("filled")
        loaded = ph.sem("loaded")
        zeroed = ph.sem("zeroed")
        padded = ph.sem("padded")
        calc = ph.sem("calc")
        in_psum = ph.sem("in_psum")
        out_sb = ph.sem("out_sb")
        n_loaded = []
        with nc.Block() as block:
            @block.gpsimd
            def _(pool):
                pool.memset(ints["src"][:, :, :], 0).then_inc(filled, 1)
                pool.memset(ints["dst"][:, :, :], FAR).then_inc(filled, 1)
                pool.memset(ints["next"][:, :, :], 2 * FAR).then_inc(filled, 1)
                pool.memset(flts["ew"][:, :, :], 0.0).then_inc(filled, 1)
                pool.memset(edge_pad[:, :], FAR).then_inc(filled, 1)
                pool.memset(k["first_dst"][:, :], -1).then_inc(filled, 1)
                pool.memset(zero[:, :, :], 0.0).then_inc(filled, 1)
                pool.memset(k["ready"][:, :], 0).then_inc(filled, 1)

            @block.sync
            def _(sp):
                sp.wait_ge(filled, 8)
                n = edge_rows_load(sp, ints["src"], a["src"], sh.e, loaded)
                n += edge_rows_load(sp, ints["dst"], a["dst"], sh.e, loaded)
                n += edge_rows_load(sp, ints["next"], a["dst"][1:sh.e], sh.e - 1, loaded)
                n += edge_rows_load(sp, flts["ew"], a["edge_weight"], sh.e, loaded)
                firsts = a["dst"][0:sh.edge_pairs * 2 * CH].rearrange("(o j e) -> o j e", o=1, e=2 * CH)[:, 1:, 0:1]
                sp.dma_start(k["ready"][0:1, 2:sh.edge_pairs + 1].unsqueeze(2), firsts, allow_slow_non_contiguous=True).then_inc(loaded, 16)
                n += 16
                n_loaded.append(n)
                dp = dram["dst_padded"]
                sp.dma_start(dp[0:1], k["first_dst"][0:1, 0:1]).then_inc(padded, 16)
                sp.dma_start(dp[1:sh.e + 1].rearrange("(a b) -> a b", a=16), a["dst"].rearrange("(a b) -> a b", a=16)).then_inc(padded, 16)
                rest = sh.edges_padded - sh.e
                sp.dma_start(dp[sh.e + 1:sh.e + 1 + rest], edge_pad[0:1, 0:rest]).then_inc(padded, 16)
                full = sh.node_chunks
                with sp.Fori(0, full) as c:
                    sp.dma_start(dram["node_sums"][bass.ds(c * CH, CH), :].rearrange("(p j) f -> p j f", j=T),
                                 zero[:, :, :]).then_inc(zeroed, 16)
                sp.dma_start(dram["degree"].rearrange("(p c) o -> p (c o)", p=P),
                             zero[:, :, :].rearrange("p j f -> p (j f)")[:, 0:full * T]).then_inc(zeroed, 16)
                sp.wait_ge(zeroed, 16 * (full + 1))
                sp.wait_ge(padded, 48)

            order = [("src", "src_idx"), ("place", "place_idx"), ("dst", "dst_idx"), ("ew", "ew_tab")]

            @block.vector
            def _(dve):
                dve.wait_ge(loaded, n_loaded[0])
                for n in ("src", "dst", "next"):
                    dve.tensor_copy(flts[n][:, :, :], ints[n][:, :, :]).then_inc(calc, 1)
                dve.wait_ge(calc, 3)
                dve.tensor_tensor(same[:, :, :], flts["dst"][:, :, :], flts["next"][:, :, :], ALU.is_equal).then_inc(calc, 1)
                dve.wait_ge(calc, 4)
                dve.scalar_tensor_tensor(out=flts["place"][:, :, :], in0=same[:, :, :], scalar=float(FAR),
                                         in1=flts["dst"][:, :, :], op0=ALU.mult, op1=ALU.add).then_inc(calc, 1)
                dve.wait_ge(calc, 5)
                dve.tensor_scalar(flts["dst"][:, :, :], flts["dst"][:, :, :], float(sh.n - 1), None, ALU.min).then_inc(calc, 1)
                for i, (n, out) in enumerate(order):
                    dve.wait_ge(in_psum, i + 1)
                    dve.tensor_copy(k[out][:, :], bank[i][:, 0:sh.edge_tiles]).then_inc(out_sb, 1)
                dve.tensor_scalar(k["ready"][:, :], k["ready"][:, :], (2 * CH).bit_length() - 1, None,
                                  ALU.arith_shift_right).then_inc(out_sb, 1)
                dve.wait_ge(out_sb, len(order) + 1)

            @block.tensor
            def _(pe):
                pe.wait_ge(calc, 6)
                for i, (n, _) in enumerate(order):
                    for g in range(groups):
                        rows = P if g < groups - 1 else tail
                        mm = pe.transpose(bank[i][:, g * P:g * P + rows], flts[n][0:rows, g, :], k["ident"][0:rows, 0:rows])
                    mm.then_inc(in_psum, 1)


def run_masks(nc, a, k, dram, sh):
    real = sh.e - (sh.edge_chunks - 1) * CH
    with Phase(nc, "runs") as ph:
        dst_all = [ph.sb(f"dst_all{b}", [P, CH + 1], I32) for b in range(2)]
        pairs = [ph.sb(f"pairs{b}", [2, CH]) for b in range(2)]
        sums = [ph.sb(f"sums{b}", [2, CH]) for b in range(2)]
        dst_in = ph.pair("dst_in")
        ew_in = ph.pair("ew_in")
        ones_set = ph.sem("ones_set")
        masked = ph.sem("masked")
        summed = ph.sem("summed")
        stored = ph.pair("stored")
        with nc.Block() as block:
            @block.gpsimd
            def _(pool):
                for b in range(2):
                    pool.memset(pairs[b][:, :], 1.0).then_inc(ones_set, 1)

            @block.sync
            def _(sp):
                sp.wait_ge(ones_set, 2)

                def step(c, b, q):
                    if used_before(c, 2):
                        sp.wait_ge(masked, c - 1)
                    at = c * CH
                    sp.dma_start(dst_all[b][:, :], dram["dst_padded"][bass.ds(at, CH + 1)].partition_broadcast(P)).then_inc(dst_in[b], 16)
                    if used_before(c, 2):
                        sp.wait_ge(summed, c - 1)
                    n = real if isinstance(c, int) and c == sh.edge_chunks - 1 else CH
                    sp.dma_start(pairs[b][0:1, 0:n], a["edge_weight"][bass.ds(at, n)].partition_broadcast(1)).then_inc(ew_in[b], 16)

                sweep(sp, sh.edge_chunks, sh.edge_chunks - 1, step)

            @block.vector
            def _(dve):
                def step(c, b, q):
                    dve.wait_ge(dst_in[b], 16 * q + 16)
                    dve.tensor_tensor(k["same_run"][:, bass.ds(c * CH, CH)], dst_all[b][:, 1:CH + 1], dst_all[b][:, 0:CH],
                                      ALU.is_equal).then_inc(masked, 1)
                    dve.wait_ge(masked, c + 1)
                    dve.wait_ge(ew_in[b], 16 * q + 16)
                    if used_before(c, 1):
                        dve.wait_ge(summed, c)
                    if used_before(c, 2):
                        dve.wait_ge(stored[b], 16 * q)
                    start = sums[1 - b][:, CH - 1:CH] if used_before(c, 1) else 0.0
                    dve.tensor_tensor_scan(sums[b][:, :], k["same_run"][0:2, bass.ds(c * CH, CH)], pairs[b][:, :],
                                           start, ALU.mult, ALU.add).then_inc(summed, 1)

                sweep(dve, sh.edge_chunks, sh.edge_chunks - 1, step)

            @block.scalar
            def _(act):
                def step(c, b, q):
                    act.wait_ge(summed, c + 1)
                    act.dma_start(dram["run_sums"][:, bass.ds(c * CH, CH)], sums[b][:, :]).then_inc(stored[b], 16)

                sweep(act, sh.edge_chunks, sh.edge_chunks - 1, step)
                act.wait_ge(stored[0], 16 * ((sh.edge_chunks + 1) // 2))
                act.wait_ge(stored[1], 16 * (sh.edge_chunks // 2))


def degrees(nc, k, dram, sh):
    groups = -(-sh.edge_tiles // P)
    tail = sh.edge_tiles - (groups - 1) * P
    rows_of = [P] * (groups - 1) + [tail]
    with Phase(nc, "deg") as ph:
        run = [ph.sb(f"run{i}", [P, groups, P]) for i in range(2)]
        deg_tab = ph.sb("deg_tab", [P, sh.edge_tiles])
        w_tab = ph.sb("w_tab", [P, sh.edge_tiles])
        w_rows = ph.sb("w_rows", [P, groups, P])
        pos = ph.sb("pos", [P, sh.node_chunks * T])
        root = ph.sb("root", [P, sh.node_chunks * T])
        k["dinv"] = ph.sb("dinv", [P, sh.node_chunks * T])
        lifted = ph.sb("lifted", [P, sh.node_chunks * T])
        root_tmp = ph.sb("root_tmp", [P, sh.node_chunks * T])
        root_step = ph.sem("root_step")
        deg_slot = ph.sb("deg_slot", [P, T])
        idx_slot = ph.sb("idx_slot", [P, T], I32)
        got = ph.sb("got", [P, T])
        bank = [ph.ps(f"bank{i}", [P, 512]) for i in range(3)]
        loaded = ph.sem("loaded")
        in_psum = ph.sem("in_psum")
        tabs = ph.sem("tabs")
        slots = ph.sem("slots")
        gate = ph.sem("gate")
        scattered = ph.sem("scattered")
        deg_in = ph.sem("deg_in")
        dinv_calc = ph.sem("dinv_calc")
        dinv_out = ph.sem("dinv_out")
        gathered = ph.sem("gathered")
        weighted = ph.sem("weighted")
        w_in_rows = ph.sem("w_in_rows")
        w_out = ph.sem("w_out")
        loads = []
        with nc.Block() as block:
            @block.sync
            def _(sp):
                n = 0
                for i in range(2):
                    n += edge_rows_load(sp, run[i], dram["run_sums"][i], sh.edges_padded, loaded)
                loads.append(n)
                sp.wait_ge(scattered, 16 * sh.edge_tiles)
                sp.dma_start(k["dinv"][:, :].rearrange("p (c j) -> p c j", j=T),
                             dram["degree"].rearrange("(c p j) o -> p c (j o)", p=P, j=T)).then_inc(deg_in, 16)
                sp.wait_ge(dinv_calc, 4)
                sp.dma_start(dram["dinv"].rearrange("(c p j) o -> p c (j o)", p=P, j=T),
                             k["dinv"][:, :].rearrange("p (c j) -> p c j", j=T)).then_inc(dinv_out, 16)
                sp.wait_ge(w_in_rows, groups)
                wr = dram["edge_w"]
                sp.dma_start(wr[0:(groups - 1) * P * P].rearrange("(g t e) -> t g e", t=P, e=P),
                             w_rows[:, 0:groups - 1, :]).then_inc(w_out, 16)
                sp.dma_start(wr[(groups - 1) * P * P:sh.edges_padded].rearrange("(t e) -> t e", e=P),
                             w_rows[0:tail, groups - 1, :]).then_inc(w_out, 16)
                sp.wait_ge(w_out, 32)

            @block.tensor
            def _(pe):
                pe.wait_ge(loaded, loads[0])
                for i in range(2):
                    for g, r in enumerate(rows_of):
                        mm = pe.transpose(bank[i][:, g * P:g * P + r], run[i][0:r, g, :], k["ident"][0:r, 0:r])
                    mm.then_inc(in_psum, 1)
                pe.wait_ge(weighted, sh.edge_chunks)
                for g, r in enumerate(rows_of):
                    if g:
                        pe.wait_ge(w_in_rows, g)
                    pe.transpose(bank[2][0:r, 0:P], w_tab[:, g * P:g * P + r], k["ident"][:, :]).then_inc(in_psum, 1)

            @block.vector
            def _(dve):
                dve.wait_ge(in_psum, 1)
                dve.tensor_copy(deg_tab[:, :], bank[0][:, 0:sh.edge_tiles]).then_inc(tabs, 1)
                dve.wait_ge(in_psum, 2)
                dve.reciprocal(k["inv_count"][:, :], bank[1][:, 0:sh.edge_tiles]).then_inc(tabs, 1)
                dve.wait_ge(deg_in, 16)
                dve.tensor_scalar(k["dinv"][:, :], k["dinv"][:, :], 1.0, None, ALU.add).then_inc(dinv_calc, 1)
                dve.wait_ge(dinv_calc, 1)
                dve.tensor_scalar(pos[:, :], k["dinv"][:, :], 0.0, None, ALU.is_gt).then_inc(dinv_calc, 1)
                dve.tensor_scalar(lifted[:, :], k["dinv"][:, :], 1e-12, None, ALU.max).then_inc(dinv_calc, 1)
                dve.wait_ge(dinv_calc, 3)
                rsqrt(dve, root[:, :], lifted[:, :], root_tmp[:, :], root_step, 0)
                dve.tensor_tensor(k["dinv"][:, :], root[:, :], pos[:, :], ALU.mult).then_inc(dinv_calc, 1)
                dve.wait_ge(dinv_calc, 4)
                dv = k["dinv"][:, :].rearrange("p (c t) -> p c t", t=T)
                dve.tensor_copy(k["dinvs"][:, :, 0, :], dv).then_inc(tabs, 1)
                dve.tensor_tensor(k["dinvs"][:, :, 1, :], dv, dv, ALU.mult).then_inc(tabs, 1)
                with dve.Fori(0, sh.edge_chunks) as c:
                    dve.wait_ge(gathered, 16 * T * c + 16 * T)
                    dve.tensor_tensor(w_tab[:, bass.ds(c * T, T)], got[:, :], k["ew_tab"][:, bass.ds(c * T, T)],
                                      ALU.mult).then_inc(weighted, 1)
                for g, r in enumerate(rows_of):
                    dve.wait_ge(in_psum, 3 + g)
                    dve.tensor_copy(w_rows[0:r, g, :], bank[2][0:r, 0:P]).then_inc(w_in_rows, 1)
                dve.wait_ge(w_in_rows, groups)
                dve.wait_ge(tabs, 4)

            @block.gpsimd
            def _(pool):
                nodes_end = pool.to_reg(sh.n - 1)
                pool.wait_ge(tabs, 1)
                with pool.Fori(0, sh.edge_chunks) as c:
                    pool.tensor_copy(deg_slot[:, :], deg_tab[:, bass.ds(c * T, T)]).then_inc(slots, 1)
                    pool.tensor_copy(idx_slot[:, :], k["place_idx"][:, bass.ds(c * T, T)]).then_inc(slots, 1)
                    pool.wait_ge(slots, 2 * c + 2)
                    pool.sem_inc(gate, 1)
                    for t in range(T):
                        pool.indirect_dma_start(dram["degree"][:, :], bass.IndirectOffsetOnAxis(idx_slot[:, t:t + 1], 0),
                                                deg_slot[:, t:t + 1], None, bounds_check=nodes_end,
                                                oob_is_err=False).then_inc(scattered, 16)
                    pool.wait_ge(scattered, 16 * T * c + 16 * T)
                    pool.sem_inc(gate, 1)
                pool.wait_ge(dinv_out, 16)
                with pool.Fori(0, sh.edge_chunks) as c:
                    pool.tensor_copy(idx_slot[:, :], k["src_idx"][:, bass.ds(c * T, T)]).then_inc(slots, 1)
                    pool.wait_ge(slots, c + 2 * sh.edge_chunks + 1)
                    pool.sem_inc(gate, 1)
                    for t in range(T):
                        pool.indirect_dma_start(got[:, t:t + 1], None, dram["dinv"][:, :],
                                                bass.IndirectOffsetOnAxis(idx_slot[:, t:t + 1], 0)).then_inc(gathered, 16)
                    pool.wait_ge(weighted, c + 1)
                    pool.sem_inc(gate, 1)



class EdgePhase(Phase):

    def __init__(self, nc, name, k, dram, sh, table, both_ends=False):
        super().__init__(nc, name)
        self.k, self.dram, self.sh, self.table = k, dram, sh, table
        self.ends = [("src", "src_idx")] + ([("dst", "dst_idx")] if both_ends else [])

    def __enter__(self):
        super().__enter__()
        self.rows = {n: [self.sb(f"rows_{n}{b}", [P, T, D]) for b in range(2)] for n, _ in self.ends}
        self.idx = {n: [self.sb(f"idx_{n}{b}", [P, T], I32) for b in range(2)] for n, _ in self.ends}
        self.place = [self.sb(f"place{b}", [P, T], I32) for b in range(2)]
        self.result = [self.sb(f"result{b}", [P, T, D]) for b in range(2)]
        self.gate = self.sem("gate")
        self.slots = self.sem("slots")
        self.place_set = self.sem("place_set")
        self.gathered = self.pair("gathered")
        self.turned = self.sem("turned")
        self.result_ready = self.sem("result_ready")
        self.scattered = self.pair("scattered")
        return self

    def pool_program(self, pool):
        sh, k, n_ends = self.sh, self.k, len(self.ends)
        nodes_end = pool.to_reg(sh.n - 1)

        def gather(c, b, q):
            if used_before(c, 2):
                pool.wait_ge(self.turned, 2 * c - 2)
                pool.sem_inc(self.gate, 1)
            for n, tab in self.ends:
                pool.tensor_copy(self.idx[n][b][:, :], k[tab][:, bass.ds(c * T, T)]).then_inc(self.slots, 1)
            pool.wait_ge(self.slots, n_ends * c + n_ends)
            pool.sem_inc(self.gate, 1)
            for t in range(T):
                for n, _ in self.ends:
                    pool.indirect_dma_start(self.rows[n][b][:, t, :], None, self.table[:, :],
                                            bass.IndirectOffsetOnAxis(self.idx[n][b][:, t:t + 1], 0)).then_inc(self.gathered[b], 16)

        def scatter(c, b):
            pool.wait_ge(self.result_ready, 2 * c + 2)
            pool.sem_inc(self.gate, 1)
            pool.tensor_copy(self.place[b][:, :], k["place_idx"][:, bass.ds(c * T, T)]).then_inc(self.place_set, 1)
            pool.wait_ge(self.place_set, c + 1)
            pool.sem_inc(self.gate, 1)
            for t in range(T):
                pool.indirect_dma_start(self.dram["node_sums"][:, :], bass.IndirectOffsetOnAxis(self.place[b][:, t:t + 1], 0),
                                        self.result[b][:, t, :], None, bounds_check=nodes_end,
                                        oob_is_err=False).then_inc(self.scattered[b], 16)

        def step(c, b, q):
            gather(c, b, q)
            if used_before(c, 2):
                scatter(c - 2, b)

        sweep(pool, sh.edge_chunks, sh.edge_chunks - 1, step)
        for c in (sh.edge_chunks - 2, sh.edge_chunks - 1):
            scatter(c, c % 2)
        pool.wait_ge(self.scattered[0], 16 * T * ((sh.edge_chunks + 1) // 2))
        pool.wait_ge(self.scattered[1], 16 * T * (sh.edge_chunks // 2))

    def rows_landed(self, eng, b, q):
        n = 16 * T * len(self.ends)
        eng.wait_ge(self.gathered[b], n * q + n)

    def result_free(self, eng, c, b, q):
        if used_before(c, 2):
            eng.wait_ge(self.scattered[b], 16 * T * q)


def half_no(c, h):
    return 2 * c + (h + 1)


def tiles_of(h):
    return range(H * h, H * h + H)


def gat_edges(nc, a, k, dram, sh, name, table):
    n_attr = a["edge_attr_16"].shape[1]
    real = sh.e - (sh.edge_chunks - 1) * CH
    with EdgePhase(nc, name, k, dram, sh, table, both_ends=True) as ph:
        attr = [ph.sb(f"attr{b}", [P, T, n_attr]) for b in range(2)]
        sT = [ph.sb(f"sT{h}", [P, HALF]) for h in range(2)]
        dT = [ph.sb(f"dT{h}", [P, HALF]) for h in range(2)]
        eT = [ph.sb(f"eT{h}", [n_attr, HALF]) for h in range(2)]
        val = [ph.sb(f"val{h}", [P, HALF]) for h in range(2)]
        pre = [ph.sb(f"pre{h}", [P, HALF]) for h in range(2)]
        top = [ph.sb(f"top{h}", [P, HALF + 1]) for h in range(2)]
        begin = [ph.sb(f"begin{h}", [P, HALF]) for h in range(2)]
        fall = [ph.sb(f"fall{h}", [P, HALF]) for h in range(2)]
        prob = [ph.sb(f"prob{h}", [P, HALF]) for h in range(2)]
        num = [ph.sb(f"num{h}", [P, HALF]) for h in range(2)]
        den = [ph.sb(f"den{h}", [P, HALF]) for h in range(2)]
        mean = [ph.sb(f"mean{h}", [P, HALF]) for h in range(2)]
        src_ps = ph.ps("src", [P, HALF])
        dst_ps = ph.ps("dst", [P, HALF])
        attr_ps = ph.ps("attr", [P, HALF])
        val_ps = ph.ps("val", [P, HALF])
        pre_ps = ph.ps("pre", [P, HALF])
        logit_ps = ph.ps("logit", [P, HALF])
        out_ps = ph.ps("out", [P, HALF])
        attr_in = ph.pair("attr_in")
        attr_set = ph.sem("attr_set")
        in_sb = ph.sem("in_sb")
        val_mm = ph.sem("val_mm")
        pre_mm = ph.sem("pre_mm")
        val_set = ph.sem("val_set")
        pre_set = ph.sem("pre_set")
        leaky = ph.sem("leaky")
        logits = ph.sem("logits")
        begun = ph.sem("begun")
        topped = ph.sem("topped")
        diffs = ph.sem("diffs")
        lowered = ph.sem("lowered")
        exps = ph.sem("exps")
        probs_v = ph.sem("probs_v")
        num_done = ph.sem("num_done")
        den_done = ph.sem("den_done")
        guarded = ph.sem("guarded")
        divided = ph.sem("divided")
        multiplied = ph.sem("multiplied")
        top_set = ph.sem("top_set")
        with nc.Block() as block:
            @block.gpsimd
            def _(pool):
                pool.memset(attr[(sh.edge_chunks - 1) % 2][:, :, :], 0.0).then_inc(attr_set, 1)
                ph.pool_program(pool)

            @block.sync
            def _(sp):
                sp.wait_ge(attr_set, 1)

                def step(c, b, q):
                    if used_before(c, 2):
                        sp.wait_ge(ph.turned, 2 * c - 2)
                    ea = a["edge_attr_16"]
                    if isinstance(c, int) and c == sh.edge_chunks - 1:
                        whole, left = real // P, real % P
                        sp.dma_start(attr[b][:, 0:whole, :], ea[c * CH:c * CH + whole * P, :].rearrange("(t p) d -> p t d", p=P)).then_inc(attr_in[b], 16)
                        sp.dma_start(attr[b][0:left, whole, :], ea[c * CH + whole * P:sh.e, :]).then_inc(attr_in[b], 16)
                    else:
                        sp.dma_start(attr[b][:, :, :], ea[bass.ds(c * CH, CH), :].rearrange("(t p) d -> p t d", p=P)).then_inc(attr_in[b], 16)

                sweep(sp, sh.edge_chunks, sh.edge_chunks - 1, step)

            @block.tensor
            def _(pe):
                def front(c, b, q, h):
                    if h == 0:
                        ph.rows_landed(pe, b, q)
                        last = isinstance(c, int) and c == sh.edge_chunks - 1
                        pe.wait_ge(attr_in[b], 16 * q + 16 + (16 if last else 0))
                    if used_before(c, 1) or h:
                        pe.wait_ge(in_sb, 3 * (2 * c + h))
                    for i, t in enumerate(tiles_of(h)):
                        pe.transpose(src_ps[:, i * P:(i + 1) * P], ph.rows["src"][b][:, t, :], k["ident"][:, :])
                        pe.transpose(dst_ps[:, i * P:(i + 1) * P], ph.rows["dst"][b][:, t, :], k["ident"][:, :])
                        mm = pe.transpose(attr_ps[0:n_attr, i * P:(i + 1) * P], attr[b][:, t, :], k["ident"][:, :])
                    mm.then_inc(ph.turned, 1)
                    pe.wait_ge(in_sb, 3 * (2 * c + h) + 3)
                    if used_before(c, 1) or h:
                        pe.wait_ge(val_set, 2 * c + h)
                    pe.matmul(val_ps[:, :], k["gat_l"][:, :], sT[h][:, :], start=True, stop=True).then_inc(val_mm, 1)
                    if used_before(c, 1) or h:
                        pe.wait_ge(pre_set, 2 * c + h)
                    pe.matmul(pre_ps[:, :], k["gat_l"][:, :], sT[h][:, :], start=True, stop=False)
                    pe.matmul(pre_ps[:, :], k["gat_r"][:, :], dT[h][:, :], start=False, stop=False)
                    pe.matmul(pre_ps[:, :], k["gat_e"][0:n_attr, :], eT[h][:, :], start=False, stop=True).then_inc(pre_mm, 1)
                    pe.wait_ge(leaky, 2 * c + h + 1)
                    if used_before(c, 1) or h:
                        pe.wait_ge(lowered, 2 * c + h)
                    pe.matmul(logit_ps[:, :], k["head_att"][:, :], pre[h][:, :], start=True, stop=True).then_inc(logits, 1)

                def back(c, b, q, h):
                    pe.wait_ge(divided, 2 * c + h + 1)
                    if used_before(c, 1) or h:
                        pe.wait_ge(ph.result_ready, 2 * c + h)
                    for i in range(H):
                        mm = pe.transpose(out_ps[:, i * P:(i + 1) * P], mean[h][:, i * P:(i + 1) * P], k["ident"][:, :])
                    mm.then_inc(multiplied, 1)

                def step(c, b, q):
                    front(c, b, q, 0)
                    front(c, b, q, 1)
                    back(c, b, q, 0)
                    back(c, b, q, 1)

                sweep(pe, sh.edge_chunks, sh.edge_chunks - 1, step)

            @block.scalar
            def _(act):
                def step(c, b, q):
                    for h in range(2):
                        act.wait_ge(ph.turned, 2 * c + h + 1)
                        if used_before(c, 1):
                            act.wait_ge(pre_mm, 2 * c + h - 1)
                        act.activation(sT[h][:, :], src_ps[:, :], ACT.Copy).then_inc(in_sb, 1)
                        act.activation(dT[h][:, :], dst_ps[:, :], ACT.Copy).then_inc(in_sb, 1)
                        act.activation(eT[h][:, :], attr_ps[0:n_attr, :], ACT.Copy).then_inc(in_sb, 1)
                        act.wait_ge(val_mm, 2 * c + h + 1)
                        if used_before(c, 1):
                            act.wait_ge(probs_v, 2 * c + h - 1)
                        act.activation(val[h][:, :], val_ps[:, :], ACT.Identity, bias=k["bl"][:, 0:1]).then_inc(val_set, 1)
                        act.wait_ge(pre_mm, 2 * c + h + 1)
                        if used_before(c, 1):
                            act.wait_ge(logits, 2 * c + h - 1)
                        act.activation(pre[h][:, :], pre_ps[:, :], ACT.Identity, bias=k["blr"][:, 0:1]).then_inc(pre_set, 1)
                        if used_before(c, 1):
                            act.wait_ge(diffs, 2 * c + h - 1)
                            act.sem_inc(ph.gate, 1)
                        act.activation(begin[h][:, :], k["same_run"][:, bass.ds(c * CH + h * HALF, HALF)], ACT.Copy,
                                       bias=-BIG, scale=BIG).then_inc(begun, 1)
                    for h in range(2):
                        act.wait_ge(lowered, 2 * c + h + 1)
                        act.activation(fall[h][:, :], fall[h][:, :], ACT.Exp).then_inc(exps, 1)
                        act.activation(prob[h][:, :], prob[h][:, :], ACT.Exp).then_inc(exps, 1)
                    for h in range(2):
                        act.wait_ge(multiplied, 2 * c + h + 1)
                        ph.result_free(act, c, b, q)
                        act.activation(ph.result[b][:, H * h:H * h + H, :].rearrange("p t f -> p (t f)"), out_ps[:, :],
                                       ACT.Copy).then_inc(ph.result_ready, 1)

                sweep(act, sh.edge_chunks, sh.edge_chunks - 1, step)

            @block.vector
            def _(dve):
                dve.memset(top[1][:, HALF:HALF + 1], 0.0).then_inc(top_set, 1)
                dve.wait_ge(top_set, 1)

                def front(c, b, q, h):
                    dve.wait_ge(pre_set, 2 * c + h + 1)
                    dve.scalar_tensor_tensor(out=pre[h][:, :], in0=pre[h][:, :], scalar=0.2, in1=pre[h][:, :], op0=ALU.mult,
                                             op1=ALU.max).then_inc(leaky, 1)
                    if used_before(c, 1):
                        dve.wait_ge(diffs, 2 * c + h - 1)
                        dve.wait_ge(exps, 2 * (2 * c + h - 1))
                    if used_before(c, 1) or h:
                        dve.wait_ge(topped, 2 * c + h)
                    dve.tensor_copy(top[h][:, 0:1], top[1 - h][:, HALF:HALF + 1]).then_inc(top_set, 1)
                    dve.wait_ge(top_set, 2 * c + h + 2)
                    dve.wait_ge(logits, 2 * c + h + 1)
                    dve.wait_ge(begun, 2 * c + h + 1)
                    dve.tensor_tensor_scan(top[h][:, 1:HALF + 1], begin[h][:, :], logit_ps[:, :], top[h][:, 0:1], ALU.add,
                                           ALU.max).then_inc(topped, 1)
                    if used_before(c, 1):
                        dve.wait_ge(num_done, 2 * c + h - 1)
                        dve.wait_ge(den_done, 2 * c + h - 1)
                    dve.wait_ge(topped, 2 * c + h + 1)
                    dve.tensor_tensor(fall[h][:, :], top[h][:, 0:HALF], begin[h][:, :], ALU.add).then_inc(diffs, 1)
                    dve.wait_ge(diffs, 2 * c + h + 1)
                    dve.tensor_tensor(prob[h][:, :], logit_ps[:, :], top[h][:, 1:HALF + 1], ALU.subtract)
                    dve.tensor_tensor(fall[h][:, :], fall[h][:, :], top[h][:, 1:HALF + 1], ALU.subtract).then_inc(lowered, 1)

                def back(c, b, q, h):
                    dve.wait_ge(exps, 2 * (2 * c + h + 1))
                    go_on = (lambda z: z[1 - h][:, HALF - 1:HALF] if h or used_before(c, 1) else 0.0)
                    if used_before(c, 1) or h:
                        dve.wait_ge(den_done, 2 * c + h)
                        dve.wait_ge(num_done, 2 * c + h)
                    if used_before(c, 1):
                        dve.wait_ge(divided, 2 * c + h - 1)
                    dve.tensor_tensor_scan(den[h][:, :], fall[h][:, :], prob[h][:, :], go_on(den), ALU.mult,
                                           ALU.add).then_inc(den_done, 1)
                    dve.tensor_tensor(val[h][:, :], val[h][:, :], prob[h][:, :], ALU.mult).then_inc(probs_v, 1)
                    dve.wait_ge(probs_v, 2 * c + h + 1)
                    dve.tensor_tensor_scan(num[h][:, :], fall[h][:, :], val[h][:, :], go_on(num), ALU.mult,
                                           ALU.add).then_inc(num_done, 1)
                    dve.wait_ge(num_done, 2 * c + h + 1)
                    dve.wait_ge(den_done, 2 * c + h + 1)
                    if used_before(c, 1):
                        dve.wait_ge(multiplied, 2 * c + h - 1)
                    dve.tensor_scalar(mean[h][:, :], den[h][:, :], 1e-16, None, ALU.add).then_inc(guarded, 1)
                    dve.wait_ge(guarded, 2 * (2 * c + h) + 1)
                    dve.reciprocal(mean[h][:, :], mean[h][:, :]).then_inc(guarded, 1)
                    dve.wait_ge(guarded, 2 * (2 * c + h) + 2)
                    dve.tensor_tensor(mean[h][:, :], num[h][:, :], mean[h][:, :], ALU.mult).then_inc(divided, 1)

                def step(c, b, q):
                    front(c, b, q, 0)
                    front(c, b, q, 1)
                    back(c, b, q, 0)
                    back(c, b, q, 1)

                sweep(dve, sh.edge_chunks, sh.edge_chunks - 1, step)



class LayerNorm:
    STEPS = 7 + RSQRT_STEPS

    def __init__(self, ph, name):
        self.stats = [ph.sb(f"{name}_stats{b}", [P, T, 6]) for b in range(2)]
        self.tmp = [ph.sb(f"{name}_tmp{b}", [P, 3, T]) for b in range(2)]
        self.scale = [ph.sb(f"{name}_scale{b}", [P, T]) for b in range(2)]
        self.shift = [ph.sb(f"{name}_shift{b}", [P, T]) for b in range(2)]
        self.step = ph.sem(f"{name}_step")
        self.ready = ph.sem(f"{name}_ready")

    def on_vector(self, dve, z, n, c, b):
        base = c * self.STEPS
        s, t = self.stats[b], self.tmp[b]
        for j in range(T):
            ins = dve.bn_stats(s[0:n, j, :], z[0:n, j, :])
        ins.then_inc(self.step, 1)
        dve.wait_ge(self.step, base + 1)
        me, mo, ve, vo = (s[0:n, :, i] for i in (1, 4, 2, 5))
        dve.tensor_tensor(t[0:n, 0, :], me, mo, ALU.subtract).then_inc(self.step, 1)
        dve.tensor_tensor(t[0:n, 1, :], ve, vo, ALU.add).then_inc(self.step, 1)
        dve.tensor_tensor(t[0:n, 2, :], me, mo, ALU.add).then_inc(self.step, 1)
        dve.wait_ge(self.step, base + 4)
        dve.scalar_tensor_tensor(out=t[0:n, 0, :], in0=t[0:n, 0, :], scalar=D / 4.0, in1=t[0:n, 0, :], op0=ALU.mult,
                                 op1=ALU.mult).then_inc(self.step, 1)
        dve.wait_ge(self.step, base + 5)
        dve.tensor_tensor(t[0:n, 1, :], t[0:n, 1, :], t[0:n, 0, :], ALU.add).then_inc(self.step, 1)
        dve.wait_ge(self.step, base + 6)
        dve.tensor_scalar(t[0:n, 1, :], t[0:n, 1, :], 1.0 / D, LN_EPS, ALU.mult, ALU.add).then_inc(self.step, 1)
        dve.wait_ge(self.step, base + 7)
        scale = self.scale[b][0:n, :]
        rsqrt(dve, scale, t[0:n, 1, :], t[0:n, 0, :], self.step, base + 7)
        dve.scalar_tensor_tensor(out=self.shift[b][0:n, :], in0=t[0:n, 2, :], scalar=-0.5, in1=scale,
                                 op0=ALU.mult, op1=ALU.mult).then_inc(self.ready, 1)

    def apply(self, act, out, z, n, c, b, done):
        act.wait_ge(self.ready, c + 1)
        for j in range(T):
            ins = act.activation(out[0:n, j, :], z[0:n, j, :], ACT.Identity, bias=self.shift[b][0:n, j:j + 1],
                                 scale=self.scale[b][0:n, j:j + 1])
        ins.then_inc(done, 1)


class PairNorm:
    STEPS = 6 + RSQRT_STEPS

    def __init__(self, ph, name):
        self.stats = ph.sb(f"{name}_stats", [P, 2 * T, 6])
        self.tmp = ph.sb(f"{name}_tmp", [P, 3, 2 * T])
        self.scale = ph.sb(f"{name}_scale", [P, 2 * T])
        self.shift = ph.sb(f"{name}_shift", [P, 2 * T])
        self.step = ph.sem(f"{name}_step")
        self.ready = ph.sem(f"{name}_ready")

    def on_vector(self, dve, z, rows, m, upto=2):
        base = m * self.STEPS
        s, t = self.stats, self.tmp
        for b in range(2):
            for j in range(T):
                ins = dve.bn_stats(s[0:rows[b], b * T + j, :], z[b][0:rows[b], j, :])
        ins.then_inc(self.step, 1)
        dve.wait_ge(self.step, base + 1)
        me, mo, ve, vo = (s[:, :, i] for i in (1, 4, 2, 5))
        dve.tensor_tensor(t[:, 0, :], me, mo, ALU.subtract).then_inc(self.step, 1)
        dve.tensor_tensor(t[:, 1, :], ve, vo, ALU.add).then_inc(self.step, 1)
        dve.tensor_tensor(t[:, 2, :], me, mo, ALU.add)
        dve.wait_ge(self.step, base + 2)
        dve.scalar_tensor_tensor(out=t[:, 0, :], in0=t[:, 0, :], scalar=D / 4.0, in1=t[:, 0, :], op0=ALU.mult,
                                 op1=ALU.mult).then_inc(self.step, 1)
        dve.wait_ge(self.step, base + 4)
        dve.tensor_tensor(t[:, 1, :], t[:, 1, :], t[:, 0, :], ALU.add).then_inc(self.step, 1)
        dve.wait_ge(self.step, base + 5)
        dve.tensor_scalar(t[:, 1, :], t[:, 1, :], 1.0 / D, LN_EPS, ALU.mult, ALU.add).then_inc(self.step, 1)
        dve.wait_ge(self.step, base + 6)
        rsqrt(dve, self.scale[:, :], t[:, 1, :], t[:, 0, :], self.step, base + 6)
        dve.scalar_tensor_tensor(out=self.shift[:, :], in0=t[:, 2, :], scalar=-0.5, in1=self.scale[:, :],
                                 op0=ALU.mult, op1=ALU.mult).then_inc(self.ready, 1)

    def apply(self, act, out, z, n, b):
        for j in range(T):
            at = b * T + j
            ins = act.activation(out[0:n, j, :], z[0:n, j, :], ACT.Identity, bias=self.shift[0:n, at:at + 1],
                                 scale=self.scale[0:n, at:at + 1])
        return ins


class NodePhase(Phase):

    def __init__(self, nc, name, sh, streams, out):
        super().__init__(nc, name)
        self.sh, self.streams, self.out_dram = sh, streams, out

    def __enter__(self):
        super().__enter__()
        self.buf = {n: [self.sb(f"in_{n}{b}", [P, T, D]) for b in range(2)] for n in self.streams}
        self.landed = {n: self.pair(f"landed_{n}") for n in self.streams}
        self.out_ready = self.sem("out_ready")
        self.stored = self.pair("stored")
        return self

    def load_program(self, sp, free):
        def step(c, b, q):
            n = self.sh.rows(c)
            for name, src in self.streams.items():
                if used_before(c, 2):
                    for sem, per in free[name]:
                        sp.wait_ge(sem, per * (c - 1))
                sp.dma_start(self.buf[name][b][0:n, :, :], node_rows(src, c, self.sh)).then_inc(self.landed[name][b], 16)

        self.node_sweep(sp, step)

    def node_sweep(self, eng, step):
        sweep(eng, self.sh.node_chunks, self.sh.node_chunks - 1, step)

    def have(self, eng, name, b, q):
        eng.wait_ge(self.landed[name][b], 16 * q + 16)

    def store(self, eng, out, c, b):
        n = self.sh.rows(c)
        eng.wait_ge(self.out_ready, c + 1)
        eng.dma_start(node_rows(self.out_dram, c, self.sh), out[b][0:n, :, 0:D]).then_inc(self.stored[b], 16)

    def out_free(self, eng, c, b, q):
        if used_before(c, 2):
            eng.wait_ge(self.stored[b], 16 * q)

    def all_stored(self, eng):
        eng.wait_ge(self.stored[0], 16 * ((self.sh.node_chunks + 1) // 2))
        eng.wait_ge(self.stored[1], 16 * (self.sh.node_chunks // 2))


def norm_nodes(nc, k, dram, sh, name, table, x0, out, scale_row, shift_row):
    with NodePhase(nc, name, sh, {"y": table, "x0": x0}, out) as ph:
        z = [ph.sb(f"z{b}", [P, T, D]) for b in range(2)]
        o = [ph.sb(f"o{b}", [P, T, D]) for b in range(2)]
        ln = LayerNorm(ph, "ln")
        shifted, scaled, z_done = ph.sem("shifted"), ph.sem("scaled"), ph.sem("z_done")
        with nc.Block() as block:
            @block.sync
            def _(sp):
                ph.load_program(sp, {"y": [(scaled, 1)], "x0": [(z_done, 1)]})

            @block.gpsimd
            def _(pool):
                def step(c, b, q):
                    n = sh.rows(c)
                    x = ph.buf["x0"][b][0:n, :, :]
                    ph.have(pool, "x0", b, q)
                    pool.tensor_tensor(x, x, spread_slots(shift_row[0:n, :], [n, T, D]), ALU.add).then_inc(shifted, 1)

                ph.node_sweep(pool, step)

            @block.vector
            def _(dve):
                def step(c, b, q):
                    n = sh.rows(c)
                    ph.have(dve, "y", b, q)
                    if used_before(c, 2):
                        dve.wait_ge(ph.out_ready, c - 1)
                    dve.tensor_tensor(z[b][0:n, :, :], ph.buf["y"][b][0:n, :, :], spread_slots(scale_row[0:n, :], [n, T, D]),
                                      ALU.mult).then_inc(scaled, 1)
                    dve.wait_ge(scaled, c + 1)
                    dve.wait_ge(shifted, c + 1)
                    dve.tensor_tensor(z[b][0:n, :, :], z[b][0:n, :, :], ph.buf["x0"][b][0:n, :, :], ALU.add).then_inc(z_done, 1)
                    dve.wait_ge(z_done, c + 1)
                    ln.on_vector(dve, z[b], n, c, b)

                ph.node_sweep(dve, step)

            @block.scalar
            def _(act):
                def step(c, b, q):
                    n = sh.rows(c)
                    ph.out_free(act, c, b, q)
                    ln.apply(act, o[b], z[b], n, c, b, ph.out_ready)
                    ph.store(act, o, c, b)

                ph.node_sweep(act, step)
                ph.all_stored(act)


def gat_nodes(nc, k, dram, sh, name, table, out):
    with NodePhase(nc, name, sh, {"sums": dram["node_sums"], "x": table}, out) as ph:
        act_out = [ph.sb(f"gelu{b}", [P, T, D]) for b in range(2)]
        x_beta = [ph.sb(f"x_beta{b}", [P, T, D]) for b in range(2)]
        z1 = [ph.sb(f"z1{b}", [P, T, D]) for b in range(2)]
        z2 = [ph.sb(f"z2{b}", [P, T, D]) for b in range(2)]
        o = [ph.sb(f"o{b}", [P, T, D]) for b in range(2)]
        ln1, ln2 = LayerNorm(ph, "ln1"), LayerNorm(ph, "ln2")
        biased, beta_added, gelu_done = ph.sem("biased"), ph.sem("beta_added"), ph.sem("gelu_done")
        z1_done, normed, scaled, z2_done = ph.sem("z1_done"), ph.sem("normed"), ph.sem("scaled"), ph.sem("z2_done")
        gate = ph.sem("gate")
        with nc.Block() as block:
            @block.sync
            def _(sp):
                ph.load_program(sp, {"sums": [(gelu_done, 1)], "x": [(z1_done, 1), (beta_added, 1)]})

            @block.gpsimd
            def _(pool):
                def scale(c, b):
                    n = sh.rows(c)
                    z = z2[b][0:n, :, :]
                    pool.wait_ge(normed, c + 1)
                    pool.tensor_tensor(z, z, spread_slots(k["gat_gamma"][0:n, :], [n, T, D]), ALU.mult).then_inc(scaled, 1)

                def step(c, b, q):
                    n = sh.rows(c)
                    g = ph.buf["sums"][b][0:n, :, :]
                    ph.have(pool, "sums", b, q)
                    pool.tensor_tensor(g, g, spread_slots(k["gat_b"][0:n, :], [n, T, D]), ALU.add).then_inc(biased, 1)
                    ph.have(pool, "x", b, q)
                    if used_before(c, 2):
                        pool.wait_ge(z2_done, c - 1)
                    pool.tensor_tensor(x_beta[b][0:n, :, :], ph.buf["x"][b][0:n, :, :],
                                       spread_slots(k["gat_beta"][0:n, :], [n, T, D]), ALU.add).then_inc(beta_added, 1)
                    if used_before(c, 1):
                        scale(c - 1, 1 - b)

                ph.node_sweep(pool, step)
                last_c = sh.node_chunks - 1
                scale(last_c, last_c % 2)

            @block.scalar
            def _(act):
                def second(c, b, q):
                    n = sh.rows(c)
                    ph.out_free(act, c, b, q)
                    ln2.apply(act, o[b], z2[b], n, c, b, ph.out_ready)
                    ph.store(act, o, c, b)

                def step(c, b, q):
                    n = sh.rows(c)
                    act.wait_ge(biased, c + 1)
                    if used_before(c, 2):
                        act.wait_ge(z1_done, c - 1)
                    act.activation(act_out[b][0:n, :, :], ph.buf["sums"][b][0:n, :, :], ACT.Gelu).then_inc(gelu_done, 1)
                    if used_before(c, 1):
                        second(c - 1, 1 - b, q if b else q - 1)
                    ln1.apply(act, z2[b], z1[b], n, c, b, normed)

                ph.node_sweep(act, step)
                last_c = sh.node_chunks - 1
                second(last_c, last_c % 2, last_c // 2)
                ph.all_stored(act)

            @block.vector
            def _(dve):
                def second(c, b):
                    n = sh.rows(c)
                    dve.wait_ge(scaled, c + 1)
                    dve.tensor_tensor(z2[b][0:n, :, :], z2[b][0:n, :, :], x_beta[b][0:n, :, :], ALU.add).then_inc(z2_done, 1)
                    dve.wait_ge(z2_done, c + 1)
                    ln2.on_vector(dve, z2[b], n, c, b)

                def step(c, b, q):
                    n = sh.rows(c)
                    dve.wait_ge(gelu_done, c + 1)
                    ph.have(dve, "x", b, q)
                    if used_before(c, 2):
                        dve.wait_ge(normed, c - 1)
                    dve.tensor_tensor(z1[b][0:n, :, :], act_out[b][0:n, :, :], ph.buf["x"][b][0:n, :, :], ALU.add).then_inc(z1_done, 1)
                    dve.wait_ge(z1_done, c + 1)
                    ln1.on_vector(dve, z1[b], n, c, b)
                    if used_before(c, 1):
                        second(c - 1, 1 - b)

                ph.node_sweep(dve, step)
                last_c = sh.node_chunks - 1
                second(last_c, last_c % 2)



def merged_sweep(eng, k, sh, edge_unit, node_unit):
    full, last = sh.edge_pairs, sh.node_pairs - 1

    def ready(j):
        at = slice(j + 1, j + 2) if isinstance(j, int) else bass.ds(j + 1, 1)
        return eng.value_load(k["ready"][0:1, at], min_val=0, max_val=last)

    def nodes(first, end, at, scattered):
        with eng.If(first < end):
            with eng.Fori(first, end) as m:
                node_unit(m, m * 4 + at, scattered)
        with eng.Else():
            pass

    edge_unit(0, 0, None, 4)
    with eng.Fori(1, full) as j:
        before2, before, end = ready(j - 2), ready(j - 1), ready(j)
        edge_unit(j, j * 4 + before * 4, j * 4 + before2 * 4 - 4, 4)
        if node_unit:
            nodes(before, end, j * 4 + 4, j)
    before2, before = ready(full - 2), ready(full - 1)
    edge_unit(full, before * 4 + 4 * full, before2 * 4 + 4 * (full - 1), 2)
    if node_unit:
        at = 4 * full + 2
        nodes(before, last, at, None)
        node_unit(last, last * 4 + at, None)


class Conv(Phase):

    def __init__(self, nc, name, k, dram, sh, table, out, streams):
        super().__init__(nc, name)
        self.k, self.dram, self.sh, self.table, self.out_dram, self.streams = k, dram, sh, table, out, streams

    def __enter__(self):
        super().__enter__()
        self.rows = [self.sb(f"rows{b}", [P, T, D]) for b in range(2)]
        self.idx = [self.sb(f"idx{b}", [P, T], I32) for b in range(2)]
        self.place = [self.sb(f"place{b}", [P, T], I32) for b in range(2)]
        self.result = [self.sb(f"result{b}", [P, T, D]) for b in range(2)]
        self.gate = self.sem("gate")
        self.slots = self.sem("slots")
        self.place_set = self.sem("place_set")
        self.gathered = self.pair("gathered")
        self.scattered = self.pair("scattered")
        self.turn_ps = [self.ps(f"turn{i}", [P, HALF]) for i in range(2)]
        self.out_ps = [self.ps(f"out{i}", [P, HALF]) for i in range(2)]
        self.turned = self.sem("turned")
        self.turn_read = self.sem("turn_read")
        self.multiplied = self.sem("multiplied")
        self.out_read = self.sem("out_read")
        self.buf = {n: [self.sb(f"in_{n}{b}", [P, T, D]) for b in range(2)] for n in self.streams}
        self.landed = {n: self.pair(f"landed_{n}") for n in self.streams}
        self.used = {n: self.sem(f"used_{n}") for n in self.streams if n != "y"}
        self.nodeT = self.sb("nodeT", [P, 4, HALF])
        self.finished = self.sem("finished")
        self.stored = self.pair("stored")
        return self

    def grant(self, eng, semaphores):
        for sem, n in semaphores:
            eng.sem_inc(sem, n)


    def pool_program(self, pool):
        sh, k = self.sh, self.k
        nodes_end = pool.to_reg(sh.n - 1)

        def gather(c, b, free_at):
            if free_at is not None:
                pool.wait_ge(self.turned, free_at)
                pool.sem_inc(self.gate, 1)
            pool.tensor_copy(self.idx[b][:, :], k["src_idx"][:, bass.ds(c * T, T)]).then_inc(self.slots, 1)
            pool.wait_ge(self.slots, c + 1)
            pool.sem_inc(self.gate, 1)
            for t in range(T):
                pool.indirect_dma_start(self.rows[b][:, t, :], None, self.table[:, :],
                                        bass.IndirectOffsetOnAxis(self.idx[b][:, t:t + 1], 0)).then_inc(self.gathered[b], 16)

        def scatter(c, b, ready_at):
            pool.wait_ge(self.out_read, ready_at)
            pool.sem_inc(self.gate, 1)
            pool.tensor_copy(self.place[b][:, :], k["place_idx"][:, bass.ds(c * T, T)]).then_inc(self.place_set, 1)
            pool.wait_ge(self.place_set, c + 1)
            pool.sem_inc(self.gate, 1)
            for t in range(T):
                pool.indirect_dma_start(self.dram["node_sums"][:, :], bass.IndirectOffsetOnAxis(self.place[b][:, t:t + 1], 0),
                                        self.result[b][:, t, :], None, bounds_check=nodes_end,
                                        oob_is_err=False).then_inc(self.scattered[b], 16)

        def unit(j, at, at_before, halves):
            for b in range(halves // 2):
                gather(2 * j + b, b, None if at_before is None else at_before + 2 * b + 2)
                if at_before is not None:
                    scatter(2 * j - 2 + b, b, at_before + 2 * b + 2)
            if halves == 2:
                scatter(2 * j - 1, 1, at_before + 4)
                scatter(2 * j, 0, at + 2)

        merged_sweep(pool, k, sh, unit, None)
        for b in range(2):
            pool.wait_ge(self.scattered[b], self.all_scattered(b))

    def all_scattered(self, b):
        return 16 * T * ((self.sh.edge_chunks + 1 - b) // 2)

    def rows_landed(self, eng, j, b):
        eng.wait_ge(self.gathered[b], 16 * T * j + 16 * T)

    def turn_edges(self, pe, j, at, halves):
        for i in range(halves):
            if i % 2 == 0:
                self.rows_landed(pe, j, i // 2)
            if not isinstance(at, int) or at + i >= 2:
                pe.wait_ge(self.turn_read, at + i - 1)
            for n in range(H):
                mm = pe.transpose(self.turn_ps[i % 2][:, n * P:(n + 1) * P], self.rows[i // 2][:, H * (i % 2) + n, :],
                                  self.k["ident"][:, :])
            mm.then_inc(self.turned, 1)

    def multiply_edges(self, pe, at, halves, ready, lhs, weight):
        for i in range(halves):
            ready(i)
            if not isinstance(at, int) or at + i >= 2:
                pe.wait_ge(self.out_read, at + i - 1)
            for n in range(H):
                mm = pe.matmul(self.out_ps[i % 2][:, n * D:(n + 1) * D], lhs(i)[:, n * P:(n + 1) * P], weight[:, :],
                               start=True, stop=True)
            mm.then_inc(self.multiplied, 1)

    def result_half(self, i):
        return self.result[i // 2][:, H * (i % 2):H * (i % 2) + H, :]

    def out_half(self, i, n=P):
        return self.out_ps[i % 2][0:n, :].rearrange("p (t f) -> p t f", f=D)

    def result_free(self, eng, j, i):
        if not isinstance(j, int) or j >= 1:
            eng.wait_ge(self.scattered[i // 2], 16 * T * j)


    def load_nodes(self, sp, m, at, scattered_pairs):
        for b in range(2):
            c = m * 2 + b
            n = self.sh.rows(c)
            for name, src in self.streams.items():
                if name == "y":
                    sp.wait_ge(self.turned, at - 2 + 2 * b)
                    sp.sem_inc(self.gate, 1)
                if name in self.used:
                    sp.wait_ge(self.used[name], 2 * m + b + 1)
                    sp.sem_inc(self.gate, 1)
                if name == "sums":
                    for s in range(2):
                        sp.wait_ge(self.scattered[s], self.all_scattered(s) if scattered_pairs is None else scattered_pairs * (16 * T))
                        sp.sem_inc(self.gate, 1)
                sp.dma_start(self.buf[name][b][0:n, :, :], node_rows(src, c, self.sh)).then_inc(self.landed[name][b], 16)

    def have(self, eng, name, m, b):
        eng.wait_ge(self.landed[name][b], 16 * m + 16)

    def turn_nodes(self, pe, m, at):
        for i in range(4):
            n = self.sh.rows(m * 2 + i // 2)
            if i % 2 == 0:
                self.have(pe, "y", m, i // 2)
            pe.wait_ge(self.turn_read, at + i - 1)
            for t in range(H):
                mm = pe.transpose(self.turn_ps[i % 2][:, t * P:t * P + n], self.buf["y"][i // 2][0:n, H * (i % 2) + t, :],
                                  self.k["ident"][0:n, 0:n])
            mm.then_inc(self.turned, 1)

    def multiply_nodes(self, pe, m, at, weight):
        for i in range(4):
            n = self.sh.rows(m * 2 + i // 2)
            pe.wait_ge(self.turn_read, at + i + 1)
            pe.wait_ge(self.out_read, at + i - 1)
            for t in range(H):
                mm = pe.matmul(self.out_ps[i % 2][0:n, t * D:(t + 1) * D], self.nodeT[:, i, t * P:t * P + n], weight[:, :],
                               start=True, stop=True)
            mm.then_inc(self.multiplied, 1)

    def turned_to_sbuf(self, act, m, at, scale_shift=None):
        for i in range(4):
            n = self.sh.rows(m * 2 + i // 2)
            act.wait_ge(self.turned, at + i + 1)
            act.wait_ge(self.multiplied, at + i - 3)
            out = self.nodeT[:, i, :].rearrange("p (t n) -> p t n", n=P)[:, :, 0:n]
            src = self.turn_ps[i % 2][:, :].rearrange("p (t n) -> p t n", n=P)[:, :, 0:n]
            if scale_shift is None:
                act.activation(out, src, ACT.Copy).then_inc(self.turn_read, 1)
            else:
                act.activation(out, src, ACT.Identity, bias=scale_shift[:, 1:2], scale=scale_shift[:, 0:1]).then_inc(self.turn_read, 1)

    def store_nodes(self, act, m, out):
        for b in range(2):
            c = m * 2 + b
            n = self.sh.rows(c)
            act.wait_ge(self.finished, 2 * m + b + 3)
            act.dma_start(node_rows(self.out_dram, c, self.sh), out[b][0:n, :, 0:D]).then_inc(self.stored[b], 16)

    def out_free(self, eng, m, b):
        eng.wait_ge(self.stored[b], 16 * m + 16)

    def all_stored(self, eng):
        for b in range(2):
            eng.wait_ge(self.stored[b], 16 * self.sh.node_pairs + 16)


class GcnEdges:

    def __init__(self, ph, weight, scale_shift):
        self.ph, self.weight, self.scale_shift = ph, weight, scale_shift
        self.w_all = [ph.sb(f"w_all{b}", [P, CH]) for b in range(2)]
        self.hT = ph.sb("hT", [P, 4, HALF])
        self.sums = ph.sb("sums", [P, 4, HALF])
        self.w_in = ph.pair("w_in")
        self.weighted, self.summed = ph.sem("weighted"), ph.sem("summed")

    def sync(self, sp, j, at, at_before, halves):
        for b in range(halves // 2):
            if at_before is not None:
                sp.wait_ge(self.weighted, 4 * j + 2 * b - 2)
                sp.sem_inc(self.ph.gate, 1)
            sp.dma_start(self.w_all[b][:, :], self.ph.dram["edge_w"][bass.ds(j * (2 * CH) + b * CH, CH)].partition_broadcast(P)).then_inc(self.w_in[b], 16)

    def tensor(self, pe, j, at, at_before, halves):
        self.ph.turn_edges(pe, j, at, halves)
        self.ph.multiply_edges(pe, at, halves, lambda i: pe.wait_ge(self.summed, 4 * j + i + 1),
                               lambda i: self.sums[:, i, :], self.weight)

    def scalar(self, act, j, at, at_before, halves):
        ph, ss = self.ph, self.scale_shift
        for i in range(halves):
            act.wait_ge(ph.turned, at + i + 1)
            if at_before is not None:
                act.wait_ge(self.weighted, 4 * j + i - 3)
                act.wait_ge(self.summed, 4 * j + i - 3)
            out, src = self.hT[:, i, :], ph.turn_ps[i % 2][:, :]
            if ss is None:
                act.activation(out, src, ACT.Copy).then_inc(ph.turn_read, 1)
            else:
                act.activation(out, src, ACT.Identity, bias=ss[:, 1:2], scale=ss[:, 0:1]).then_inc(ph.turn_read, 1)

    def vector(self, dve, j, at, at_before, halves):
        ph = self.ph
        for i in range(halves):
            dve.wait_ge(ph.turn_read, at + i + 1)
            if i % 2 == 0:
                dve.wait_ge(self.w_in[i // 2], 16 * j + 16)
            s = slice(i % 2 * HALF, (i % 2 + 1) * HALF)
            dve.tensor_tensor(self.hT[:, i, :], self.hT[:, i, :], self.w_all[i // 2][:, s], ALU.mult).then_inc(self.weighted, 1)
            dve.wait_ge(self.weighted, 4 * j + i + 1)
            if at_before is not None:
                dve.wait_ge(ph.multiplied, at + i - 3)
            start = scan_start(dve, self.summed, self.sums, j, i, at_before)
            dve.tensor_tensor_scan(self.sums[:, i, :], ph.k["same_run"][:, bass.ds(j * (4 * HALF) + i * HALF, HALF)], self.hT[:, i, :],
                                   start, ALU.mult, ALU.add).then_inc(self.summed, 1)
        for i in range(halves):
            dve.wait_ge(ph.multiplied, at + i + 1)
            ph.result_free(dve, j, i)
            dve.tensor_copy(ph.result_half(i), ph.out_half(i)).then_inc(ph.out_read, 1)


def scan_start(dve, done, states, j, i, at_before):
    if i == 0 and at_before is None:
        return 0.0
    dve.wait_ge(done, 4 * j + i)
    return states[:, (i - 1) % 4, HALF - 1:HALF]


class EveEdges:

    def __init__(self, ph, no):
        k = ph.k
        self.ph = ph
        self.wpool, self.weve, self.bpool = k[f"pool{no}"], k[f"eve{no}"], k[f"bpool{no}"]
        self.wconv, self.bconv, self.const = k[f"wconv{no}"], k[f"bconv{no}"], k[f"eve_c{no}"]
        self.xT = ph.sb("xT", [P, 2, HALF])
        self.begin = ph.sb("begin", [P, 2, HALF])
        self.pT, self.hi, self.lo, self.mix = (ph.sb(n, [P, 4, HALF]) for n in ("pT", "hi", "lo", "mix"))
        self.pool_ps = [ph.ps(f"pool{i}", [P, HALF]) for i in range(2)]
        self.pooled_ps, self.pooled, self.begun = ph.sem("pooled_ps"), ph.sem("pooled"), ph.sem("begun")
        self.hi_done, self.lo_done = ph.sem("hi_done"), ph.sem("lo_done")
        self.lo_scaled, self.mixed, self.mix_relu = ph.sem("lo_scaled"), ph.sem("mixed"), ph.sem("mix_relu")

    def sync(self, sp, j, at, at_before, halves):
        pass

    def tensor(self, pe, j, at, at_before, halves):
        ph = self.ph
        ph.turn_edges(pe, j, at, halves)
        for i in range(halves):
            pe.wait_ge(ph.turn_read, at + i + 1)
            if at_before is not None or i >= 2:
                pe.wait_ge(self.pooled, 4 * j + i - 1)
            pe.matmul(self.pool_ps[i % 2][:, :], self.wpool[:, :], self.xT[:, i % 2, :], start=True,
                      stop=True).then_inc(self.pooled_ps, 1)
        ph.multiply_edges(pe, at, halves, lambda i: pe.wait_ge(self.mix_relu, 4 * j + i + 1),
                          lambda i: self.mix[:, i, :], self.weve)

    def scalar(self, act, j, at, at_before, halves):
        ph = self.ph
        later = at_before is not None

        def begin(i):
            if later or i >= 2:
                act.wait_ge(self.lo_done, 4 * j + i - 1)
            act.sem_inc(ph.gate, 1)
            act.activation(self.begin[:, i % 2, :], ph.k["same_run"][:, bass.ds(j * (4 * HALF) + i * HALF, HALF)], ACT.Copy,
                           bias=BIG, scale=-BIG).then_inc(self.begun, 1)

        def copy(i):
            act.wait_ge(ph.turned, at + i + 1)
            if later or i >= 2:
                act.wait_ge(self.pooled_ps, 4 * j + i - 1)
            act.activation(self.xT[:, i % 2, :], ph.turn_ps[i % 2][:, :], ACT.Copy).then_inc(ph.turn_read, 1)

        def pool(i):
            act.wait_ge(self.pooled_ps, 4 * j + i + 1)
            if later:
                act.wait_ge(self.lo_done, 4 * j + i - 3)
                act.wait_ge(self.hi_done, 4 * j + i - 3)
            act.activation(self.pT[:, i, :], self.pool_ps[i % 2][:, :], ACT.Relu, bias=self.bpool[:, 0:1]).then_inc(self.pooled, 1)

        def scale(i):
            act.wait_ge(self.lo_done, 4 * j + i + 1)
            if later:
                act.wait_ge(ph.multiplied, at + i - 3)
            act.activation(self.mix[:, i, :], self.lo[:, i, :], ACT.Identity, bias=self.bconv[:, 0:1],
                           scale=self.wconv[:, 1:2]).then_inc(self.lo_scaled, 1)

        def relu(i):
            act.wait_ge(self.mixed, 4 * j + i + 1)
            act.activation(self.mix[:, i, :], self.mix[:, i, :], ACT.Relu).then_inc(self.mix_relu, 1)

        for i in range(halves):
            copy(i)
            if i < 2:
                begin(i)
        for i in range(halves):
            pool(i)
        for i in range(halves):
            scale(i)
            if i + 2 < halves:
                begin(i + 2)
        for i in range(halves):
            relu(i)

    def vector(self, dve, j, at, at_before, halves):
        ph = self.ph
        later = at_before is not None

        def scans(i):
            dve.wait_ge(self.pooled, 4 * j + i + 1)
            if later:
                dve.wait_ge(self.mixed, 4 * j + i - 3)
            start = scan_start(dve, self.hi_done, self.hi, j, i, at_before)
            dve.tensor_tensor_scan(self.hi[:, i, :], ph.k["same_run"][:, bass.ds(j * (4 * HALF) + i * HALF, HALF)], self.pT[:, i, :],
                                   start, ALU.mult, ALU.max).then_inc(self.hi_done, 1)
            if later:
                dve.wait_ge(self.lo_scaled, 4 * j + i - 3)
            dve.wait_ge(self.begun, 4 * j + i + 1)
            start = scan_start(dve, self.lo_done, self.lo, j, i, at_before)
            dve.tensor_tensor_scan(self.lo[:, i, :], self.begin[:, i % 2, :], self.pT[:, i, :], start, ALU.add,
                                   ALU.min).then_inc(self.lo_done, 1)

        def mix(i):
            dve.wait_ge(self.lo_scaled, 4 * j + i + 1)
            dve.wait_ge(self.hi_done, 4 * j + i + 1)
            dve.scalar_tensor_tensor(out=self.mix[:, i, :], in0=self.hi[:, i, :], scalar=self.wconv[:, 0:1], in1=self.mix[:, i, :],
                                     op0=ALU.mult, op1=ALU.add).then_inc(self.mixed, 1)

        for i in range(halves):
            scans(i)
        for i in range(halves):
            mix(i)
        for i in range(halves):
            dve.wait_ge(ph.multiplied, at + i + 1)
            ph.result_free(dve, j, i)
            dve.tensor_tensor(ph.result_half(i), ph.out_half(i), spread_slots(self.const[:, :], [P, H, D]),
                              ALU.subtract).then_inc(ph.out_read, 1)


class SageEdges:

    def __init__(self, ph, weight):
        self.ph, self.weight = ph, weight
        self.xT = ph.sb("xT", [P, 4, HALF])
        self.sums = ph.sb("sums", [P, 4, HALF])
        self.summed = ph.sem("summed")

    def sync(self, sp, j, at, at_before, halves):
        pass

    def tensor(self, pe, j, at, at_before, halves):
        self.ph.turn_edges(pe, j, at, halves)
        self.ph.multiply_edges(pe, at, halves, lambda i: pe.wait_ge(self.summed, 4 * j + i + 1),
                               lambda i: self.sums[:, i, :], self.weight)

    def scalar(self, act, j, at, at_before, halves):
        ph = self.ph
        for i in range(halves):
            act.wait_ge(ph.turned, at + i + 1)
            if at_before is not None:
                act.wait_ge(self.summed, 4 * j + i - 3)
            act.activation(self.xT[:, i, :], ph.turn_ps[i % 2][:, :], ACT.Copy).then_inc(ph.turn_read, 1)

    def vector(self, dve, j, at, at_before, halves):
        ph = self.ph
        for i in range(halves):
            dve.wait_ge(ph.turn_read, at + i + 1)
            if at_before is not None:
                dve.wait_ge(ph.multiplied, at + i - 3)
            start = scan_start(dve, self.summed, self.sums, j, i, at_before)
            dve.tensor_tensor_scan(self.sums[:, i, :], ph.k["same_run"][:, bass.ds(j * (4 * HALF) + i * HALF, HALF)], self.xT[:, i, :],
                                   start, ALU.mult, ALU.add).then_inc(self.summed, 1)
        for i in range(halves):
            dve.wait_ge(ph.multiplied, at + i + 1)
            ph.result_free(dve, j, i)
            counts = ph.k["inv_count"][:, bass.ds(j * (2 * T) + i * H, H)]
            dve.tensor_tensor(ph.result_half(i), ph.out_half(i), spread_features(counts, [P, H, D]), ALU.mult).then_inc(ph.out_read, 1)


class GcnNodes:

    def __init__(self, ph, no, scale_shift, next_scale_shift, as_rows):
        self.ph, self.no, self.scale_shift, self.next_ss, self.as_rows = ph, no, scale_shift, next_scale_shift, as_rows
        k = ph.k
        self.last = no == 2
        self.weight, self.bias = k[f"gcn{no}"], k[f"gcn_b{no}"]
        self.res = "x0" if "x0" in ph.streams else "y"
        if self.res == "y":
            ph.used["y"] = ph.sem("used_y")
        self.res_b = [ph.sb(f"res_b{b}", [P, T, D]) for b in range(2)]
        self.acc = [ph.sb(f"acc{b}", [P, T, D]) for b in range(2)]
        self.y1 = [ph.sb(f"y1{b}", [P, T, D + 1]) for b in range(2)]
        self.scales = [ph.sb(f"scales{b}", [P, 2, T]) for b in range(2)]
        self.small = ph.sb("small", [P, 8])
        self.diag = ph.sb("diag", [P, D])
        self.gram = ph.ps("gram", [P, 512])
        self.ones_set = ph.sem("ones_set")
        self.scales_set, self.added, self.acc_done = ph.sem("scales_set"), ph.sem("added"), ph.sem("acc_done")
        self.gram_done, self.bn_step, self.root_step = ph.sem("gram_done"), ph.sem("bn_step"), ph.sem("root_step")
        self.grants = [(ph.used[n], 2) for n in ph.used] + [(ph.finished, 2), (self.gram_done, 2)] + [(s, 16) for s in ph.stored]

    def tensor_start(self, pe):
        pe.wait_ge(self.ones_set, 2)
        zeros = self.ph.k["zeros"]
        pe.matmul(self.gram[:, 0:D + 1], zeros[:, 0:P], zeros[:, 0:D + 1], start=True, stop=False, skip_group_check=True)

    def tensor(self, pe, m, at, scattered):
        ph = self.ph
        ph.turn_nodes(pe, m, at)
        ph.multiply_nodes(pe, m, at, self.weight)
        for b in range(2):
            n = ph.sh.rows(m * 2 + b)
            pe.wait_ge(ph.finished, 2 * m + b + 3)
            for t in range(T):
                mm = pe.matmul(self.gram[:, 0:D + 1], self.y1[b][0:n, t, 0:D], self.y1[b][0:n, t, :], start=False, stop=False,
                               skip_group_check=True)
            mm.then_inc(self.gram_done, 1)

    def tensor_end(self, pe):
        if self.last:
            pe.wait_ge(self.bn_step, 12)
            for i in range(2):
                pe.matmul(self.ph.turn_ps[0][:, i * D:(i + 1) * D], self.as_rows[2][:, i, :], self.ph.k["ident"][:, :], start=True,
                          stop=True).then_inc(self.gram_done, 1)

    def scalar(self, act, m, at, scattered):
        ph = self.ph
        ph.turned_to_sbuf(act, m, at, self.scale_shift)
        if not self.last:
            for b in range(2):
                n = ph.sh.rows(m * 2 + b)
                act.wait_ge(self.acc_done, 2 * m + b + 1)
                ph.out_free(act, m, b)
                act.wait_ge(self.gram_done, 2 * m + b + 1)
                act.activation(self.y1[b][0:n, :, 0:D], self.acc[b][0:n, :, :], ACT.Relu).then_inc(ph.finished, 1)
        ph.store_nodes(act, m, self.y1)

    def vector(self, dve, m, at, scattered):
        ph, k = self.ph, self.ph.k
        for b in range(2):
            n = ph.sh.rows(m * 2 + b)
            s = slice(None)
            dve.tensor_copy(self.scales[b][:, :, :], k["dinvs"][:, bass.ds(m * 2 + b, 1), :, :].rearrange("p o a t -> p (o a) t")).then_inc(self.scales_set, 1)
            ph.have(dve, self.res, m, b)
            dve.tensor_tensor(self.res_b[b][0:n, :, :], ph.buf[self.res][b][0:n, :, :], spread_slots(self.bias[0:n, :], [n, T, D]),
                              ALU.add).then_inc(ph.used[self.res], 1)
        for b in range(2):
            n = ph.sh.rows(m * 2 + b)
            ph.have(dve, "sums", m, b)
            dve.wait_ge(ph.used[self.res], 2 * m + b + 3)
            dve.wait_ge(self.scales_set, 2 * m + b + 1)
            dve.wait_ge(ph.finished, 2 * m + b + 1)
            for t in range(T):
                ins = dve.scalar_tensor_tensor(out=self.res_b[b][0:n, t, :], in0=ph.buf["sums"][b][0:n, t, :],
                                               scalar=self.scales[b][0:n, 0, t:t + 1], in1=self.res_b[b][0:n, t, :],
                                               op0=ALU.mult, op1=ALU.add)
            ins.then_inc(ph.used["sums"], 1)
        for i in range(4):
            b = i // 2
            n = ph.sh.rows(m * 2 + b)
            dve.wait_ge(ph.multiplied, at + i + 1)
            if i % 2 == 0:
                dve.wait_ge(ph.used["sums"], 2 * m + b + 3)
                if self.last:
                    ph.out_free(dve, m, b)
                    dve.wait_ge(self.gram_done, 2 * m + b + 1)
            for t in range(H):
                tt = H * (i % 2) + t
                out = self.y1[b][0:n, tt, 0:D] if self.last else self.acc[b][0:n, tt, :]
                ins = dve.scalar_tensor_tensor(out=out, in0=ph.out_ps[i % 2][0:n, t * D:(t + 1) * D],
                                               scalar=self.scales[b][0:n, 1, tt:tt + 1], in1=self.res_b[b][0:n, tt, :],
                                               op0=ALU.mult, op1=ALU.add)
            ins.then_inc(ph.out_read, 1)
            if i % 2:
                dve.wait_ge(ph.out_read, at + i + 1)
                dve.sem_inc(ph.finished if self.last else self.acc_done, 1)

    def vector_start(self, dve):
        for b in range(2):
            dve.memset(self.y1[b][:, :, D:D + 1], 1.0).then_inc(self.ones_set, 1)

    def vector_end(self, dve):
        ph, k, sh = self.ph, self.ph.k, self.ph.sh
        gamma, beta = k[f"gamma{self.no}"], k[f"beta{self.no}"]
        mean, sq, var, m2, root = (self.small[:, i:i + 1] for i in range(5))
        ss, step, gram = self.next_ss, self.bn_step, self.gram
        dve.wait_ge(self.gram_done, sh.node_chunks + 2)
        dve.tensor_tensor(self.diag[:, :], gram[:, 0:D], k["ident"][:, :], ALU.mult).then_inc(step, 1)
        dve.tensor_scalar(mean, gram[:, D:D + 1], 1.0 / sh.n, None, ALU.mult).then_inc(step, 1)
        dve.wait_ge(step, 2)
        dve.tensor_reduce(sq, self.diag[:, :], AX.X, ALU.add).then_inc(step, 1)
        dve.tensor_tensor(m2, mean, mean, ALU.mult).then_inc(step, 1)
        dve.wait_ge(step, 4)
        dve.scalar_tensor_tensor(out=var, in0=sq, scalar=1.0 / sh.n, in1=m2, op0=ALU.mult, op1=ALU.subtract).then_inc(step, 1)
        dve.wait_ge(step, 5)
        dve.tensor_scalar(var, var, 0.0, BN_EPS, ALU.max, ALU.add).then_inc(step, 1)
        dve.wait_ge(step, 6)
        rsqrt(dve, root, var, sq, self.root_step, 0)
        dve.tensor_tensor(ss[:, 0:1], root, gamma[:, :], ALU.mult).then_inc(step, 1)
        dve.wait_ge(step, 7)
        dve.tensor_tensor(m2, mean, ss[:, 0:1], ALU.mult).then_inc(step, 1)
        dve.wait_ge(step, 8)
        dve.tensor_tensor(ss[:, 1:2], beta[:, :], m2, ALU.subtract).then_inc(step, 1)
        dve.wait_ge(step, 9)
        if self.last:
            for i in range(2):
                dve.tensor_scalar(self.as_rows[2][:, i, :], k["ones"][:, :], ss[:, i:i + 1], None, ALU.mult).then_inc(step, 1)
            dve.wait_ge(step, 11)
            dve.sem_inc(step, 1)
            dve.wait_ge(self.gram_done, sh.node_chunks + 4)
            for i in range(2):
                dve.tensor_copy(self.as_rows[i][:, :], ph.turn_ps[0][:, i * D:(i + 1) * D]).then_inc(step, 1)
            dve.wait_ge(step, 14)


class LinearNodes:

    def __init__(self, ph, weight, bias, finish):
        self.ph, self.weight, self.bias, self.finish = ph, weight, bias, finish
        self.z = [ph.sb(f"z{b}", [P, T, D]) for b in range(2)]
        self.o = [ph.sb(f"o{b}", [P, T, D]) for b in range(2)]
        self.gated = ph.sem("gated")
        if finish == "norm":
            self.ln = PairNorm(ph, "ln")
        self.grants = [(ph.used[n], 2) for n in ph.used] + [(ph.finished, 2)] + [(s, 16) for s in ph.stored]

    def tensor_start(self, pe):
        pass

    def tensor(self, pe, m, at, scattered):
        self.ph.turn_nodes(pe, m, at)
        self.ph.multiply_nodes(pe, m, at, self.weight)

    def tensor_end(self, pe):
        pass

    def vector_start(self, dve):
        pass

    def vector(self, dve, m, at, scattered):
        ph = self.ph
        per = 1 if self.finish != "norm" else 2
        for b in range(2):
            n = ph.sh.rows(m * 2 + b)
            z = self.z[b][0:n, :, :]
            ph.have(dve, "sums", m, b)
            dve.wait_ge(ph.finished, 2 * m + b + 1)
            dve.tensor_tensor(z, ph.buf["sums"][b][0:n, :, :], spread_slots(self.bias[0:n, :], [n, T, D]), ALU.add).then_inc(ph.used["sums"], 1)
        if self.finish == "norm":
            for b in range(2):
                n = ph.sh.rows(m * 2 + b)
                z = self.z[b][0:n, :, :]
                dve.wait_ge(ph.used["sums"], 2 * m + b + 3)
                ph.have(dve, "x0", m, b)
                dve.tensor_tensor(z, z, ph.buf["x0"][b][0:n, :, :], ALU.add).then_inc(ph.used["x0"], 1)
        last_used = ph.used["x0" if self.finish == "norm" else "sums"]
        for i in range(4):
            b = i // 2
            n = ph.sh.rows(m * 2 + b)
            z = self.z[b][0:n, H * (i % 2):H * (i % 2) + H, :]
            dve.wait_ge(ph.multiplied, at + i + 1)
            if i % 2 == 0:
                dve.wait_ge(last_used, 2 * m + b + 3)
            dve.tensor_tensor(z, ph.out_half(i, n), z, ALU.add).then_inc(ph.out_read, 1)
        if self.finish == "norm":
            dve.wait_ge(ph.out_read, at + 4)
            self.ln.on_vector(dve, self.z, [ph.sh.rows(m * 2 + b) for b in range(2)], m)
        if self.finish == "swish":
            for b in range(2):
                n = ph.sh.rows(m * 2 + b)
                dve.wait_ge(self.gated, 2 * m + b + 1)
                dve.tensor_tensor(self.o[b][0:n, :, :], self.o[b][0:n, :, :], self.z[b][0:n, :, :], ALU.mult).then_inc(ph.finished, 1)

    def vector_end(self, dve):
        pass

    def scalar(self, act, m, at, scattered):
        ph = self.ph
        ph.turned_to_sbuf(act, m, at)
        if self.finish == "norm":
            act.wait_ge(self.ln.ready, m + 1)
            for b in range(2):
                n = ph.sh.rows(m * 2 + b)
                ph.out_free(act, m, b)
                self.ln.apply(act, self.o[b], self.z[b], n, b).then_inc(ph.finished, 1)
        else:
            f, done = (ACT.Relu, ph.finished) if self.finish == "relu" else (ACT.Sigmoid, self.gated)
            for b in range(2):
                n = ph.sh.rows(m * 2 + b)
                act.wait_ge(ph.out_read, at + 2 * b + 2)
                ph.out_free(act, m, b)
                act.activation(self.o[b][0:n, :, :], self.z[b][0:n, :, :], f).then_inc(done, 1)
        ph.store_nodes(act, m, self.o)


def run_conv(nc, ph, edges, nodes):
    k, sh = ph.k, ph.sh
    with nc.Block() as block:
        @block.gpsimd
        def _(pool):
            ph.grant(pool, nodes.grants)
            ph.pool_program(pool)

        @block.sync
        def _(sp):
            merged_sweep(sp, k, sh, lambda *u: edges.sync(sp, *u), lambda *u: ph.load_nodes(sp, *u))

        @block.tensor
        def _(pe):
            nodes.tensor_start(pe)
            merged_sweep(pe, k, sh, lambda *u: edges.tensor(pe, *u), lambda *u: nodes.tensor(pe, *u))
            nodes.tensor_end(pe)

        @block.scalar
        def _(act):
            merged_sweep(act, k, sh, lambda *u: edges.scalar(act, *u), lambda *u: nodes.scalar(act, *u))
            ph.all_stored(act)

        @block.vector
        def _(dve):
            nodes.vector_start(dve)
            merged_sweep(dve, k, sh, lambda *u: edges.vector(dve, *u), lambda *u: nodes.vector(dve, *u))
            nodes.vector_end(dve)


def gcn_conv(nc, k, dram, sh, name, no, table, x0, out, scale_shift, next_scale_shift, as_rows=None):
    streams = {"y": table, "sums": dram["node_sums"]}
    if no:
        streams["x0"] = x0
    with Conv(nc, name, k, dram, sh, table, out, streams) as ph:
        run_conv(nc, ph, GcnEdges(ph, k[f"gcn{no}"], scale_shift), GcnNodes(ph, no, scale_shift, next_scale_shift, as_rows))


def eve_conv(nc, k, dram, sh, name, no, table, out, finish, x0=None):
    streams = {"y": table, "sums": dram["node_sums"]} | ({"x0": x0} if x0 is not None else {})
    with Conv(nc, name, k, dram, sh, table, out, streams) as ph:
        run_conv(nc, ph, EveEdges(ph, no), LinearNodes(ph, k[f"self{no}"], k[f"eve_b{no}"], finish))


def sage_conv(nc, k, dram, sh, name, no, table, out, finish, x0=None):
    streams = {"y": table, "sums": dram["node_sums"]} | ({"x0": x0} if x0 is not None else {})
    with Conv(nc, name, k, dram, sh, table, out, streams) as ph:
        run_conv(nc, ph, SageEdges(ph, k[f"sage_l{no}"]), LinearNodes(ph, k[f"sage_r{no}"], k[f"sage_b{no}"], finish))



def build(nc, a, out):
    sh = Shapes(a["x"].shape[0], a["src"].shape[0])
    nodes_padded = sh.node_chunks * CH

    def scratch(name, shape, dt=F32):
        return nc.dram_tensor(name, shape, dt, kind="Internal")

    dram = {"node_sums": scratch("node_sums", [nodes_padded, D]).ap(),
            "degree": scratch("degree", [nodes_padded, 1]).ap(),
            "dinv": scratch("dinv", [nodes_padded, 1]).ap(),
            "dst_padded": scratch("dst_padded", [sh.edges_padded + 1], I32).ap(),
            "run_sums": scratch("run_sums", [2, sh.edges_padded]).ap(),
            "edge_w": scratch("edge_w", [sh.edges_padded]).ap()}
    rows_a, rows_b, rows_c = (scratch(f"node_rows_{i}", [sh.n, D]).ap() for i in "abc")

    with ExitStack() as ctx:
        k = {}

        def keep(name, shape, dt=F32):
            k[name] = ctx.enter_context(nc.sbuf_tensor(f"k_{name}", shape, dt))

        for n in ("pool1", "self1", "eve1", "pool2", "self2", "eve2", "sage_l1", "sage_r1", "sage_l2", "sage_r2",
                  "gcn0", "gcn1", "gcn2", "gat_l", "gat_r", "gat_e", "ident", "ones", "head_att",
                  "gcn_b0", "gcn_b1", "gcn_b2", "eve_b1", "eve_b2", "eve_c1", "eve_c2", "sage_b1", "sage_b2",
                  "gat_b", "gat_gamma", "gat_beta", "bn_scale_row", "bn_shift_row"):
            keep(n, [P, D])
        keep("zeros", [P, D + 1])
        keep("bn_cols", [P, 2, D])
        for n in ("gamma0", "gamma1", "gamma2", "beta0", "beta1", "beta2", "bpool1", "bpool2", "bl", "br", "blr", "att",
                  "bconv1", "bconv2"):
            keep(n, [P, 1])
        for n in ("wconv1", "wconv2", "bn1", "bn2", "bn3"):
            keep(n, [P, 2])
        keep("first_dst", [1, 1], I32)
        keep("ready", [1, sh.edge_pairs + 1], I32)
        for n in ("src_idx", "place_idx", "dst_idx"):
            keep(n, [P, sh.edge_tiles], I32)
        for n in ("ew_tab", "inv_count"):
            keep(n, [P, sh.edge_tiles])
        keep("dinvs", [P, sh.node_chunks, 2, T])
        keep("same_run", [P, sh.edges_padded], U8)

        load_constants(nc, a, k)
        index_tables(nc, a, k, dram, sh)
        run_masks(nc, a, k, dram, sh)
        degrees(nc, k, dram, sh)

        x = a["x"]
        gcn_conv(nc, k, dram, sh, "m0", 0, x, x, rows_a, None, k["bn1"])
        gcn_conv(nc, k, dram, sh, "m1", 1, rows_a, x, rows_b, k["bn1"], k["bn2"])
        gcn_conv(nc, k, dram, sh, "m2", 2, rows_b, x, rows_a, k["bn2"], k["bn3"],
                 as_rows=(k["bn_scale_row"], k["bn_shift_row"], k["bn_cols"]))
        norm_nodes(nc, k, dram, sh, "n3", rows_a, x, rows_b, k["bn_scale_row"], k["bn_shift_row"])
        eve_conv(nc, k, dram, sh, "m4", 1, rows_b, rows_a, "relu")
        eve_conv(nc, k, dram, sh, "m5", 2, rows_a, rows_c, "norm", x0=rows_b)
        sage_conv(nc, k, dram, sh, "m6", 1, rows_c, rows_a, "swish")
        sage_conv(nc, k, dram, sh, "m7", 2, rows_a, rows_b, "norm", x0=rows_c)
        gat_edges(nc, a, k, dram, sh, "e8", rows_b)
        gat_nodes(nc, k, dram, sh, "n8", rows_b, out)


def kernel(**inputs):
    import numpy as _np
    import concourse.bacc as _bacc
    from concourse import mybir as _mybir
    from concourse.bass_utils import run_bass_kernel_spmd as _run

    nc = _bacc.Bacc("TRN2", target_bir_lowering=False, num_devices=1)
    arrays, args = {}, {}
    for name, value in inputs.items():
        v = _np.ascontiguousarray(value)
        arrays[f"in_{name}_dram"] = v
        args[name] = nc.dram_tensor(f"in_{name}_dram", v.shape, _mybir.dt.from_np(v.dtype), kind="ExternalInput").ap()
    out = nc.dram_tensor("out_0_dram", args["x"].shape, _mybir.dt.float32, kind="ExternalOutput").ap()
    build(nc, args, out)
    r = _run(nc, [arrays], core_ids=[0])
    return r.results[0]["out_0_dram"]
```

```python
from contextlib import ExitStack

import concourse.bass as bass
from concourse import mybir

F32 = mybir.dt.float32
I32 = mybir.dt.int32
U8 = mybir.dt.uint8
ALU = mybir.AluOpType
ACT = mybir.ActivationFunctionType
AX = mybir.AxisListType

P = 128
D = 128
T = 8
H = 4
CH = P * T
HALF = CH // 2
BN_EPS = 1e-5
LN_EPS = 1e-5
BIG = 3.0e38
FAR = 1 << 20


class Shapes:

    def __init__(self, n_nodes, n_edges):
        self.n, self.e = n_nodes, n_edges
        self.node_chunks = -(-n_nodes // CH)
        self.edge_chunks = -(-n_edges // CH)
        self.edge_tiles = self.edge_chunks * T
        self.edges_padded = self.edge_chunks * CH
        self.node_pairs, self.edge_pairs = self.node_chunks // 2, self.edge_chunks // 2
        assert self.node_chunks % 2 == 0 and self.edge_chunks % 2 == 1 and self.edge_pairs > 2
        self.last_nodes = n_nodes - (self.node_chunks - 1) * CH
        assert self.last_nodes % T == 0 and n_nodes < FAR
        self.last_rows = self.last_nodes // T

    def rows(self, c):
        return self.last_rows if isinstance(c, int) and c == self.node_chunks - 1 else P


def used_before(c, lag):
    return not isinstance(c, int) or c >= lag


def sweep(eng, chunks, full, step, peeled=1):
    for c in range(2 * peeled):
        step(c, c % 2, c // 2)
    with eng.Fori(peeled, full // 2) as q:
        step(2 * q, 0, q)
        step(2 * q + 1, 1, q)
    for c in range(full // 2 * 2, chunks):
        step(c, c % 2, c // 2)


def node_rows(t, c, sh):
    if isinstance(c, int):
        part = t[c * CH:c * CH + sh.rows(c) * T, :]
    else:
        part = t[bass.ds(c * CH, CH), :]
    return part.rearrange("(p j) f -> p j f", j=T)


class Phase:

    def __init__(self, nc, name):
        self.nc, self.name, self.stack, self.sems = nc, name, ExitStack(), []

    def __enter__(self):
        self.stack.__enter__()
        return self

    def __exit__(self, *a):
        self.nc.clear_and_free_semaphores(self.sems)
        self.nc.all_engine_barrier()
        return self.stack.__exit__(*a)

    def sb(self, name, shape, dt=F32):
        return self.stack.enter_context(self.nc.sbuf_tensor(f"{self.name}_{name}", shape, dt))

    def ps(self, name, shape):
        return self.stack.enter_context(self.nc.psum_tensor(f"{self.name}_{name}", shape, F32))

    def sem(self, name):
        s = self.nc.alloc_semaphore(f"{self.name}_{name}")
        self.sems.append(s)
        return s

    def pair(self, name):
        return [self.sem(f"{name}{b}") for b in range(2)]


def spread_slots(ap, shape):
    return ap.unsqueeze(1).to_broadcast(shape)


def spread_features(ap, shape):
    return ap.unsqueeze(2).to_broadcast(shape)


RSQRT_GUESS = 0x5F3759DF
RSQRT_STEPS = 11


def rsqrt(dve, y, x, tmp, step, base):
    yi = y.bitcast(I32)
    dve.tensor_scalar(yi, x.bitcast(I32), 1, None, ALU.logical_shift_right).then_inc(step, 1)
    dve.wait_ge(step, base + 1)
    dve.tensor_scalar(yi, yi, -1.0, float(RSQRT_GUESS), ALU.mult, ALU.add).then_inc(step, 1)
    for i in range(3):
        dve.wait_ge(step, base + 2 + 3 * i)
        dve.tensor_tensor(tmp, y, y, ALU.mult).then_inc(step, 1)
        dve.wait_ge(step, base + 3 + 3 * i)
        dve.scalar_tensor_tensor(out=tmp, in0=tmp, scalar=-0.5, in1=x, op0=ALU.mult, op1=ALU.mult).then_inc(step, 1)
        dve.wait_ge(step, base + 4 + 3 * i)
        dve.scalar_tensor_tensor(out=y, in0=tmp, scalar=1.5, in1=y, op0=ALU.add, op1=ALU.mult).then_inc(step, 1)
    dve.wait_ge(step, base + RSQRT_STEPS)



def load_constants(nc, a, k):
    turned = {"pool1": a["L1_gnn_wpool1"], "self1": a["L1_gnn_wself1"], "eve1": a["L1_gnn_weve1"],
              "pool2": a["L1_gnn_wpool2"], "self2": a["L1_gnn_wself2"], "eve2": a["L1_gnn_weve2"],
              "sage_l1": a["L2_gnn_W1_l"], "sage_r1": a["L2_gnn_W1_r"],
              "sage_l2": a["L2_gnn_W2_l"], "sage_r2": a["L2_gnn_W2_r"]}
    plain = {"gcn0": a["L0_gnn_Ws"][0], "gcn1": a["L0_gnn_Ws"][1], "gcn2": a["L0_gnn_Ws"][2],
             "gat_l": a["L3_gnn_Wl"], "gat_r": a["L3_gnn_Wr"], "gat_e": a["L3_gnn_We"]}
    columns = {"gamma0": a["L0_gnn_gammas"][0], "gamma1": a["L0_gnn_gammas"][1], "gamma2": a["L0_gnn_gammas"][2],
               "beta0": a["L0_gnn_betas"][0], "beta1": a["L0_gnn_betas"][1], "beta2": a["L0_gnn_betas"][2],
               "bpool1": a["L1_gnn_bpool1"], "bpool2": a["L1_gnn_bpool2"],
               "bl": a["L3_gnn_bl"], "br": a["L3_gnn_br"],
               "att": a["L3_gnn_att"].rearrange("h c -> (h c)")}
    rows = {"gcn_b0": a["L0_gnn_bs"][0], "gcn_b1": a["L0_gnn_bs"][1], "gcn_b2": a["L0_gnn_bs"][2],
            "eve_b1": a["L1_gnn_bias1"], "eve_b2": a["L1_gnn_bias2"],
            "sage_b1": a["L2_gnn_b1"], "sage_b2": a["L2_gnn_b2"],
            "gat_b": a["L3_gnn_bias"], "gat_gamma": a["L3_gnn_gamma"], "gat_beta": a["L3_gnn_beta"]}
    heads, width = a["L3_gnn_att"].shape
    with Phase(nc, "const") as ph:
        raw = {n: ph.sb(f"raw_{n}", [P, D]) for n in turned}
        relu_b = ph.sb("relu_b", [P, 2])
        relu_bm = ph.sb("relu_bm", [P, 2, P])
        att_cols = ph.sb("att_cols", [P, D])
        psum = [ph.ps(f"turn{i}", [P, 512]) for i in range(2)]
        eve_ps = ph.ps("eve", [P, 512])
        loaded = ph.sem("loaded")
        cleared = ph.sem("cleared")
        ident_made = ph.sem("ident_made")
        turned_ps = ph.sem("turned_ps")
        turned_sb = ph.sem("turned_sb")
        relu_done = ph.sem("relu_done")
        eve_const = ph.sem("eve_const")
        misc = ph.sem("misc")
        loads = [(raw[n][:, :], w) for n, w in turned.items()]
        loads += [(k[n][0:w.shape[0], :], w) for n, w in plain.items()]
        loads += [(k[n][:, 0:1], w.rearrange("(f o) -> f o", o=1)) for n, w in columns.items()]
        loads += [(k[n][:, :], w.partition_broadcast(P)) for n, w in rows.items()]
        for i in (1, 2):
            loads += [(k[f"wconv{i}"][:, :], a[f"L1_gnn_wconv{i}"].partition_broadcast(P)),
                      (k[f"bconv{i}"][:, :], a[f"L1_gnn_bconv{i}"].partition_broadcast(P))]
        with nc.Block() as block:
            @block.sync
            def _(sp):
                for out, src in loads:
                    sp.dma_start(out, src).then_inc(loaded, 16)

            @block.gpsimd
            def _(pool):
                pool.memset(k["ident"][:, :], 0.0).then_inc(cleared, 1)
                pool.memset(k["head_att"][:, :], 0.0).then_inc(cleared, 1)
                pool.memset(k["ones"][:, :], 1.0).then_inc(cleared, 1)
                pool.memset(k["zeros"][:, :], 0.0).then_inc(cleared, 1)
                pool.memset(k["ln_eps"][:, :], LN_EPS).then_inc(cleared, 1)
                pool.wait_ge(cleared, 5)
                pool.affine_select(out=k["ident"][:, :], in_=k["ident"][:, :], compare_op=ALU.not_equal,
                                   fill=1.0, base=0, pattern=[[-1, P]], channel_multiplier=1).then_inc(ident_made, 1)

            @block.tensor
            def _(pe):
                pe.wait_ge(loaded, 16 * len(loads))
                pe.wait_ge(ident_made, 1)
                for i, n in enumerate(turned):
                    if i >= 2:
                        pe.wait_ge(turned_sb, i - 1)
                    pe.transpose(psum[i % 2][:, 0:D], raw[n][:, :], k["ident"][:, :]).then_inc(turned_ps, 1)
                pe.wait_ge(relu_done, 2)
                pe.wait_ge(turned_sb, len(turned))
                for i in (1, 2):
                    pe.matmul(eve_ps[:, (i - 1) * D:i * D], relu_bm[:, i - 1, :], k[f"eve{i}"][:, :],
                              start=True, stop=True).then_inc(eve_const, 1)

            @block.vector
            def _(dve):
                for i, n in enumerate(turned):
                    dve.wait_ge(turned_ps, i + 1)
                    dve.tensor_copy(k[n][:, :], psum[i % 2][:, 0:D]).then_inc(turned_sb, 1)
                for i in (1, 2):
                    dve.tensor_scalar(relu_b[:, i - 1:i], k[f"bconv{i}"][:, :], 0.0, None, ALU.max).then_inc(misc, 1)
                dve.wait_ge(misc, 2)
                for i in (1, 2):
                    dve.tensor_scalar(relu_bm[:, i - 1, :], k["ones"][:, :], relu_b[:, i - 1:i], None,
                                      ALU.mult).then_inc(relu_done, 1)
                dve.wait_ge(eve_const, 2)
                for i in (1, 2):
                    dve.tensor_copy(k[f"eve_c{i}"][:, :], eve_ps[:, (i - 1) * D:i * D]).then_inc(misc, 1)
                dve.wait_ge(misc, 4)
                for i in (1, 2):
                    dve.tensor_tensor(k[f"eve_b{i}"][:, :], k[f"eve_b{i}"][:, :], k[f"eve_c{i}"][:, :],
                                      ALU.add).then_inc(misc, 1)
                dve.tensor_tensor(k["blr"][:, :], k["bl"][:, :], k["br"][:, :], ALU.add).then_inc(misc, 1)
                dve.tensor_scalar(att_cols[:, :], k["ones"][:, :], k["att"][:, 0:1], None, ALU.mult).then_inc(misc, 1)
                dve.wait_ge(misc, 8)
                for h in range(heads):
                    s = slice(h * width, (h + 1) * width)
                    dve.tensor_copy(k["head_att"][s, s], att_cols[s, s]).then_inc(misc, 1)
                dve.wait_ge(misc, 8 + heads)


def edge_rows_load(eng, out, src, count, sem):
    groups = count // (P * P)
    whole = count // P
    eng.dma_start(out[:, 0:groups, :], src[0:groups * P * P].rearrange("(g t e) -> t g e", t=P, e=P)).then_inc(sem, 16)
    n = 16
    left = whole - groups * P
    if left:
        eng.dma_start(out[0:left, groups, :], src[groups * P * P:whole * P].rearrange("(t e) -> t e", e=P)).then_inc(sem, 16)
        n += 16
    rest = count - whole * P
    if rest:
        eng.dma_start(out[left:left + 1, groups, 0:rest], src[whole * P:count].rearrange("(t e) -> t e", t=1)).then_inc(sem, 16)
        n += 16
    return n


def index_tables(nc, a, k, dram, sh):
    groups = -(-sh.edge_tiles // P)
    tail = sh.edge_tiles - (groups - 1) * P
    with Phase(nc, "index") as ph:
        ints = {n: ph.sb(f"int_{n}", [P, groups, P], I32) for n in ("src", "dst", "next")}
        flts = {n: ph.sb(f"flt_{n}", [P, groups, P]) for n in ("src", "dst", "next", "ew", "place")}
        same = ph.sb("same", [P, groups, P])
        zero = ph.sb("zero", [P, sh.node_chunks * T])
        edge_pad = ph.sb("edge_pad", [1, CH], I32)
        bank = [ph.ps(f"bank{i}", [P, 512]) for i in range(4)]
        filled = ph.sem("filled")
        loaded = ph.sem("loaded")
        zeroed = ph.sem("zeroed")
        padded = ph.sem("padded")
        calc = ph.sem("calc")
        in_psum = ph.sem("in_psum")
        out_sb = ph.sem("out_sb")
        n_loaded = []
        with nc.Block() as block:
            @block.gpsimd
            def _(pool):
                pool.memset(ints["src"][:, :, :], 0).then_inc(filled, 1)
                pool.memset(ints["dst"][:, :, :], FAR).then_inc(filled, 1)
                pool.memset(ints["next"][:, :, :], 2 * FAR).then_inc(filled, 1)
                pool.memset(flts["ew"][:, :, :], 0.0).then_inc(filled, 1)
                pool.memset(edge_pad[:, :], FAR).then_inc(filled, 1)
                pool.memset(k["first_dst"][:, :], -1).then_inc(filled, 1)
                pool.memset(zero[:, :], 0.0).then_inc(filled, 1)
                pool.memset(k["ready"][:, :], 0).then_inc(filled, 1)

            @block.sync
            def _(sp):
                sp.wait_ge(filled, 8)
                n = edge_rows_load(sp, ints["src"], a["src"], sh.e, loaded)
                n += edge_rows_load(sp, ints["dst"], a["dst"], sh.e, loaded)
                n += edge_rows_load(sp, ints["next"], a["dst"][1:sh.e], sh.e - 1, loaded)
                n += edge_rows_load(sp, flts["ew"], a["edge_weight"], sh.e, loaded)
                firsts = a["dst"][0:sh.edge_pairs * 2 * CH].rearrange("(o j e) -> o j e", o=1, e=2 * CH)[:, 1:, 0:1]
                sp.dma_start(k["ready"][0:1, 2:sh.edge_pairs + 1].unsqueeze(2), firsts, allow_slow_non_contiguous=True).then_inc(loaded, 16)
                n += 16
                n_loaded.append(n)
                dp = dram["dst_padded"]
                sp.dma_start(dp[0:1], k["first_dst"][0:1, 0:1]).then_inc(padded, 16)
                sp.dma_start(dp[1:sh.e + 1].rearrange("(a b) -> a b", a=16), a["dst"].rearrange("(a b) -> a b", a=16)).then_inc(padded, 16)
                rest = sh.edges_padded - sh.e
                sp.dma_start(dp[sh.e + 1:sh.e + 1 + rest], edge_pad[0:1, 0:rest]).then_inc(padded, 16)
                sp.dma_start(dram["degree"].rearrange("(p c) o -> p (c o)", p=P), zero[:, :]).then_inc(zeroed, 16)
                sp.wait_ge(zeroed, 16)
                sp.wait_ge(padded, 48)

            order = [("src", "src_idx"), ("place", "place_idx"), ("dst", "dst_idx"), ("ew", "ew_tab")]

            @block.vector
            def _(dve):
                dve.wait_ge(loaded, n_loaded[0])
                for n in ("src", "dst", "next"):
                    dve.tensor_copy(flts[n][:, :, :], ints[n][:, :, :]).then_inc(calc, 1)
                dve.wait_ge(calc, 3)
                dve.tensor_tensor(same[:, :, :], flts["dst"][:, :, :], flts["next"][:, :, :], ALU.is_equal).then_inc(calc, 1)
                dve.wait_ge(calc, 4)
                dve.scalar_tensor_tensor(out=flts["place"][:, :, :], in0=same[:, :, :], scalar=float(FAR),
                                         in1=flts["dst"][:, :, :], op0=ALU.mult, op1=ALU.add).then_inc(calc, 1)
                dve.wait_ge(calc, 5)
                dve.tensor_scalar(flts["dst"][:, :, :], flts["dst"][:, :, :], float(sh.n - 1), None, ALU.min).then_inc(calc, 1)
                for i, (n, out) in enumerate(order):
                    dve.wait_ge(in_psum, i + 1)
                    dve.tensor_copy(k[out][:, :], bank[i][:, 0:sh.edge_tiles]).then_inc(out_sb, 1)
                dve.tensor_scalar(k["ready"][:, :], k["ready"][:, :], (2 * CH).bit_length() - 1, None,
                                  ALU.arith_shift_right).then_inc(out_sb, 1)
                dve.wait_ge(out_sb, len(order) + 1)

            @block.tensor
            def _(pe):
                pe.wait_ge(calc, 6)
                for i, (n, _) in enumerate(order):
                    for g in range(groups):
                        rows = P if g < groups - 1 else tail
                        mm = pe.transpose(bank[i][:, g * P:g * P + rows], flts[n][0:rows, g, :], k["ident"][0:rows, 0:rows])
                    mm.then_inc(in_psum, 1)


def degrees(nc, a, k, dram, sh):
    groups = -(-sh.edge_tiles // P)
    tail = sh.edge_tiles - (groups - 1) * P
    rows_of = [P] * (groups - 1) + [tail]
    real = sh.e - (sh.edge_chunks - 1) * CH
    in_slot = [(sh.edge_chunks + 1) // 2, sh.edge_chunks // 2]
    with Phase(nc, "deg") as ph:
        dst_all = [ph.sb(f"dst_all{b}", [P, CH + 1], I32) for b in range(2)]
        pairs = [ph.sb(f"pairs{b}", [2, CH]) for b in range(2)]
        sums = [ph.sb(f"sums{b}", [2, CH]) for b in range(2)]
        zero = ph.sb("zero", [P, T, D])
        w_tab = ph.sb("w_tab", [P, sh.edge_tiles])
        w_rows = ph.sb("w_rows", [P, groups, P])
        pos = ph.sb("pos", [P, sh.node_chunks * T])
        root = ph.sb("root", [P, sh.node_chunks * T])
        k["dinv"] = ph.sb("dinv", [P, sh.node_chunks * T])
        lifted = ph.sb("lifted", [P, sh.node_chunks * T])
        root_tmp = ph.sb("root_tmp", [P, sh.node_chunks * T])
        root_step = ph.sem("root_step")
        deg_slot = [ph.sb(f"deg_slot{b}", [P, T]) for b in range(2)]
        place_slot = [ph.sb(f"place_slot{b}", [P, T], I32) for b in range(2)]
        src_slot = [ph.sb(f"src_slot{b}", [P, T], I32) for b in range(2)]
        got = [ph.sb(f"got{b}", [P, T]) for b in range(2)]
        sums_bank = [ph.ps(f"sums_bank{b}", [P, T, 2]) for b in range(2)]
        w_bank = ph.ps("w_bank", [P, 512])
        dst_in, ew_in, scattered, gathered = ph.pair("dst_in"), ph.pair("ew_in"), ph.pair("scattered"), ph.pair("gathered")
        constants_set = ph.sem("constants_set")
        masked, summed = ph.sem("masked"), ph.sem("summed")
        turned, deg_ready, counts_ready = ph.sem("turned"), ph.sem("deg_ready"), ph.sem("counts_ready")
        place_set, src_set = ph.sem("place_set"), ph.sem("src_set")
        gate = ph.sem("gate")
        zeroed = ph.sem("zeroed")
        deg_in = ph.sem("deg_in")
        dinv_calc = ph.sem("dinv_calc")
        dinv_out = ph.sem("dinv_out")
        tabs = ph.sem("tabs")
        weighted = ph.sem("weighted")
        w_turned = ph.sem("w_turned")
        w_in_rows = ph.sem("w_in_rows")
        w_out = ph.sem("w_out")
        with nc.Block() as block:
            @block.sync
            def _(sp):
                sp.wait_ge(constants_set, 3)

                def step(c, b, q):
                    if used_before(c, 2):
                        sp.wait_ge(masked, c - 1)
                    at = c * CH
                    sp.dma_start(dst_all[b][:, :], dram["dst_padded"][bass.ds(at, CH + 1)].partition_broadcast(P)).then_inc(dst_in[b], 16)
                    if used_before(c, 2):
                        sp.wait_ge(summed, c - 1)
                    n = real if isinstance(c, int) and c == sh.edge_chunks - 1 else CH
                    sp.dma_start(pairs[b][0:1, 0:n], a["edge_weight"][bass.ds(at, n)].partition_broadcast(1)).then_inc(ew_in[b], 16)

                sweep(sp, sh.edge_chunks, sh.edge_chunks - 1, step)
                for b in range(2):
                    sp.wait_ge(scattered[b], 16 * T * in_slot[b])
                sp.dma_start(k["dinv"][:, :].rearrange("p (c j) -> p c j", j=T),
                             dram["degree"].rearrange("(c p j) o -> p c (j o)", p=P, j=T)).then_inc(deg_in, 16)
                sp.wait_ge(dinv_calc, 4)
                sp.dma_start(dram["dinv"].rearrange("(c p j) o -> p c (j o)", p=P, j=T),
                             k["dinv"][:, :].rearrange("p (c j) -> p c j", j=T)).then_inc(dinv_out, 16)
                sp.wait_ge(w_in_rows, groups)
                wr = dram["edge_w"]
                sp.dma_start(wr[0:(groups - 1) * P * P].rearrange("(g t e) -> t g e", t=P, e=P),
                             w_rows[:, 0:groups - 1, :]).then_inc(w_out, 16)
                sp.dma_start(wr[(groups - 1) * P * P:sh.edges_padded].rearrange("(t e) -> t e", e=P),
                             w_rows[0:tail, groups - 1, :]).then_inc(w_out, 16)
                sp.wait_ge(w_out, 32)

            @block.scalar
            def _(act):
                act.wait_ge(constants_set, 3)
                with act.Fori(0, sh.node_chunks) as c:
                    act.dma_start(dram["node_sums"][bass.ds(c * CH, CH), :].rearrange("(p j) f -> p j f", j=T),
                                  zero[:, :, :]).then_inc(zeroed, 16)
                act.wait_ge(zeroed, 16 * sh.node_chunks)

            @block.tensor
            def _(pe):
                def step(c, b, q):
                    pe.wait_ge(summed, c + 1)
                    pe.sem_inc(gate, 1)
                    if used_before(c, 2):
                        pe.wait_ge(counts_ready, c - 1)
                        pe.sem_inc(gate, 1)
                    for t in range(T):
                        mm = pe.transpose(sums_bank[b][:, t, :], sums[b][:, t * P:(t + 1) * P], k["ident"][0:2, 0:2])
                    mm.then_inc(turned, 1)

                sweep(pe, sh.edge_chunks, sh.edge_chunks - 1, step)
                pe.wait_ge(weighted, sh.edge_chunks)
                for g, r in enumerate(rows_of):
                    if g:
                        pe.wait_ge(w_in_rows, g)
                    pe.transpose(w_bank[0:r, 0:P], w_tab[:, g * P:g * P + r], k["ident"][:, :]).then_inc(w_turned, 1)

            @block.vector
            def _(dve):
                for b in range(2):
                    dve.memset(pairs[b][:, :], 1.0).then_inc(constants_set, 1)
                dve.memset(zero[:, :, :], 0.0).then_inc(constants_set, 1)

                def step(c, b, q):
                    dve.wait_ge(dst_in[b], 16 * q + 16)
                    dve.tensor_tensor(k["same_run"][:, bass.ds(c * CH, CH)], dst_all[b][:, 1:CH + 1], dst_all[b][:, 0:CH],
                                      ALU.is_equal).then_inc(masked, 1)
                    dve.wait_ge(masked, c + 1)
                    dve.wait_ge(ew_in[b], 16 * q + 16)
                    if used_before(c, 1):
                        dve.wait_ge(summed, c)
                    if used_before(c, 2):
                        dve.wait_ge(turned, c - 1)
                    start = sums[1 - b][:, CH - 1:CH] if used_before(c, 1) else 0.0
                    dve.tensor_tensor_scan(sums[b][:, :], k["same_run"][0:2, bass.ds(c * CH, CH)], pairs[b][:, :],
                                           start, ALU.mult, ALU.add).then_inc(summed, 1)
                    if used_before(c, 2):
                        dve.wait_ge(scattered[b], 16 * T * q)
                    dve.wait_ge(turned, c + 1)
                    dve.tensor_copy(deg_slot[b][:, :], sums_bank[b][:, :, 0]).then_inc(deg_ready, 1)
                    dve.tensor_copy(k["inv_count"][:, bass.ds(c * T, T)], sums_bank[b][:, :, 1]).then_inc(counts_ready, 1)

                sweep(dve, sh.edge_chunks, sh.edge_chunks - 1, step)
                dve.wait_ge(counts_ready, sh.edge_chunks)
                dve.reciprocal(k["inv_count"][:, :], k["inv_count"][:, :]).then_inc(tabs, 1)
                dve.wait_ge(deg_in, 16)
                dve.tensor_scalar(k["dinv"][:, :], k["dinv"][:, :], 1.0, None, ALU.add).then_inc(dinv_calc, 1)
                dve.wait_ge(dinv_calc, 1)
                dve.tensor_scalar(pos[:, :], k["dinv"][:, :], 0.0, None, ALU.is_gt).then_inc(dinv_calc, 1)
                dve.tensor_scalar(lifted[:, :], k["dinv"][:, :], 1e-12, None, ALU.max).then_inc(dinv_calc, 1)
                dve.wait_ge(dinv_calc, 3)
                rsqrt(dve, root[:, :], lifted[:, :], root_tmp[:, :], root_step, 0)
                dve.tensor_tensor(k["dinv"][:, :], root[:, :], pos[:, :], ALU.mult).then_inc(dinv_calc, 1)
                dve.wait_ge(dinv_calc, 4)
                dv = k["dinv"][:, :].rearrange("p (c t) -> p c t", t=T)
                dve.tensor_copy(k["dinvs"][:, :, 0, :], dv).then_inc(tabs, 1)
                dve.tensor_tensor(k["dinvs"][:, :, 1, :], dv, dv, ALU.mult).then_inc(tabs, 1)

                def weigh(c, b, q):
                    dve.wait_ge(gathered[b], 16 * T * q + 16 * T)
                    dve.tensor_tensor(w_tab[:, bass.ds(c * T, T)], got[b][:, :], k["ew_tab"][:, bass.ds(c * T, T)],
                                      ALU.mult).then_inc(weighted, 1)

                sweep(dve, sh.edge_chunks, sh.edge_chunks - 1, weigh)
                for g, r in enumerate(rows_of):
                    dve.wait_ge(w_turned, g + 1)
                    dve.tensor_copy(w_rows[0:r, g, :], w_bank[0:r, 0:P]).then_inc(w_in_rows, 1)
                dve.wait_ge(w_in_rows, groups)
                dve.wait_ge(tabs, 3)

            @block.gpsimd
            def _(pool):
                nodes_end = pool.to_reg(sh.n - 1)

                def scatter(c, b, q):
                    if used_before(c, 2):
                        pool.wait_ge(scattered[b], 16 * T * q)
                        pool.sem_inc(gate, 1)
                    pool.tensor_copy(place_slot[b][:, :], k["place_idx"][:, bass.ds(c * T, T)]).then_inc(place_set, 1)
                    pool.wait_ge(deg_ready, c + 1)
                    pool.sem_inc(gate, 1)
                    pool.wait_ge(place_set, c + 1)
                    pool.sem_inc(gate, 1)
                    for t in range(T):
                        pool.indirect_dma_start(dram["degree"][:, :], bass.IndirectOffsetOnAxis(place_slot[b][:, t:t + 1], 0),
                                                deg_slot[b][:, t:t + 1], None, bounds_check=nodes_end,
                                                oob_is_err=False).then_inc(scattered[b], 16)

                sweep(pool, sh.edge_chunks, sh.edge_chunks - 1, scatter)
                pool.wait_ge(dinv_out, 16)

                def gather(c, b, q):
                    if used_before(c, 2):
                        pool.wait_ge(weighted, c - 1)
                        pool.sem_inc(gate, 1)
                    pool.tensor_copy(src_slot[b][:, :], k["src_idx"][:, bass.ds(c * T, T)]).then_inc(src_set, 1)
                    pool.wait_ge(src_set, c + 1)
                    pool.sem_inc(gate, 1)
                    for t in range(T):
                        pool.indirect_dma_start(got[b][:, t:t + 1], None, dram["dinv"][:, :],
                                                bass.IndirectOffsetOnAxis(src_slot[b][:, t:t + 1], 0)).then_inc(gathered[b], 16)

                sweep(pool, sh.edge_chunks, sh.edge_chunks - 1, gather)



class EdgePhase(Phase):

    def __init__(self, nc, name, k, dram, sh, table, both_ends=False):
        super().__init__(nc, name)
        self.k, self.dram, self.sh, self.table = k, dram, sh, table
        self.ends = [("src", "src_idx")] + ([("dst", "dst_idx")] if both_ends else [])

    def __enter__(self):
        super().__enter__()
        self.rows = {n: [self.sb(f"rows_{n}{b}", [P, T, D]) for b in range(2)] for n, _ in self.ends}
        self.idx = {n: [self.sb(f"idx_{n}{b}", [P, T], I32) for b in range(2)] for n, _ in self.ends}
        self.place = [self.sb(f"place{b}", [P, T], I32) for b in range(2)]
        self.result = [self.sb(f"result{b}", [P, T, D]) for b in range(2)]
        self.gate = self.sem("gate")
        self.slots = self.sem("slots")
        self.place_set = self.sem("place_set")
        self.gathered = self.pair("gathered")
        self.turned = self.sem("turned")
        self.result_ready = self.sem("result_ready")
        self.scattered = self.pair("scattered")
        return self

    def pool_program(self, pool):
        sh, k, n_ends = self.sh, self.k, len(self.ends)
        nodes_end = pool.to_reg(sh.n - 1)

        def gather(c, b, q):
            if used_before(c, 2):
                pool.wait_ge(self.turned, 2 * c - 2)
                pool.sem_inc(self.gate, 1)
            for n, tab in self.ends:
                pool.tensor_copy(self.idx[n][b][:, :], k[tab][:, bass.ds(c * T, T)]).then_inc(self.slots, 1)
            pool.wait_ge(self.slots, n_ends * c + n_ends)
            pool.sem_inc(self.gate, 1)
            for t in range(T):
                for n, _ in self.ends:
                    pool.indirect_dma_start(self.rows[n][b][:, t, :], None, self.table[:, :],
                                            bass.IndirectOffsetOnAxis(self.idx[n][b][:, t:t + 1], 0)).then_inc(self.gathered[b], 16)

        def scatter(c, b):
            pool.wait_ge(self.result_ready, 2 * c + 2)
            pool.sem_inc(self.gate, 1)
            pool.tensor_copy(self.place[b][:, :], k["place_idx"][:, bass.ds(c * T, T)]).then_inc(self.place_set, 1)
            pool.wait_ge(self.place_set, c + 1)
            pool.sem_inc(self.gate, 1)
            for t in range(T):
                pool.indirect_dma_start(self.dram["node_sums"][:, :], bass.IndirectOffsetOnAxis(self.place[b][:, t:t + 1], 0),
                                        self.result[b][:, t, :], None, bounds_check=nodes_end,
                                        oob_is_err=False).then_inc(self.scattered[b], 16)

        def step(c, b, q):
            gather(c, b, q)
            if used_before(c, 2):
                scatter(c - 2, b)

        sweep(pool, sh.edge_chunks, sh.edge_chunks - 1, step)
        for c in (sh.edge_chunks - 2, sh.edge_chunks - 1):
            scatter(c, c % 2)
        pool.wait_ge(self.scattered[0], 16 * T * ((sh.edge_chunks + 1) // 2))
        pool.wait_ge(self.scattered[1], 16 * T * (sh.edge_chunks // 2))

    def rows_landed(self, eng, b, q):
        n = 16 * T * len(self.ends)
        eng.wait_ge(self.gathered[b], n * q + n)

    def result_free(self, eng, c, b, q):
        if used_before(c, 2):
            eng.wait_ge(self.scattered[b], 16 * T * q)


def half_no(c, h):
    return 2 * c + (h + 1)


def tiles_of(h):
    return range(H * h, H * h + H)


def gat_edges(nc, a, k, dram, sh, name, table):
    n_attr = a["edge_attr_16"].shape[1]
    heads, width = a["L3_gnn_att"].shape
    real = sh.e - (sh.edge_chunks - 1) * CH
    last_chunk = (sh.edge_chunks - 1, (sh.edge_chunks - 1) % 2, (sh.edge_chunks - 1) // 2)

    def chunk_before(c, b, q):
        return c - 1, 1 - b, q - (1 - b)

    with EdgePhase(nc, name, k, dram, sh, table, both_ends=True) as ph:
        attr = [ph.sb(f"attr{b}", [P, T, n_attr]) for b in range(2)]
        sT = [ph.sb(f"sT{h}", [P, HALF]) for h in range(2)]
        dT = [ph.sb(f"dT{h}", [P, HALF]) for h in range(2)]
        eT = [ph.sb(f"eT{h}", [n_attr, HALF]) for h in range(2)]
        val = [ph.sb(f"val{h}", [P, HALF]) for h in range(2)]
        pre = [ph.sb(f"pre{h}", [P, HALF]) for h in range(2)]
        top = [ph.sb(f"top{h}", [P, HALF + 1]) for h in range(2)]
        begin = [ph.sb(f"begin{h}", [P, HALF]) for h in range(2)]
        fall = [ph.sb(f"fall{h}", [P, HALF]) for h in range(2)]
        prob = [ph.sb(f"prob{h}", [P, HALF]) for h in range(2)]
        num = [ph.sb(f"num{h}", [P, HALF]) for h in range(2)]
        den = [ph.sb(f"den{h}", [P, HALF]) for h in range(2)]
        inv_den = [ph.sb(f"inv_den{h}", [P, H, heads]) for h in range(2)]
        src_ps = ph.ps("src", [P, HALF])
        dst_ps = ph.ps("dst", [P, HALF])
        attr_ps = ph.ps("attr", [P, HALF])
        val_ps = ph.ps("val", [P, HALF])
        pre_ps = ph.ps("pre", [P, HALF])
        logit_ps = ph.ps("logit", [P, HALF])
        out_ps = ph.ps("out", [P, HALF])
        den_ps = ph.ps("den", [P, HALF])
        attr_in = ph.pair("attr_in")
        attr_set = ph.sem("attr_set")
        in_sb = ph.sem("in_sb")
        val_mm = ph.sem("val_mm")
        pre_mm = ph.sem("pre_mm")
        val_set = ph.sem("val_set")
        pre_set = ph.sem("pre_set")
        leaky = ph.sem("leaky")
        logits = ph.sem("logits")
        begun = ph.sem("begun")
        topped = ph.sem("topped")
        diffs = ph.sem("diffs")
        lowered = ph.sem("lowered")
        exps = ph.sem("exps")
        probs_v = ph.sem("probs_v")
        num_done = ph.sem("num_done")
        den_done = ph.sem("den_done")
        guarded = ph.sem("guarded")
        multiplied = ph.sem("multiplied")
        top_set = ph.sem("top_set")
        with nc.Block() as block:
            @block.gpsimd
            def _(pool):
                pool.memset(attr[(sh.edge_chunks - 1) % 2][:, :, :], 0.0).then_inc(attr_set, 1)
                ph.pool_program(pool)

            @block.sync
            def _(sp):
                sp.wait_ge(attr_set, 1)

                def step(c, b, q):
                    if used_before(c, 2):
                        sp.wait_ge(ph.turned, 2 * c - 2)
                    ea = a["edge_attr_16"]
                    if isinstance(c, int) and c == sh.edge_chunks - 1:
                        whole, left = real // P, real % P
                        sp.dma_start(attr[b][:, 0:whole, :], ea[c * CH:c * CH + whole * P, :].rearrange("(t p) d -> p t d", p=P)).then_inc(attr_in[b], 16)
                        sp.dma_start(attr[b][0:left, whole, :], ea[c * CH + whole * P:sh.e, :]).then_inc(attr_in[b], 16)
                    else:
                        sp.dma_start(attr[b][:, :, :], ea[bass.ds(c * CH, CH), :].rearrange("(t p) d -> p t d", p=P)).then_inc(attr_in[b], 16)

                sweep(sp, sh.edge_chunks, sh.edge_chunks - 1, step)

            @block.tensor
            def _(pe):
                def front(c, b, q, h):
                    if h == 0:
                        ph.rows_landed(pe, b, q)
                        last = isinstance(c, int) and c == sh.edge_chunks - 1
                        pe.wait_ge(attr_in[b], 16 * q + 16 + (16 if last else 0))
                    if used_before(c, 1) or h:
                        pe.wait_ge(in_sb, 3 * (2 * c + h))
                    for i, t in enumerate(tiles_of(h)):
                        pe.transpose(src_ps[:, i * P:(i + 1) * P], ph.rows["src"][b][:, t, :], k["ident"][:, :])
                        pe.transpose(dst_ps[:, i * P:(i + 1) * P], ph.rows["dst"][b][:, t, :], k["ident"][:, :])
                        mm = pe.transpose(attr_ps[0:n_attr, i * P:(i + 1) * P], attr[b][:, t, :], k["ident"][:, :])
                    mm.then_inc(ph.turned, 1)
                    pe.wait_ge(in_sb, 3 * (2 * c + h) + 3)
                    if used_before(c, 1) or h:
                        pe.wait_ge(val_set, 2 * c + h)
                    pe.matmul(val_ps[:, :], k["gat_l"][:, :], sT[h][:, :], start=True, stop=True).then_inc(val_mm, 1)
                    if used_before(c, 1) or h:
                        pe.wait_ge(pre_set, 2 * c + h)
                    pe.matmul(pre_ps[:, :], k["gat_l"][:, :], sT[h][:, :], start=True, stop=False)
                    pe.matmul(pre_ps[:, :], k["gat_r"][:, :], dT[h][:, :], start=False, stop=False)
                    pe.matmul(pre_ps[:, :], k["gat_e"][0:n_attr, :], eT[h][:, :], start=False, stop=True).then_inc(pre_mm, 1)

                def logit(c, b, q, h):
                    pe.wait_ge(leaky, 2 * c + h + 1)
                    if used_before(c, 1) or h:
                        pe.wait_ge(lowered, 2 * c + h)
                    pe.matmul(logit_ps[:, :], k["head_att"][:, :], pre[h][:, :], start=True, stop=True).then_inc(logits, 1)

                def back(c, b, q, h):
                    pe.wait_ge(den_done, 2 * c + h + 1)
                    pe.wait_ge(num_done, 2 * c + h + 1)
                    if used_before(c, 1) or h:
                        pe.wait_ge(ph.result_ready, 2 * c + h)
                    for i in range(H):
                        pe.transpose(den_ps[:, i * P:(i + 1) * P], den[h][:, i * P:(i + 1) * P], k["ident"][:, :])
                        mm = pe.transpose(out_ps[:, i * P:(i + 1) * P], num[h][:, i * P:(i + 1) * P], k["ident"][:, :])
                    mm.then_inc(multiplied, 1)

                def step(c, b, q):
                    for h in range(2):
                        front(c, b, q, h)
                        if used_before(c, 1):
                            back(*chunk_before(c, b, q), h)
                    logit(c, b, q, 0)
                    logit(c, b, q, 1)

                sweep(pe, sh.edge_chunks, sh.edge_chunks - 1, step)
                for h in range(2):
                    back(*last_chunk, h)

            @block.scalar
            def _(act):
                def step(c, b, q):
                    for h in range(2):
                        act.wait_ge(ph.turned, 2 * c + h + 1)
                        if used_before(c, 1):
                            act.wait_ge(pre_mm, 2 * c + h - 1)
                        act.activation(sT[h][:, :], src_ps[:, :], ACT.Copy).then_inc(in_sb, 1)
                        act.activation(dT[h][:, :], dst_ps[:, :], ACT.Copy).then_inc(in_sb, 1)
                        act.activation(eT[h][:, :], attr_ps[0:n_attr, :], ACT.Copy).then_inc(in_sb, 1)
                        act.wait_ge(val_mm, 2 * c + h + 1)
                        if used_before(c, 1):
                            act.wait_ge(num_done, 2 * c + h - 1)
                        act.activation(val[h][:, :], val_ps[:, :], ACT.Identity, bias=k["bl"][:, 0:1]).then_inc(val_set, 1)
                        act.wait_ge(pre_mm, 2 * c + h + 1)
                        if used_before(c, 1):
                            act.wait_ge(logits, 2 * c + h - 1)
                        act.activation(pre[h][:, :], pre_ps[:, :], ACT.Identity, bias=k["blr"][:, 0:1]).then_inc(pre_set, 1)
                        if used_before(c, 1):
                            act.wait_ge(diffs, 2 * c + h - 1)
                            act.sem_inc(ph.gate, 1)
                        act.activation(begin[h][:, :], k["same_run"][:, bass.ds(c * CH + h * HALF, HALF)], ACT.Copy,
                                       bias=-BIG, scale=BIG).then_inc(begun, 1)
                    for h in range(2):
                        act.wait_ge(lowered, 2 * c + h + 1)
                        act.activation(fall[h][:, :], fall[h][:, :], ACT.Exp).then_inc(exps, 1)
                        act.activation(prob[h][:, :], prob[h][:, :], ACT.Exp).then_inc(exps, 1)

                sweep(act, sh.edge_chunks, sh.edge_chunks - 1, step)

            @block.vector
            def _(dve):
                dve.memset(top[1][:, HALF:HALF + 1], 0.0).then_inc(top_set, 1)
                dve.wait_ge(top_set, 1)

                def leak(c, b, q, h):
                    dve.wait_ge(pre_set, 2 * c + h + 1)
                    dve.scalar_tensor_tensor(out=pre[h][:, :], in0=pre[h][:, :], scalar=0.2, in1=pre[h][:, :], op0=ALU.mult,
                                             op1=ALU.max).then_inc(leaky, 1)

                def front(c, b, q, h):
                    if used_before(c, 1):
                        dve.wait_ge(diffs, 2 * c + h - 1)
                        dve.wait_ge(exps, 2 * (2 * c + h - 1))
                    if used_before(c, 1) or h:
                        dve.wait_ge(topped, 2 * c + h)
                    dve.tensor_copy(top[h][:, 0:1], top[1 - h][:, HALF:HALF + 1]).then_inc(top_set, 1)
                    dve.wait_ge(top_set, 2 * c + h + 2)
                    dve.wait_ge(logits, 2 * c + h + 1)
                    dve.wait_ge(begun, 2 * c + h + 1)
                    dve.tensor_tensor_scan(top[h][:, 1:HALF + 1], begin[h][:, :], logit_ps[:, :], top[h][:, 0:1], ALU.add,
                                           ALU.max).then_inc(topped, 1)
                    if used_before(c, 1):
                        dve.wait_ge(num_done, 2 * c + h - 1)
                        dve.wait_ge(den_done, 2 * c + h - 1)
                    dve.wait_ge(topped, 2 * c + h + 1)
                    dve.tensor_tensor(fall[h][:, :], top[h][:, 0:HALF], begin[h][:, :], ALU.add).then_inc(diffs, 1)
                    dve.wait_ge(diffs, 2 * c + h + 1)
                    dve.tensor_tensor(prob[h][:, :], logit_ps[:, :], top[h][:, 1:HALF + 1], ALU.subtract)
                    dve.tensor_tensor(fall[h][:, :], fall[h][:, :], top[h][:, 1:HALF + 1], ALU.subtract).then_inc(lowered, 1)

                def back(c, b, q, h):
                    dve.wait_ge(exps, 2 * (2 * c + h + 1))
                    go_on = (lambda z: z[1 - h][:, HALF - 1:HALF] if h or used_before(c, 1) else 0.0)
                    if used_before(c, 1) or h:
                        dve.wait_ge(den_done, 2 * c + h)
                        dve.wait_ge(num_done, 2 * c + h)
                    if used_before(c, 1):
                        dve.wait_ge(multiplied, 2 * c + h - 1)
                    dve.tensor_tensor_scan(den[h][:, :], fall[h][:, :], prob[h][:, :], go_on(den), ALU.mult,
                                           ALU.add).then_inc(den_done, 1)
                    dve.tensor_tensor(val[h][:, :], val[h][:, :], prob[h][:, :], ALU.mult).then_inc(probs_v, 1)
                    dve.wait_ge(probs_v, 2 * c + h + 1)
                    dve.tensor_tensor_scan(num[h][:, :], fall[h][:, :], val[h][:, :], go_on(num), ALU.mult,
                                           ALU.add).then_inc(num_done, 1)

                def divide(c, b, q, h):
                    dve.wait_ge(multiplied, 2 * c + h + 1)
                    dens = den_ps[:, :].rearrange("p (t a w) -> p t a w", t=H, w=width)[:, :, :, 0]
                    dve.tensor_scalar(inv_den[h][:, :, :], dens, 1e-16, None, ALU.add).then_inc(guarded, 1)
                    dve.wait_ge(guarded, 2 * (2 * c + h) + 1)
                    dve.reciprocal(inv_den[h][:, :, :], inv_den[h][:, :, :]).then_inc(guarded, 1)
                    dve.wait_ge(guarded, 2 * (2 * c + h) + 2)
                    ph.result_free(dve, c, b, q)
                    dve.tensor_tensor(ph.result[b][:, H * h:H * h + H, :].rearrange("p t (a w) -> p (t a) w", w=width),
                                      out_ps[:, :].rearrange("p (t w) -> p t w", w=width),
                                      spread_features(inv_den[h][:, :, :].rearrange("p t a -> p (t a)"), [P, H * heads, width]),
                                      ALU.mult).then_inc(ph.result_ready, 1)

                def step(c, b, q):
                    for h in range(2):
                        leak(c, b, q, h)
                        if used_before(c, 1):
                            divide(*chunk_before(c, b, q), h)
                    front(c, b, q, 0)
                    front(c, b, q, 1)
                    back(c, b, q, 0)
                    back(c, b, q, 1)

                sweep(dve, sh.edge_chunks, sh.edge_chunks - 1, step, peeled=2)
                for h in range(2):
                    divide(*last_chunk, h)



class Norm:

    def __init__(self, ph, name, slots, newton=False, copies=1):
        self.slots, self.newton = slots, newton
        self.stats = ph.sb(f"{name}_stats", [P, slots, 6])
        self.tmp = ph.sb(f"{name}_tmp", [P, 3, slots])
        self.root = ph.sb(f"{name}_root", [P, slots])
        self.scale = [ph.sb(f"{name}_scale{i}", [P, slots]) for i in range(copies)]
        self.shift = [ph.sb(f"{name}_shift{i}", [P, slots]) for i in range(copies)]
        self.step = ph.sem(f"{name}_step")
        self.steps = 5 + (RSQRT_STEPS + 1 if newton else 1)
        self.var_ready = ph.sem(f"{name}_var")
        self.rooted = ph.sem(f"{name}_rooted")
        self.ready = ph.sem(f"{name}_ready")

    def take(self, dve, z, n, slot):
        for j in range(T):
            ins = dve.bn_stats(self.stats[0:n, slot + j, :], z[0:n, j, :])
        return ins

    def solve(self, dve, turn, copy=0):
        self.solve_var(dve, turn, copy)
        self.solve_scale(dve, turn, copy)

    def solve_var(self, dve, turn, copy=0):
        base, t, scale, eps = turn * self.steps, self.tmp, self.scale[copy], LN_EPS
        me, mo, ve, vo = (self.stats[:, :, i] for i in (1, 4, 2, 5))
        dve.wait_ge(self.step, base + 1)
        dve.tensor_tensor(t[:, 0, :], me, mo, ALU.subtract).then_inc(self.step, 1)
        dve.tensor_tensor(t[:, 1, :], ve, vo, ALU.add).then_inc(self.step, 1)
        dve.tensor_tensor(t[:, 2, :], me, mo, ALU.add).then_inc(self.step, 1)
        dve.wait_ge(self.step, base + 2)
        dve.scalar_tensor_tensor(out=t[:, 0, :], in0=t[:, 0, :], scalar=D / 4.0, in1=t[:, 0, :], op0=ALU.mult,
                                 op1=ALU.mult).then_inc(self.step, 1)
        dve.wait_ge(self.step, base + 5)
        if self.newton:
            dve.tensor_tensor(t[:, 1, :], t[:, 1, :], t[:, 0, :], ALU.add).then_inc(self.step, 1)
            dve.wait_ge(self.step, base + 6)
            dve.tensor_scalar(t[:, 1, :], t[:, 1, :], 1.0 / D, eps, ALU.mult, ALU.add).then_inc(self.var_ready, 1)
            dve.wait_ge(self.var_ready, turn + 1)
            rsqrt(dve, scale[:, :], t[:, 1, :], t[:, 0, :], self.step, base + 6)
        else:
            dve.tensor_tensor(t[:, 1, :], t[:, 1, :], t[:, 0, :], ALU.add).then_inc(self.var_ready, 1)

    def solve_scale(self, dve, turn, copy=0):
        base, t, scale = turn * self.steps, self.tmp, self.scale[copy]
        if not self.newton:
            dve.wait_ge(self.rooted, turn + 1)
            dve.reciprocal(scale[:, :], self.root[:, :]).then_inc(self.step, 1)
            dve.wait_ge(self.step, base + 6)
        dve.scalar_tensor_tensor(out=self.shift[copy][:, :], in0=t[:, 2, :], scalar=-0.5, in1=scale[:, :],
                                 op0=ALU.mult, op1=ALU.mult).then_inc(self.ready, 1)

    def take_root(self, act, turn, eps):
        act.wait_ge(self.var_ready, turn + 1)
        act.activation(self.root[:, :], self.tmp[:, 1, :], ACT.Sqrt, bias=eps[:, 0:1], scale=1.0 / D).then_inc(self.rooted, 1)

    def apply(self, act, out, z, n, slot, copy=0):
        for j in range(T):
            at = slot + j
            ins = act.activation(out[0:n, j, :], z[0:n, j, :], ACT.Identity, bias=self.shift[copy][0:n, at:at + 1],
                                 scale=self.scale[copy][0:n, at:at + 1])
        return ins


class NodePhase(Phase):

    def __init__(self, nc, name, sh, streams, out):
        super().__init__(nc, name)
        self.sh, self.streams, self.out_dram = sh, streams, out

    def __enter__(self):
        super().__enter__()
        self.buf = {n: [self.sb(f"in_{n}{b}", [P, T, D]) for b in range(2)] for n in self.streams}
        self.landed = {n: self.pair(f"landed_{n}") for n in self.streams}
        self.out_ready = self.sem("out_ready")
        return self

    def load_program(self, sp, free):
        def step(c, b, q):
            n = self.sh.rows(c)
            for name, src in self.streams.items():
                if used_before(c, 2):
                    for sem, per in free[name]:
                        sp.wait_ge(sem, per * (c - 1))
                sp.dma_start(self.buf[name][b][0:n, :, :], node_rows(src, c, self.sh)).then_inc(self.landed[name][b], 16)

        self.node_sweep(sp, step)

    def node_sweep(self, eng, step):
        sweep(eng, self.sh.node_chunks, self.sh.node_chunks - 1, step)

    def have(self, eng, name, b, q):
        eng.wait_ge(self.landed[name][b], 16 * q + 16)


def norm_nodes(nc, k, dram, sh, name, table, x0, out, scale_row, shift_row):
    pairs = sh.node_pairs
    with NodePhase(nc, name, sh, {"y": table, "x0": x0}, out) as ph:
        z = [ph.sb(f"z{i}", [P, T, D]) for i in range(4)]
        o = [ph.sb(f"o{i}", [P, T, D]) for i in range(4)]
        ln = Norm(ph, "ln", 2 * T, copies=2)
        stored = [ph.sem(f"stored_o{i}") for i in range(4)]
        shifted, scaled, z_done = ph.sem("shifted"), ph.sem("scaled"), ph.sem("z_done")

        def pair_units(eng, unit):
            unit(0, 0)
            unit(1, 1)
            with eng.Fori(1, pairs // 2) as q:
                unit(2 * q, 0)
                unit(2 * q + 1, 1)
            for m in range(pairs // 2 * 2, pairs):
                unit(m, m % 2)

        def chunks(m, par):
            for b in range(2):
                yield 2 * m + b, b, 2 * par + b, sh.rows(2 * m + b)

        with nc.Block() as block:
            @block.sync
            def _(sp):
                ph.load_program(sp, {"y": [(scaled, 1)], "x0": [(z_done, 1)]})

            @block.gpsimd
            def _(pool):
                def step(c, b, q):
                    n = sh.rows(c)
                    x = ph.buf["x0"][b][0:n, :, :]
                    ph.have(pool, "x0", b, q)
                    pool.tensor_tensor(x, x, spread_slots(shift_row[0:n, :], [n, T, D]), ALU.add).then_inc(shifted, 1)

                ph.node_sweep(pool, step)

            @block.vector
            def _(dve):
                def unit(m, par):
                    for c, b, i, n in chunks(m, par):
                        ph.have(dve, "y", b, m)
                        if not isinstance(m, int) or m >= 2:
                            dve.wait_ge(ph.out_ready, c - 3)
                        dve.tensor_tensor(z[i][0:n, :, :], ph.buf["y"][b][0:n, :, :], spread_slots(scale_row[0:n, :], [n, T, D]),
                                          ALU.mult).then_inc(scaled, 1)
                        dve.wait_ge(scaled, c + 1)
                        dve.wait_ge(shifted, c + 1)
                        dve.tensor_tensor(z[i][0:n, :, :], z[i][0:n, :, :], ph.buf["x0"][b][0:n, :, :], ALU.add).then_inc(z_done, 1)
                    for c, b, i, n in chunks(m, par):
                        dve.wait_ge(z_done, c + 1)
                        ins = ln.take(dve, z[i], n, b * T)
                    ins.then_inc(ln.step, 1)
                    ln.solve(dve, m, copy=par)

                pair_units(dve, unit)

            @block.scalar
            def _(act):
                def unit(m, par):
                    ln.take_root(act, m, k["ln_eps"])
                    act.wait_ge(ln.ready, m + 1)
                    for c, b, i, n in chunks(m, par):
                        if not isinstance(m, int) or m >= 2:
                            act.wait_ge(stored[i], (m - par) * 8)
                        ln.apply(act, o[i], z[i], n, b * T, copy=par).then_inc(ph.out_ready, 1)
                    for c, b, i, n in chunks(m, par):
                        act.wait_ge(ph.out_ready, c + 1)
                        act.dma_start(node_rows(out, c, sh), o[i][0:n, :, :]).then_inc(stored[i], 16)

                pair_units(act, unit)
                for i in range(4):
                    act.wait_ge(stored[i], 16 * ((pairs + 1 - i // 2) // 2))


def gat_nodes(nc, k, dram, sh, name, table, out):
    pairs = sh.node_pairs
    with Phase(nc, name) as ph:
        sums, x, z1, z2 = ([ph.sb(f"{n}{i}", [P, T, D]) for i in range(4)] for n in ("sums", "x", "z1", "z2"))
        o = [ph.sb(f"o{b}", [P, T, D]) for b in range(2)]
        ln = Norm(ph, "ln", 4 * T, newton=True, copies=2)
        sums_in, x_in = ([ph.sem(f"{n}_in{i}") for i in range(4)] for n in ("sums", "x"))
        biased, gelu_done, z1_done, beta_added = ph.sem("biased"), ph.sem("gelu_done"), ph.sem("z1_done"), ph.sem("beta_added")
        normed, scaled, z2_done, out_ready = ph.sem("normed"), ph.sem("scaled"), ph.sem("z2_done"), ph.sem("out_ready")
        stored = ph.pair("stored")
        stats_set = ph.sem("stats_set")

        def stages(eng, a, b, c):
            def unit(m, par):
                for stage, lag in ((a, 0), (b, 1), (c, 2)):
                    if not isinstance(m, int) or 0 <= m - lag < pairs:
                        stage(m - lag, (par + lag) % 2)

            for m in range(4):
                unit(m, m % 2)
            with eng.Fori(2, pairs // 2) as q:
                unit(2 * q, 0)
                unit(2 * q + 1, 1)
            for m in range(pairs // 2 * 2, pairs + 2):
                unit(m, m % 2)

        def chunks(m, par):
            for b in range(2):
                c = m * 2 + b
                yield c, 2 * par + b, sh.rows(c), not isinstance(m, int) or m >= 2

        def nothing(m, par):
            pass

        def landed(m, par):
            return 16 * ((m - par) // 2) + 16 if isinstance(m, int) else (m - par) * 8 + 16

        with nc.Block() as block:
            @block.sync
            def _(sp):
                def load(m, par):
                    for c, i, n, again in chunks(m, par):
                        if again:
                            sp.wait_ge(z1_done, c - 3)
                            sp.wait_ge(z2_done, c - 3)
                        sp.dma_start(sums[i][0:n, :, :], node_rows(dram["node_sums"], c, sh)).then_inc(sums_in[i], 16)
                        sp.dma_start(x[i][0:n, :, :], node_rows(table, c, sh)).then_inc(x_in[i], 16)

                stages(sp, load, nothing, nothing)

            @block.gpsimd
            def _(pool):
                def bias(m, par):
                    for c, i, n, again in chunks(m, par):
                        pool.wait_ge(sums_in[i], landed(m, par))
                        pool.tensor_tensor(sums[i][0:n, :, :], sums[i][0:n, :, :], spread_slots(k["gat_b"][0:n, :], [n, T, D]),
                                           ALU.add).then_inc(biased, 1)

                def gamma(m, par):
                    for c, i, n, again in chunks(m, par):
                        pool.wait_ge(z1_done, c + 1)
                        pool.tensor_tensor(x[i][0:n, :, :], x[i][0:n, :, :], spread_slots(k["gat_beta"][0:n, :], [n, T, D]),
                                           ALU.add).then_inc(beta_added, 1)
                    for c, i, n, again in chunks(m, par):
                        pool.wait_ge(normed, c + 1)
                        pool.tensor_tensor(z2[i][0:n, :, :], z2[i][0:n, :, :], spread_slots(k["gat_gamma"][0:n, :], [n, T, D]),
                                           ALU.mult).then_inc(scaled, 1)

                stages(pool, bias, gamma, nothing)

            @block.scalar
            def _(act):
                def gelu(m, par):
                    for c, i, n, again in chunks(m, par):
                        act.wait_ge(biased, c + 1)
                        act.activation(sums[i][0:n, :, :], sums[i][0:n, :, :], ACT.Gelu).then_inc(gelu_done, 1)

                def norm1(m, par):
                    act.wait_ge(ln.ready, m + 1)
                    for c, i, n, again in chunks(m, par):
                        if again:
                            act.wait_ge(out_ready, c - 3)
                        ln.apply(act, z2[i], z1[i], n, (i % 2) * T, copy=par).then_inc(normed, 1)

                def norm2(m, par):
                    act.wait_ge(ln.ready, m + 2)
                    for c, i, n, again in chunks(m, par):
                        if not isinstance(m, int) or m >= 1:
                            act.wait_ge(stored[i % 2], m * 16)
                        ln.apply(act, o[i % 2], z2[i], n, (2 + i % 2) * T, copy=1 - par).then_inc(out_ready, 1)
                    for c, i, n, again in chunks(m, par):
                        act.wait_ge(out_ready, c + 1)
                        act.dma_start(node_rows(out, c, sh), o[i % 2][0:n, :, :]).then_inc(stored[i % 2], 16)

                stages(act, gelu, norm1, norm2)
                for b in range(2):
                    act.wait_ge(stored[b], 16 * pairs)

            @block.vector
            def _(dve):
                dve.memset(ln.stats[:, :, :], 1.0).then_inc(stats_set, 1)
                dve.wait_ge(stats_set, 1)

                def sum1(m, par):
                    for c, i, n, again in chunks(m, par):
                        dve.wait_ge(gelu_done, c + 1)
                        dve.wait_ge(x_in[i], landed(m, par))
                        if again:
                            dve.wait_ge(normed, c - 3)
                        dve.tensor_tensor(z1[i][0:n, :, :], sums[i][0:n, :, :], x[i][0:n, :, :], ALU.add).then_inc(z1_done, 1)
                    for c, i, n, again in chunks(m, par):
                        dve.wait_ge(z1_done, c + 1)
                        ins = ln.take(dve, z1[i], n, (i % 2) * T)
                    if isinstance(m, int) and m == 0:
                        ins.then_inc(ln.step, 1)
                        ln.solve(dve, 0, copy=0)

                def sum2(m, par):
                    for c, i, n, again in chunks(m, par):
                        dve.wait_ge(scaled, c + 1)
                        dve.wait_ge(beta_added, c + 1)
                        dve.tensor_tensor(z2[i][0:n, :, :], z2[i][0:n, :, :], x[i][0:n, :, :], ALU.add).then_inc(z2_done, 1)
                    for c, i, n, again in chunks(m, par):
                        dve.wait_ge(z2_done, c + 1)
                        ins = ln.take(dve, z2[i], n, (2 + i % 2) * T)
                    ins.then_inc(ln.step, 1)
                    if not isinstance(m, int) or m >= 1:
                        dve.wait_ge(out_ready, 2 * m)
                    ln.solve(dve, m + 1, copy=1 - par)

                stages(dve, sum1, sum2, nothing)



def merged_sweep(eng, k, sh, edge_unit, node_unit):
    full, last = sh.edge_pairs, sh.node_pairs - 1

    def ready(j):
        at = slice(j + 1, j + 2) if isinstance(j, int) else bass.ds(j + 1, 1)
        return eng.value_load(k["ready"][0:1, at], min_val=0, max_val=last)

    def nodes(first, end, at, scattered):
        with eng.If(first < end):
            with eng.Fori(first, end) as m:
                node_unit(m, m * 4 + at, scattered)
        with eng.Else():
            pass

    edge_unit(0, 0, None, 4)
    with eng.Fori(1, full) as j:
        before2, before, end = ready(j - 2), ready(j - 1), ready(j)
        edge_unit(j, j * 4 + before * 4, j * 4 + before2 * 4 - 4, 4)
        if node_unit:
            nodes(before, end, j * 4 + 4, j)
    before2, before = ready(full - 2), ready(full - 1)
    edge_unit(full, before * 4 + 4 * full, before2 * 4 + 4 * (full - 1), 2)
    if node_unit:
        at = 4 * full + 2
        nodes(before, last, at, None)
        node_unit(last, last * 4 + at, None)


class Conv(Phase):

    def __init__(self, nc, name, k, dram, sh, table, out, streams):
        super().__init__(nc, name)
        self.k, self.dram, self.sh, self.table, self.out_dram, self.streams = k, dram, sh, table, out, streams

    def __enter__(self):
        super().__enter__()
        self.rows = [self.sb(f"rows{b}", [P, T, D]) for b in range(2)]
        self.idx = [self.sb(f"idx{b}", [P, T], I32) for b in range(2)]
        self.place = [self.sb(f"place{b}", [P, T], I32) for b in range(2)]
        self.result = [self.sb(f"result{b}", [P, T, D]) for b in range(2)]
        self.gate = self.sem("gate")
        self.slots = self.sem("slots")
        self.place_set = self.sem("place_set")
        self.gathered = self.pair("gathered")
        self.scattered = self.pair("scattered")
        self.turn_ps = [self.ps(f"turn{i}", [P, HALF]) for i in range(2)]
        self.out_ps = [self.ps(f"out{i}", [P, HALF]) for i in range(2)]
        self.turned = self.sem("turned")
        self.turn_read = self.sem("turn_read")
        self.multiplied = self.sem("multiplied")
        self.out_read = self.sem("out_read")
        self.buf = {n: [self.sb(f"in_{n}{b}", [P, T, D]) for b in range(2)] for n in self.streams}
        self.landed = {n: self.pair(f"landed_{n}") for n in self.streams}
        self.used = {n: self.sem(f"used_{n}") for n in self.streams if n != "y"}
        self.nodeT = self.sb("nodeT", [P, 4, HALF])
        self.nodes_turned = self.sem("nodes_turned")
        self.finished = self.sem("finished")
        self.stored = self.pair("stored")
        return self

    def grant(self, eng, semaphores):
        for sem, n in semaphores:
            eng.sem_inc(sem, n)


    def pool_program(self, pool):
        sh, k = self.sh, self.k
        nodes_end = pool.to_reg(sh.n - 1)

        def gather(c, b, free_at):
            if free_at is not None:
                pool.wait_ge(self.turned, free_at)
                pool.sem_inc(self.gate, 1)
            pool.tensor_copy(self.idx[b][:, :], k["src_idx"][:, bass.ds(c * T, T)]).then_inc(self.slots, 1)
            pool.wait_ge(self.slots, c + 1)
            pool.sem_inc(self.gate, 1)
            for t in range(T):
                pool.indirect_dma_start(self.rows[b][:, t, :], None, self.table[:, :],
                                        bass.IndirectOffsetOnAxis(self.idx[b][:, t:t + 1], 0)).then_inc(self.gathered[b], 16)

        def scatter(c, b, ready_at):
            pool.wait_ge(self.out_read, ready_at)
            pool.sem_inc(self.gate, 1)
            pool.tensor_copy(self.place[b][:, :], k["place_idx"][:, bass.ds(c * T, T)]).then_inc(self.place_set, 1)
            pool.wait_ge(self.place_set, c + 1)
            pool.sem_inc(self.gate, 1)
            for t in range(T):
                pool.indirect_dma_start(self.dram["node_sums"][:, :], bass.IndirectOffsetOnAxis(self.place[b][:, t:t + 1], 0),
                                        self.result[b][:, t, :], None, bounds_check=nodes_end,
                                        oob_is_err=False).then_inc(self.scattered[b], 16)

        def unit(j, at, at_before, halves):
            for b in range(halves // 2):
                gather(2 * j + b, b, None if at_before is None else at_before + 2 * b + 2)
                if at_before is not None:
                    scatter(2 * j - 2 + b, b, at_before + 2 * b + 2)
            if halves == 2:
                scatter(2 * j - 1, 1, at_before + 4)
                scatter(2 * j, 0, at + 2)

        merged_sweep(pool, k, sh, unit, None)
        for b in range(2):
            pool.wait_ge(self.scattered[b], self.all_scattered(b))

    def all_scattered(self, b):
        return 16 * T * ((self.sh.edge_chunks + 1 - b) // 2)

    def rows_landed(self, eng, j, b):
        eng.wait_ge(self.gathered[b], 16 * T * j + 16 * T)

    def turn_edges(self, pe, j, at, halves):
        for i in range(halves):
            if i % 2 == 0:
                self.rows_landed(pe, j, i // 2)
            if not isinstance(at, int) or at + i >= 2:
                pe.wait_ge(self.turn_read, at + i - 1)
            for n in range(H):
                mm = pe.transpose(self.turn_ps[i % 2][:, n * P:(n + 1) * P], self.rows[i // 2][:, H * (i % 2) + n, :],
                                  self.k["ident"][:, :])
            mm.then_inc(self.turned, 1)

    def multiply_edges(self, pe, at, halves, ready, lhs, weight):
        for i in range(halves):
            ready(i)
            if not isinstance(at, int) or at + i >= 2:
                pe.wait_ge(self.out_read, at + i - 1)
            for n in range(H):
                mm = pe.matmul(self.out_ps[i % 2][:, n * D:(n + 1) * D], lhs(i)[:, n * P:(n + 1) * P], weight[:, :],
                               start=True, stop=True)
            mm.then_inc(self.multiplied, 1)

    def result_half(self, i):
        return self.result[i // 2][:, H * (i % 2):H * (i % 2) + H, :]

    def out_half(self, i, n=P):
        return self.out_ps[i % 2][0:n, :].rearrange("p (t f) -> p t f", f=D)

    def result_free(self, eng, j, i):
        if not isinstance(j, int) or j >= 1:
            eng.wait_ge(self.scattered[i // 2], 16 * T * j)


    def load_nodes(self, sp, m, at, scattered_pairs):
        for name in sorted(self.streams, key=lambda name: name == "sums"):
            for b in range(2):
                c = m * 2 + b
                if name == "y":
                    sp.wait_ge(self.nodes_turned, 2 * m + b + 1)
                    sp.sem_inc(self.gate, 1)
                if name in self.used:
                    sp.wait_ge(self.used[name], 2 * m + b + 1)
                    sp.sem_inc(self.gate, 1)
                if name == "sums" and b == 0:
                    for s in range(2):
                        sp.wait_ge(self.scattered[s], self.all_scattered(s) if scattered_pairs is None else scattered_pairs * (16 * T))
                        sp.sem_inc(self.gate, 1)
                sp.dma_start(self.buf[name][b][0:self.sh.rows(c), :, :],
                             node_rows(self.streams[name], c, self.sh)).then_inc(self.landed[name][b], 16)

    def have(self, eng, name, m, b):
        eng.wait_ge(self.landed[name][b], 16 * m + 16)

    def turn_nodes(self, pe, m, at):
        for i in range(4):
            n = self.sh.rows(m * 2 + i // 2)
            if i % 2 == 0:
                self.have(pe, "y", m, i // 2)
            pe.wait_ge(self.turn_read, at + i - 1)
            for t in range(H):
                mm = pe.transpose(self.turn_ps[i % 2][:, t * P:t * P + n], self.buf["y"][i // 2][0:n, H * (i % 2) + t, :],
                                  self.k["ident"][0:n, 0:n])
            mm.then_inc(self.turned, 1)

    def multiply_nodes(self, pe, m, at, weight, between=None):
        for i in range(4):
            if i == 2 and between:
                between()
            n = self.sh.rows(m * 2 + i // 2)
            pe.wait_ge(self.turn_read, at + i + 1)
            pe.wait_ge(self.out_read, at + i - 1)
            for t in range(H):
                mm = pe.matmul(self.out_ps[i % 2][0:n, t * D:(t + 1) * D], self.nodeT[:, i, t * P:t * P + n], weight[:, :],
                               start=True, stop=True)
            mm.then_inc(self.multiplied, 1)

    def turned_to_sbuf(self, act, m, at, scale_shift=None):
        for i in range(4):
            n = self.sh.rows(m * 2 + i // 2)
            act.wait_ge(self.turned, at + i + 1)
            if i % 2:
                act.sem_inc(self.nodes_turned, 1)
            act.wait_ge(self.multiplied, at + i - 3)
            out = self.nodeT[:, i, :].rearrange("p (t n) -> p t n", n=P)[:, :, 0:n]
            src = self.turn_ps[i % 2][:, :].rearrange("p (t n) -> p t n", n=P)[:, :, 0:n]
            if scale_shift is None:
                act.activation(out, src, ACT.Copy).then_inc(self.turn_read, 1)
            else:
                act.activation(out, src, ACT.Identity, bias=scale_shift[:, 1:2], scale=scale_shift[:, 0:1]).then_inc(self.turn_read, 1)


    def store_before(self, act, m, out):
        act.wait_ge(self.finished, 2 * m + 2)
        act.sem_inc(self.gate, 1)
        if isinstance(m, int):
            self.store_pair(act, m - 1, out)
        else:
            with act.If(0 < m):
                self.store_pair(act, (m - 1).with_bounds(min_val=0), out)
            with act.Else():
                for b in range(2):
                    act.sem_inc(self.stored[b], 16)

    def store_pair(self, act, m, out):
        for b in range(2):
            c = m * 2 + b
            act.dma_start(node_rows(self.out_dram, c, self.sh), out[b][0:self.sh.rows(c), :, 0:D]).then_inc(self.stored[b], 16)

    def out_free(self, eng, m, b):
        eng.wait_ge(self.stored[b], 16 * m + 16)

    def all_stored(self, eng):
        for b in range(2):
            eng.wait_ge(self.stored[b], 16 * self.sh.node_pairs + 32)


class GcnEdges:

    def __init__(self, ph, weight, scale_shift):
        self.ph, self.weight, self.scale_shift = ph, weight, scale_shift
        self.w_all = [ph.sb(f"w_all{b}", [P, CH]) for b in range(2)]
        self.hT = ph.sb("hT", [P, 4, HALF])
        self.sums = ph.sb("sums", [P, 4, HALF])
        self.w_in = ph.pair("w_in")
        self.weighted, self.summed = ph.sem("weighted"), ph.sem("summed")

    def sync(self, sp, j, at, at_before, halves):
        for b in range(halves // 2):
            if at_before is not None:
                sp.wait_ge(self.weighted, 4 * j + 2 * b - 2)
                sp.sem_inc(self.ph.gate, 1)
            sp.dma_start(self.w_all[b][:, :], self.ph.dram["edge_w"][bass.ds(j * (2 * CH) + b * CH, CH)].partition_broadcast(P)).then_inc(self.w_in[b], 16)

    def tensor(self, pe, j, at, at_before, halves):
        self.ph.turn_edges(pe, j, at, halves)
        self.ph.multiply_edges(pe, at, halves, lambda i: pe.wait_ge(self.summed, 4 * j + i + 1),
                               lambda i: self.sums[:, i, :], self.weight)

    def scalar(self, act, j, at, at_before, halves):
        ph, ss = self.ph, self.scale_shift
        for i in range(halves):
            act.wait_ge(ph.turned, at + i + 1)
            if at_before is not None:
                act.wait_ge(self.weighted, 4 * j + i - 3)
                act.wait_ge(self.summed, 4 * j + i - 3)
            out, src = self.hT[:, i, :], ph.turn_ps[i % 2][:, :]
            if ss is None:
                act.activation(out, src, ACT.Copy).then_inc(ph.turn_read, 1)
            else:
                act.activation(out, src, ACT.Identity, bias=ss[:, 1:2], scale=ss[:, 0:1]).then_inc(ph.turn_read, 1)
        for i in range(halves):
            act.wait_ge(ph.multiplied, at + i + 1)
            ph.result_free(act, j, i)
            act.activation(ph.result_half(i), ph.out_half(i), ACT.Copy).then_inc(ph.out_read, 1)

    def vector(self, dve, j, at, at_before, halves):
        ph = self.ph
        for i in range(halves):
            dve.wait_ge(ph.turn_read, at + i + 1)
            if i % 2 == 0:
                dve.wait_ge(self.w_in[i // 2], 16 * j + 16)
            s = slice(i % 2 * HALF, (i % 2 + 1) * HALF)
            dve.tensor_tensor(self.hT[:, i, :], self.hT[:, i, :], self.w_all[i // 2][:, s], ALU.mult).then_inc(self.weighted, 1)
            dve.wait_ge(self.weighted, 4 * j + i + 1)
            if at_before is not None:
                dve.wait_ge(ph.multiplied, at + i - 3)
            start = scan_start(dve, self.summed, self.sums, j, i, at_before)
            dve.tensor_tensor_scan(self.sums[:, i, :], ph.k["same_run"][:, bass.ds(j * (4 * HALF) + i * HALF, HALF)], self.hT[:, i, :],
                                   start, ALU.mult, ALU.add).then_inc(self.summed, 1)


def scan_start(dve, done, states, j, i, at_before):
    if i == 0 and at_before is None:
        return 0.0
    dve.wait_ge(done, 4 * j + i)
    return states[:, (i - 1) % 4, HALF - 1:HALF]


class EveEdges:

    def __init__(self, ph, no):
        k = ph.k
        self.ph = ph
        self.wpool, self.weve, self.bpool = k[f"pool{no}"], k[f"eve{no}"], k[f"bpool{no}"]
        self.wconv, self.bconv, self.const = k[f"wconv{no}"], k[f"bconv{no}"], k[f"eve_c{no}"]
        self.xT = ph.sb("xT", [P, 2, HALF])
        self.begin = ph.sb("begin", [P, 2, HALF])
        self.pT, self.hi, self.lo, self.mix = (ph.sb(n, [P, 4, HALF]) for n in ("pT", "hi", "lo", "mix"))
        self.pool_ps = [ph.ps(f"pool{i}", [P, HALF]) for i in range(2)]
        self.pooled_ps, self.pooled, self.begun = ph.sem("pooled_ps"), ph.sem("pooled"), ph.sem("begun")
        self.hi_done, self.lo_done = ph.sem("hi_done"), ph.sem("lo_done")
        self.lo_scaled, self.mixed, self.mix_relu = ph.sem("lo_scaled"), ph.sem("mixed"), ph.sem("mix_relu")

    def sync(self, sp, j, at, at_before, halves):
        pass

    def tensor(self, pe, j, at, at_before, halves):
        ph = self.ph
        ph.turn_edges(pe, j, at, halves)
        for i in range(halves):
            pe.wait_ge(ph.turn_read, at + i + 1)
            if at_before is not None or i >= 2:
                pe.wait_ge(self.pooled, 4 * j + i - 1)
            pe.matmul(self.pool_ps[i % 2][:, :], self.wpool[:, :], self.xT[:, i % 2, :], start=True,
                      stop=True).then_inc(self.pooled_ps, 1)
        ph.multiply_edges(pe, at, halves, lambda i: pe.wait_ge(self.mix_relu, 4 * j + i + 1),
                          lambda i: self.mix[:, i, :], self.weve)

    def scalar(self, act, j, at, at_before, halves):
        ph = self.ph
        later = at_before is not None

        def begin(i):
            if later or i >= 2:
                act.wait_ge(self.lo_done, 4 * j + i - 1)
            act.sem_inc(ph.gate, 1)
            act.activation(self.begin[:, i % 2, :], ph.k["same_run"][:, bass.ds(j * (4 * HALF) + i * HALF, HALF)], ACT.Copy,
                           bias=BIG, scale=-BIG).then_inc(self.begun, 1)

        def copy(i):
            act.wait_ge(ph.turned, at + i + 1)
            if later or i >= 2:
                act.wait_ge(self.pooled_ps, 4 * j + i - 1)
            act.activation(self.xT[:, i % 2, :], ph.turn_ps[i % 2][:, :], ACT.Copy).then_inc(ph.turn_read, 1)

        def pool(i):
            act.wait_ge(self.pooled_ps, 4 * j + i + 1)
            if later:
                act.wait_ge(self.lo_done, 4 * j + i - 3)
                act.wait_ge(self.hi_done, 4 * j + i - 3)
            act.activation(self.pT[:, i, :], self.pool_ps[i % 2][:, :], ACT.Relu, bias=self.bpool[:, 0:1]).then_inc(self.pooled, 1)

        def scale(i):
            act.wait_ge(self.lo_done, 4 * j + i + 1)
            if later:
                act.wait_ge(ph.multiplied, at + i - 3)
            act.activation(self.mix[:, i, :], self.lo[:, i, :], ACT.Identity, bias=self.bconv[:, 0:1],
                           scale=self.wconv[:, 1:2]).then_inc(self.lo_scaled, 1)

        def relu(i):
            act.wait_ge(self.mixed, 4 * j + i + 1)
            act.activation(self.mix[:, i, :], self.mix[:, i, :], ACT.Relu).then_inc(self.mix_relu, 1)

        for i in range(halves):
            copy(i)
            if i < 2:
                begin(i)
        for i in range(halves):
            pool(i)
        for i in range(halves):
            scale(i)
            if i + 2 < halves:
                begin(i + 2)
        for i in range(halves):
            relu(i)

    def vector(self, dve, j, at, at_before, halves):
        ph = self.ph
        later = at_before is not None

        def scans(i):
            dve.wait_ge(self.pooled, 4 * j + i + 1)
            if later:
                dve.wait_ge(self.mixed, 4 * j + i - 3)
            start = scan_start(dve, self.hi_done, self.hi, j, i, at_before)
            dve.tensor_tensor_scan(self.hi[:, i, :], ph.k["same_run"][:, bass.ds(j * (4 * HALF) + i * HALF, HALF)], self.pT[:, i, :],
                                   start, ALU.mult, ALU.max).then_inc(self.hi_done, 1)
            if later:
                dve.wait_ge(self.lo_scaled, 4 * j + i - 3)
            dve.wait_ge(self.begun, 4 * j + i + 1)
            start = scan_start(dve, self.lo_done, self.lo, j, i, at_before)
            dve.tensor_tensor_scan(self.lo[:, i, :], self.begin[:, i % 2, :], self.pT[:, i, :], start, ALU.add,
                                   ALU.min).then_inc(self.lo_done, 1)

        def mix(i):
            dve.wait_ge(self.lo_scaled, 4 * j + i + 1)
            dve.wait_ge(self.hi_done, 4 * j + i + 1)
            dve.scalar_tensor_tensor(out=self.mix[:, i, :], in0=self.hi[:, i, :], scalar=self.wconv[:, 0:1], in1=self.mix[:, i, :],
                                     op0=ALU.mult, op1=ALU.add).then_inc(self.mixed, 1)

        for i in range(halves):
            scans(i)
        for i in range(halves):
            mix(i)
        for i in range(halves):
            dve.wait_ge(ph.multiplied, at + i + 1)
            ph.result_free(dve, j, i)
            dve.tensor_tensor(ph.result_half(i), ph.out_half(i), spread_slots(self.const[:, :], [P, H, D]),
                              ALU.subtract).then_inc(ph.out_read, 1)


class SageEdges:

    def __init__(self, ph, weight):
        self.ph, self.weight = ph, weight
        self.xT = ph.sb("xT", [P, 4, HALF])
        self.sums = ph.sb("sums", [P, 4, HALF])
        self.summed = ph.sem("summed")

    def sync(self, sp, j, at, at_before, halves):
        pass

    def tensor(self, pe, j, at, at_before, halves):
        self.ph.turn_edges(pe, j, at, halves)
        self.ph.multiply_edges(pe, at, halves, lambda i: pe.wait_ge(self.summed, 4 * j + i + 1),
                               lambda i: self.sums[:, i, :], self.weight)

    def scalar(self, act, j, at, at_before, halves):
        ph = self.ph
        for i in range(halves):
            act.wait_ge(ph.turned, at + i + 1)
            if at_before is not None:
                act.wait_ge(self.summed, 4 * j + i - 3)
            act.activation(self.xT[:, i, :], ph.turn_ps[i % 2][:, :], ACT.Copy).then_inc(ph.turn_read, 1)

    def vector(self, dve, j, at, at_before, halves):
        ph = self.ph
        for i in range(halves):
            dve.wait_ge(ph.turn_read, at + i + 1)
            if at_before is not None:
                dve.wait_ge(ph.multiplied, at + i - 3)
            start = scan_start(dve, self.summed, self.sums, j, i, at_before)
            dve.tensor_tensor_scan(self.sums[:, i, :], ph.k["same_run"][:, bass.ds(j * (4 * HALF) + i * HALF, HALF)], self.xT[:, i, :],
                                   start, ALU.mult, ALU.add).then_inc(self.summed, 1)
        for i in range(halves):
            dve.wait_ge(ph.multiplied, at + i + 1)
            ph.result_free(dve, j, i)
            counts = ph.k["inv_count"][:, bass.ds(j * (2 * T) + i * H, H)]
            dve.tensor_tensor(ph.result_half(i), ph.out_half(i), spread_features(counts, [P, H, D]), ALU.mult).then_inc(ph.out_read, 1)


class GcnNodes:

    def __init__(self, ph, no, scale_shift, next_scale_shift, as_rows):
        self.ph, self.no, self.scale_shift, self.next_ss, self.as_rows = ph, no, scale_shift, next_scale_shift, as_rows
        k = ph.k
        self.last = no == 2
        self.weight, self.bias = k[f"gcn{no}"], k[f"gcn_b{no}"]
        self.res = "x0" if "x0" in ph.streams else "y"
        if self.res == "y":
            ph.used["y"] = ph.sem("used_y")
        self.res_b = [ph.sb(f"res_b{b}", [P, T, D]) for b in range(2)]
        self.acc = [ph.sb(f"acc{b}", [P, T, D]) for b in range(2)]
        self.y1 = [ph.sb(f"y1{b}", [P, T, D + 1]) for b in range(2)]
        self.scales = [ph.sb(f"scales{b}", [P, 2, T]) for b in range(2)]
        self.small = ph.sb("small", [P, 8])
        self.diag = ph.sb("diag", [P, D])
        self.gram = ph.ps("gram", [P, 512])
        self.ones_set = ph.sem("ones_set")
        self.scales_set, self.added, self.acc_done = ph.sem("scales_set"), ph.sem("added"), ph.sem("acc_done")
        self.gram_done, self.bn_step, self.root_step = ph.sem("gram_done"), ph.sem("bn_step"), ph.sem("root_step")
        self.grants = [(ph.nodes_turned, 2)] + [(ph.used[n], 2) for n in ph.used] + [(s, 16) for s in ph.stored]

    def tensor_start(self, pe):
        pe.wait_ge(self.ones_set, 2)
        zeros = self.ph.k["zeros"]
        pe.matmul(self.gram[:, 0:D + 1], zeros[:, 0:P], zeros[:, 0:D + 1], start=True, stop=False, skip_group_check=True).then_inc(self.gram_done, 1)

    def tensor(self, pe, m, at, scattered):
        ph = self.ph
        ph.turn_nodes(pe, m, at)
        ph.multiply_nodes(pe, m, at, self.weight, lambda: self.add_gram(pe, m, (P, P)))

    def add_gram(self, pe, m, rows):
        for b in range(2):
            pe.wait_ge(self.ph.finished, 2 * m + b + 1)
            for t in range(T):
                mm = pe.matmul(self.gram[:, 0:D + 1], self.y1[b][0:rows[b], t, 0:D], self.y1[b][0:rows[b], t, :], start=False,
                               stop=False, skip_group_check=True)
            mm.then_inc(self.gram_done, 1)

    def tensor_end(self, pe):
        last = self.ph.sh.node_chunks - 2
        self.add_gram(pe, self.ph.sh.node_pairs, (self.ph.sh.rows(last), self.ph.sh.rows(last + 1)))
        if self.last:
            pe.wait_ge(self.bn_step, 12)
            for i in range(2):
                pe.matmul(self.ph.turn_ps[0][:, i * D:(i + 1) * D], self.as_rows[2][:, i, :], self.ph.k["ident"][:, :], start=True,
                          stop=True).then_inc(self.gram_done, 1)

    def scalar(self, act, m, at, scattered):
        ph = self.ph
        ph.turned_to_sbuf(act, m, at, self.scale_shift)
        self.finish_scalar(act, m)

    def finish_scalar(self, act, m):
        ph = self.ph
        for b in range(2):
            n = ph.sh.rows((m - 1) * 2 + b)
            act.wait_ge(self.acc_done, 2 * m + b + 1)
            ph.out_free(act, m, b)
            act.wait_ge(self.gram_done, 2 * m + 1)
            act.activation(self.y1[b][0:n, :, 0:D], self.acc[b][0:n, :, :], ACT.Copy if self.last else ACT.Relu).then_inc(ph.finished, 1)
        ph.store_before(act, m, self.y1)

    def finish_vector(self, dve, m):
        pass

    def vector(self, dve, m, at, scattered):
        ph, k = self.ph, self.ph.k
        for b in range(2):
            n = ph.sh.rows(m * 2 + b)
            s = slice(None)
            dve.tensor_copy(self.scales[b][:, :, :], k["dinvs"][:, bass.ds(m * 2 + b, 1), :, :].rearrange("p o a t -> p (o a) t")).then_inc(self.scales_set, 1)
            ph.have(dve, self.res, m, b)
            dve.tensor_tensor(self.res_b[b][0:n, :, :], ph.buf[self.res][b][0:n, :, :], spread_slots(self.bias[0:n, :], [n, T, D]),
                              ALU.add).then_inc(ph.used[self.res], 1)
        for b in range(2):
            n = ph.sh.rows(m * 2 + b)
            ph.have(dve, "sums", m, b)
            dve.wait_ge(ph.used[self.res], 2 * m + b + 3)
            dve.wait_ge(self.scales_set, 2 * m + b + 1)
            for t in range(T):
                ins = dve.scalar_tensor_tensor(out=self.res_b[b][0:n, t, :], in0=ph.buf["sums"][b][0:n, t, :],
                                               scalar=self.scales[b][0:n, 0, t:t + 1], in1=self.res_b[b][0:n, t, :],
                                               op0=ALU.mult, op1=ALU.add)
            ins.then_inc(ph.used["sums"], 1)
        for i in range(4):
            b = i // 2
            n = ph.sh.rows(m * 2 + b)
            dve.wait_ge(ph.multiplied, at + i + 1)
            if i % 2 == 0:
                dve.wait_ge(ph.used["sums"], 2 * m + b + 3)
                dve.wait_ge(ph.finished, 2 * m + b + 1)
            for t in range(H):
                tt = H * (i % 2) + t
                ins = dve.scalar_tensor_tensor(out=self.acc[b][0:n, tt, :], in0=ph.out_ps[i % 2][0:n, t * D:(t + 1) * D],
                                               scalar=self.scales[b][0:n, 1, tt:tt + 1], in1=self.res_b[b][0:n, tt, :],
                                               op0=ALU.mult, op1=ALU.add)
            ins.then_inc(ph.out_read, 1)
            if i % 2:
                dve.wait_ge(ph.out_read, at + i + 1)
                dve.sem_inc(self.acc_done, 1)

    def vector_start(self, dve):
        for b in range(2):
            dve.memset(self.acc[b][:, :, :], 0.0).then_inc(self.acc_done, 1)
            dve.memset(self.y1[b][:, :, D:D + 1], 1.0).then_inc(self.ones_set, 1)

    def vector_end(self, dve):
        ph, k, sh = self.ph, self.ph.k, self.ph.sh
        gamma, beta = k[f"gamma{self.no}"], k[f"beta{self.no}"]
        mean, sq, var, m2, root = (self.small[:, i:i + 1] for i in range(5))
        ss, step, gram = self.next_ss, self.bn_step, self.gram
        dve.wait_ge(self.gram_done, sh.node_chunks + 3)
        dve.tensor_tensor(self.diag[:, :], gram[:, 0:D], k["ident"][:, :], ALU.mult).then_inc(step, 1)
        dve.tensor_scalar(mean, gram[:, D:D + 1], 1.0 / sh.n, None, ALU.mult).then_inc(step, 1)
        dve.wait_ge(step, 2)
        dve.tensor_reduce(sq, self.diag[:, :], AX.X, ALU.add).then_inc(step, 1)
        dve.tensor_tensor(m2, mean, mean, ALU.mult).then_inc(step, 1)
        dve.wait_ge(step, 4)
        dve.scalar_tensor_tensor(out=var, in0=sq, scalar=1.0 / sh.n, in1=m2, op0=ALU.mult, op1=ALU.subtract).then_inc(step, 1)
        dve.wait_ge(step, 5)
        dve.tensor_scalar(var, var, 0.0, BN_EPS, ALU.max, ALU.add).then_inc(step, 1)
        dve.wait_ge(step, 6)
        rsqrt(dve, root, var, sq, self.root_step, 0)
        dve.tensor_tensor(ss[:, 0:1], root, gamma[:, :], ALU.mult).then_inc(step, 1)
        dve.wait_ge(step, 7)
        dve.tensor_tensor(m2, mean, ss[:, 0:1], ALU.mult).then_inc(step, 1)
        dve.wait_ge(step, 8)
        dve.tensor_tensor(ss[:, 1:2], beta[:, :], m2, ALU.subtract).then_inc(step, 1)
        dve.wait_ge(step, 9)
        if self.last:
            for i in range(2):
                dve.tensor_scalar(self.as_rows[2][:, i, :], k["ones"][:, :], ss[:, i:i + 1], None, ALU.mult).then_inc(step, 1)
            dve.wait_ge(step, 11)
            dve.sem_inc(step, 1)
            dve.wait_ge(self.gram_done, sh.node_chunks + 5)
            for i in range(2):
                dve.tensor_copy(self.as_rows[i][:, :], ph.turn_ps[0][:, i * D:(i + 1) * D]).then_inc(step, 1)
            dve.wait_ge(step, 14)


class LinearNodes:

    def __init__(self, ph, weight, bias, finish):
        self.ph, self.weight, self.bias, self.finish = ph, weight, bias, finish
        self.part, self.z, self.o = ([ph.sb(f"{n}{b}", [P, T, D]) for b in range(2)] for n in ("part", "z", "o"))
        self.part_done, self.z_done, self.gated = ph.sem("part_done"), ph.sem("z_done"), ph.sem("gated")
        if finish == "norm":
            self.ln = Norm(ph, "ln", 2 * T)
        self.grants = [(ph.nodes_turned, 2)] + [(ph.used[n], 2) for n in ph.used] + [(s, 16) for s in ph.stored]

    def tensor_start(self, pe):
        pass

    def tensor(self, pe, m, at, scattered):
        self.ph.turn_nodes(pe, m, at)
        self.ph.multiply_nodes(pe, m, at, self.weight)

    def tensor_end(self, pe):
        pass

    def vector_start(self, dve):
        for b in range(2):
            dve.memset(self.z[b][:, :, :], 0.0).then_inc(self.z_done, 1)
        if self.finish == "norm":
            dve.wait_ge(self.z_done, 2)
            dve.memset(self.ln.stats[:, :, :], 1.0).then_inc(self.ln.step, 1)
            self.ln.solve_var(dve, 0)

    def vector(self, dve, m, at, scattered):
        ph = self.ph
        norm = self.finish == "norm"
        if norm:
            self.finish_vector(dve, m)
        for b in range(2):
            n = ph.sh.rows(m * 2 + b)
            part, sums = self.part[b][0:n, :, :], ph.buf["sums"][b][0:n, :, :]
            ph.have(dve, "sums", m, b)
            if norm:
                ph.have(dve, "x0", m, b)
                ins = dve.tensor_tensor(part, sums, ph.buf["x0"][b][0:n, :, :], ALU.add)
            else:
                ins = dve.tensor_tensor(part, sums, spread_slots(self.bias[0:n, :], [n, T, D]), ALU.add)
            ins.then_inc(ph.used["sums"], 1)
        if norm:
            for b in range(2):
                n = ph.sh.rows(m * 2 + b)
                part = self.part[b][0:n, :, :]
                dve.wait_ge(ph.used["sums"], 2 * m + b + 3)
                dve.sem_inc(ph.used["x0"], 1)
                dve.tensor_tensor(part, part, spread_slots(self.bias[0:n, :], [n, T, D]), ALU.add).then_inc(self.part_done, 1)
        if not norm:
            self.finish_vector(dve, m)
        for i in range(4):
            b = i // 2
            n = ph.sh.rows(m * 2 + b)
            half = slice(H * (i % 2), H * (i % 2) + H)
            dve.wait_ge(ph.multiplied, at + i + 1)
            if i % 2 == 0:
                if norm:
                    dve.wait_ge(self.part_done, 2 * m + b + 1)
                else:
                    dve.wait_ge(ph.used["sums"], 2 * m + b + 3)
                dve.wait_ge(ph.finished, 2 * m + b + 1)
            dve.tensor_tensor(self.z[b][0:n, half, :], ph.out_half(i, n), self.part[b][0:n, half, :], ALU.add).then_inc(ph.out_read, 1)
            if i % 2:
                dve.wait_ge(ph.out_read, at + i + 1)
                if norm:
                    ins = self.ln.take(dve, self.z[b], n, b * T)
                else:
                    dve.sem_inc(self.z_done, 1)
        if norm:
            ins.then_inc(self.ln.step, 1)
            dve.wait_ge(self.ln.ready, m + 1)
            self.ln.solve_var(dve, m + 1)

    def finish_vector(self, dve, m):
        if self.finish == "norm":
            self.ln.solve_scale(dve, m)
        if self.finish == "swish":
            for b in range(2):
                n = self.ph.sh.rows((m - 1) * 2 + b)
                dve.wait_ge(self.gated, 2 * m + b + 1)
                dve.tensor_tensor(self.o[b][0:n, :, :], self.o[b][0:n, :, :], self.z[b][0:n, :, :], ALU.mult).then_inc(self.ph.finished, 1)

    def vector_end(self, dve):
        pass

    def scalar(self, act, m, at, scattered):
        self.ph.turned_to_sbuf(act, m, at)
        self.finish_scalar(act, m)

    def finish_scalar(self, act, m):
        ph = self.ph
        if self.finish == "norm":
            self.ln.take_root(act, m, ph.k["ln_eps"])
            act.wait_ge(self.ln.ready, m + 1)
        for b in range(2):
            n = ph.sh.rows((m - 1) * 2 + b)
            ph.out_free(act, m, b)
            if self.finish == "norm":
                self.ln.apply(act, self.o[b], self.z[b], n, b * T).then_inc(ph.finished, 1)
            else:
                f, done = (ACT.Relu, ph.finished) if self.finish == "relu" else (ACT.Sigmoid, self.gated)
                act.wait_ge(self.z_done, 2 * m + b + 1)
                act.activation(self.o[b][0:n, :, :], self.z[b][0:n, :, :], f).then_inc(done, 1)
        ph.store_before(act, m, self.o)


def run_conv(nc, ph, edges, nodes):
    k, sh = ph.k, ph.sh
    with nc.Block() as block:
        @block.gpsimd
        def _(pool):
            ph.grant(pool, nodes.grants)
            ph.pool_program(pool)

        @block.sync
        def _(sp):
            merged_sweep(sp, k, sh, lambda *u: edges.sync(sp, *u), lambda *u: ph.load_nodes(sp, *u))

        @block.tensor
        def _(pe):
            nodes.tensor_start(pe)
            merged_sweep(pe, k, sh, lambda *u: edges.tensor(pe, *u), lambda *u: nodes.tensor(pe, *u))
            nodes.tensor_end(pe)

        @block.scalar
        def _(act):
            merged_sweep(act, k, sh, lambda *u: edges.scalar(act, *u), lambda *u: nodes.scalar(act, *u))
            nodes.finish_scalar(act, sh.node_pairs)
            ph.all_stored(act)

        @block.vector
        def _(dve):
            nodes.vector_start(dve)
            merged_sweep(dve, k, sh, lambda *u: edges.vector(dve, *u), lambda *u: nodes.vector(dve, *u))
            nodes.finish_vector(dve, sh.node_pairs)
            nodes.vector_end(dve)


def gcn_conv(nc, k, dram, sh, name, no, table, x0, out, scale_shift, next_scale_shift, as_rows=None):
    streams = {"y": table, "sums": dram["node_sums"]}
    if no:
        streams["x0"] = x0
    with Conv(nc, name, k, dram, sh, table, out, streams) as ph:
        run_conv(nc, ph, GcnEdges(ph, k[f"gcn{no}"], scale_shift), GcnNodes(ph, no, scale_shift, next_scale_shift, as_rows))


def eve_conv(nc, k, dram, sh, name, no, table, out, finish, x0=None):
    streams = {"y": table, "sums": dram["node_sums"]} | ({"x0": x0} if x0 is not None else {})
    with Conv(nc, name, k, dram, sh, table, out, streams) as ph:
        run_conv(nc, ph, EveEdges(ph, no), LinearNodes(ph, k[f"self{no}"], k[f"eve_b{no}"], finish))


def sage_conv(nc, k, dram, sh, name, no, table, out, finish, x0=None):
    streams = {"y": table, "sums": dram["node_sums"]} | ({"x0": x0} if x0 is not None else {})
    with Conv(nc, name, k, dram, sh, table, out, streams) as ph:
        run_conv(nc, ph, SageEdges(ph, k[f"sage_l{no}"]), LinearNodes(ph, k[f"sage_r{no}"], k[f"sage_b{no}"], finish))



def build(nc, a, out):
    sh = Shapes(a["x"].shape[0], a["src"].shape[0])
    nodes_padded = sh.node_chunks * CH

    def scratch(name, shape, dt=F32):
        return nc.dram_tensor(name, shape, dt, kind="Internal")

    dram = {"node_sums": scratch("node_sums", [nodes_padded, D]).ap(),
            "degree": scratch("degree", [nodes_padded, 1]).ap(),
            "dinv": scratch("dinv", [nodes_padded, 1]).ap(),
            "dst_padded": scratch("dst_padded", [sh.edges_padded + 1], I32).ap(),
            "edge_w": scratch("edge_w", [sh.edges_padded]).ap()}
    rows_a, rows_b, rows_c = (scratch(f"node_rows_{i}", [sh.n, D]).ap() for i in "abc")

    with ExitStack() as ctx:
        k = {}

        def keep(name, shape, dt=F32):
            k[name] = ctx.enter_context(nc.sbuf_tensor(f"k_{name}", shape, dt))

        for n in ("pool1", "self1", "eve1", "pool2", "self2", "eve2", "sage_l1", "sage_r1", "sage_l2", "sage_r2",
                  "gcn0", "gcn1", "gcn2", "gat_l", "gat_r", "gat_e", "ident", "ones", "head_att",
                  "gcn_b0", "gcn_b1", "gcn_b2", "eve_b1", "eve_b2", "eve_c1", "eve_c2", "sage_b1", "sage_b2",
                  "gat_b", "gat_gamma", "gat_beta", "bn_scale_row", "bn_shift_row"):
            keep(n, [P, D])
        keep("zeros", [P, D + 1])
        keep("bn_cols", [P, 2, D])
        for n in ("gamma0", "gamma1", "gamma2", "beta0", "beta1", "beta2", "bpool1", "bpool2", "bl", "br", "blr", "att",
                  "bconv1", "bconv2", "ln_eps"):
            keep(n, [P, 1])
        for n in ("wconv1", "wconv2", "bn1", "bn2", "bn3"):
            keep(n, [P, 2])
        keep("first_dst", [1, 1], I32)
        keep("ready", [1, sh.edge_pairs + 1], I32)
        for n in ("src_idx", "place_idx", "dst_idx"):
            keep(n, [P, sh.edge_tiles], I32)
        for n in ("ew_tab", "inv_count"):
            keep(n, [P, sh.edge_tiles])
        keep("dinvs", [P, sh.node_chunks, 2, T])
        keep("same_run", [P, sh.edges_padded], U8)

        load_constants(nc, a, k)
        index_tables(nc, a, k, dram, sh)
        degrees(nc, a, k, dram, sh)

        x = a["x"]
        gcn_conv(nc, k, dram, sh, "m0", 0, x, x, rows_a, None, k["bn1"])
        gcn_conv(nc, k, dram, sh, "m1", 1, rows_a, x, rows_b, k["bn1"], k["bn2"])
        gcn_conv(nc, k, dram, sh, "m2", 2, rows_b, x, rows_a, k["bn2"], k["bn3"],
                 as_rows=(k["bn_scale_row"], k["bn_shift_row"], k["bn_cols"]))
        norm_nodes(nc, k, dram, sh, "n3", rows_a, x, rows_b, k["bn_scale_row"], k["bn_shift_row"])
        eve_conv(nc, k, dram, sh, "m4", 1, rows_b, rows_a, "relu")
        eve_conv(nc, k, dram, sh, "m5", 2, rows_a, rows_c, "norm", x0=rows_b)
        sage_conv(nc, k, dram, sh, "m6", 1, rows_c, rows_a, "swish")
        sage_conv(nc, k, dram, sh, "m7", 2, rows_a, rows_b, "norm", x0=rows_c)
        gat_edges(nc, a, k, dram, sh, "e8", rows_b)
        gat_nodes(nc, k, dram, sh, "n8", rows_b, out)


def kernel(**inputs):
    import numpy as _np
    import concourse.bacc as _bacc
    from concourse import mybir as _mybir
    from concourse.bass_utils import run_bass_kernel_spmd as _run

    nc = _bacc.Bacc("TRN2", target_bir_lowering=False, num_devices=1)
    arrays, args = {}, {}
    for name, value in inputs.items():
        v = _np.ascontiguousarray(value)
        arrays[f"in_{name}_dram"] = v
        args[name] = nc.dram_tensor(f"in_{name}_dram", v.shape, _mybir.dt.from_np(v.dtype), kind="ExternalInput").ap()
    out = nc.dram_tensor("out_0_dram", args["x"].shape, _mybir.dt.float32, kind="ExternalOutput").ap()
    build(nc, args, out)
    r = _run(nc, [arrays], core_ids=[0])
    return r.results[0]["out_0_dram"]
```
